# Optimizing a Trainium2 kernel written in Bass

```python
import numpy as np
import jax
import jax.numpy as jnp

def _softmax(x, axis=-1):
    return jax.nn.softmax(x, axis=axis)

def _gelu(x):
    return jax.nn.gelu(x, approximate=True)

def _silu(x):
    return jax.nn.silu(x)

def _sigmoid(x):
    return jax.nn.sigmoid(x)

def _layernorm(x, axis=-1, eps=1e-05):
    m = jnp.mean(x, axis=axis, keepdims=True)
    v = jnp.var(x, axis=axis, keepdims=True)
    return (x - m) / jnp.sqrt(v + eps)

def _scatter_add(tgt, idx, src, axis=0):
    return tgt.at[idx].add(src)

def _segment_sum(src, seg, n):
    return jax.ops.segment_sum(src, seg, n)
kernel_name = 'mk_hybrid_d2_jaxref_r8_3735cc'

def setup_inputs(seed: int=0):
    np.random.seed(seed)
    _w = jnp.asarray

    def _L0_attn_a_setup():
        import jax, jax.numpy as jnp
        import numpy as np
        D_MODEL, N_HEADS = (128, 16)
        D_H = D_MODEL // N_HEADS
        D_HR = D_H // 2
        D_LATENT = 32
        THETA = 10000.0

        def rope(x, theta=THETA):
            S, d = (x.shape[-2], x.shape[-1])
            inv = theta ** (-jnp.arange(0, d, 2, dtype=jnp.float32) / d)
            ang = jnp.arange(S, dtype=jnp.float32)[:, None] * inv
            cos, sin = (jnp.cos(ang), jnp.sin(ang))
            x1, x2 = (x[..., 0::2], x[..., 1::2])
            r1 = x1 * cos - x2 * sin
            r2 = x1 * sin + x2 * cos
            return jnp.stack([r1, r2], axis=-1).reshape(x.shape)
        key = jax.random.key(seed)
        ks = jax.random.split(key, 9)
        s = lambda fan_in: 1.0 / np.sqrt(fan_in)
        return {'x': jax.random.normal(ks[0], (4, 256, D_MODEL), jnp.float32), 'W_DQ': jax.random.normal(ks[1], (D_MODEL, D_LATENT), jnp.float32) * s(D_MODEL), 'W_UQ': jax.random.normal(ks[2], (D_LATENT, N_HEADS * D_H), jnp.float32) * s(D_LATENT), 'W_QR': jax.random.normal(ks[3], (D_LATENT, N_HEADS * D_HR), jnp.float32) * s(D_LATENT), 'W_DKV': jax.random.normal(ks[4], (D_MODEL, D_LATENT), jnp.float32) * s(D_MODEL), 'W_UK': jax.random.normal(ks[5], (D_LATENT, N_HEADS * D_H), jnp.float32) * s(D_LATENT), 'W_UV': jax.random.normal(ks[6], (D_LATENT, N_HEADS * D_H), jnp.float32) * s(D_LATENT), 'W_KR': jax.random.normal(ks[7], (D_MODEL, D_HR), jnp.float32) * s(D_MODEL), 'W_O': jax.random.normal(ks[8], (N_HEADS * D_H, D_MODEL), jnp.float32) * s(N_HEADS * D_H)}
    _L0_attn_a_in = _L0_attn_a_setup()

    def _L0_attn_b_setup():
        import jax, jax.numpy as jnp
        import numpy as np
        D_MODEL = 128
        N_HEADS = 16
        D_K = D_MODEL // N_HEADS
        MAX_POS = 64
        ATT_SPAN = MAX_POS
        B, T = (4, 128)
        SCALE_FACTOR = 3

        def _heads(y):
            b, t, _ = y.shape
            return y.reshape(b, t, N_HEADS, D_K).transpose(0, 2, 1, 3)
        key = jax.random.key(seed)
        ks = jax.random.split(key, 16)
        init = lambda k, shape: jax.random.normal(k, shape, dtype=jnp.float32) * 0.02
        inp = {'x': jax.random.normal(ks[0], (B, T, D_MODEL), dtype=jnp.float32), 'Wq': init(ks[1], (D_MODEL, D_MODEL)), 'bq': jnp.zeros((D_MODEL,), jnp.float32), 'Wk': init(ks[2], (D_MODEL, D_MODEL)), 'bk': jnp.zeros((D_MODEL,), jnp.float32), 'Wv': init(ks[3], (D_MODEL, D_MODEL)), 'bv': jnp.zeros((D_MODEL,), jnp.float32), 'Wo': init(ks[4], (D_MODEL, D_MODEL)), 'bo': jnp.zeros((D_MODEL,), jnp.float32), 'Wpk': init(ks[5], (D_MODEL, D_MODEL)), 'bpk': jnp.zeros((D_MODEL,), jnp.float32), 'Wpq': init(ks[6], (D_MODEL, D_MODEL)), 'bpq': jnp.zeros((D_MODEL,), jnp.float32), 'rel_emb': init(ks[7], (2 * ATT_SPAN, D_MODEL))}
        return inp
    _L0_attn_b_in = _L0_attn_b_setup()

    def _L0_ffn_setup():
        import jax, jax.numpy as jnp
        import numpy as np
        IN_DIM = 128
        OUT_DIM = 128
        NUM_EXPERTS = 8
        TOP_K = 2
        key = jax.random.key(seed)
        ks = jax.random.split(key, 5)
        s = 1.0 / np.sqrt(IN_DIM)
        x = jax.random.normal(ks[0], (4, 256, IN_DIM), dtype=jnp.float32)
        Wg = jax.random.uniform(ks[1], (IN_DIM, NUM_EXPERTS), jnp.float32, -s, s)
        bg = jnp.zeros((NUM_EXPERTS,), jnp.float32)
        We = jax.random.uniform(ks[2], (NUM_EXPERTS, OUT_DIM, IN_DIM), jnp.float32, -s, s)
        be = jax.random.uniform(ks[3], (NUM_EXPERTS, OUT_DIM), jnp.float32, -s, s)
        return {'x': x, 'Wg': Wg, 'bg': bg, 'We': We, 'be': be}
    _L0_ffn_in = _L0_ffn_setup()

    def _L1_attn_a_setup():
        import jax, jax.numpy as jnp
        import numpy as np
        B, T, D = (2, 256, 128)
        H = 16
        DH = D // H
        EPS = 1e-06

        def _feature_map(x):
            return jax.nn.elu(x) + 1.0
        key = jax.random.key(seed)
        ks = jax.random.split(key, 9)
        s = 0.02
        return {'x': jax.random.normal(ks[0], (B, T, D), dtype=jnp.float32), 'Wq': jax.random.normal(ks[1], (D, D), dtype=jnp.float32) * s, 'bq': jnp.zeros((D,), dtype=jnp.float32), 'Wk': jax.random.normal(ks[2], (D, D), dtype=jnp.float32) * s, 'bk': jnp.zeros((D,), dtype=jnp.float32), 'Wv': jax.random.normal(ks[3], (D, D), dtype=jnp.float32) * s, 'bv': jnp.zeros((D,), dtype=jnp.float32), 'Wo': jax.random.normal(ks[4], (D, D), dtype=jnp.float32) * s, 'bo': jnp.zeros((D,), dtype=jnp.float32)}
    _L1_attn_a_in = _L1_attn_a_setup()

    def _L1_attn_b_setup():
        import jax, jax.numpy as jnp
        import numpy as np
        B, M, D, H = (2, 256, 128, 16)

        def _rope(x):
            b, m, d = x.shape
            i = jnp.arange(d // 2, dtype=jnp.float32)
            theta = 10000.0 ** (-2.0 * (i - 1.0) / d)
            ang = jnp.arange(m, dtype=jnp.float32)[:, None] * theta[None, :]
            c, s = (jnp.cos(ang), jnp.sin(ang))
            xe, xo = (x[..., 0::2], x[..., 1::2])
            ye = xe * c + xo * s
            yo = -xe * s + xo * c
            return jnp.stack([ye, yo], axis=-1).reshape(b, m, d)
        key = jax.random.key(seed)
        ks = jax.random.split(key, 8)
        w = lambda k, shape: jax.random.normal(k, shape, jnp.float32) * 0.02
        return {'x': jax.random.normal(ks[0], (B, M, D), jnp.float32), 'wq': w(ks[1], (D, D)), 'wk': w(ks[2], (D, D)), 'wv': w(ks[3], (D, D)), 'in_proj_w': w(ks[4], (3 * D, D)), 'in_proj_b': w(ks[5], (3 * D,)), 'out_w': w(ks[6], (D, D)), 'out_b': w(ks[7], (D,))}
    _L1_attn_b_in = _L1_attn_b_setup()

    def _L1_ffn_setup():
        import jax, jax.numpy as jnp
        import numpy as np
        CAPACITY = 2
        B, S, D, E, I = (4, 512, 128, 8, 512)
        key = jax.random.key(seed)
        k0, k1, k2, k3, k4 = jax.random.split(key, 5)
        x = jax.random.normal(k0, (B, S, D), dtype=jnp.float32)
        gate_w = jax.random.normal(k1, (E, D), dtype=jnp.float32) * 0.006
        w_gate = jax.random.normal(k2, (E, I, D), dtype=jnp.float32) * (1.0 / np.sqrt(D))
        w_up = jax.random.normal(k3, (E, I, D), dtype=jnp.float32) * (1.0 / np.sqrt(D))
        w_down = jax.random.normal(k4, (E, D, I), dtype=jnp.float32) * (1.0 / np.sqrt(I))
        return {'x': x, 'gate_w': gate_w, 'w_gate': w_gate, 'w_up': w_up, 'w_down': w_down}
    _L1_ffn_in = _L1_ffn_setup()
    _d = {'L0_attn_a_x': _L0_attn_a_in['x'], 'L0_attn_a_W_DQ': _L0_attn_a_in['W_DQ'], 'L0_attn_a_W_UQ': _L0_attn_a_in['W_UQ'], 'L0_attn_a_W_QR': _L0_attn_a_in['W_QR'], 'L0_attn_a_W_DKV': _L0_attn_a_in['W_DKV'], 'L0_attn_a_W_UK': _L0_attn_a_in['W_UK'], 'L0_attn_a_W_UV': _L0_attn_a_in['W_UV'], 'L0_attn_a_W_KR': _L0_attn_a_in['W_KR'], 'L0_attn_a_W_O': _L0_attn_a_in['W_O'], 'L0_attn_b_Wq': _L0_attn_b_in['Wq'], 'L0_attn_b_bq': _L0_attn_b_in['bq'], 'L0_attn_b_Wk': _L0_attn_b_in['Wk'], 'L0_attn_b_bk': _L0_attn_b_in['bk'], 'L0_attn_b_Wv': _L0_attn_b_in['Wv'], 'L0_attn_b_bv': _L0_attn_b_in['bv'], 'L0_attn_b_Wo': _L0_attn_b_in['Wo'], 'L0_attn_b_bo': _L0_attn_b_in['bo'], 'L0_attn_b_Wpk': _L0_attn_b_in['Wpk'], 'L0_attn_b_bpk': _L0_attn_b_in['bpk'], 'L0_attn_b_Wpq': _L0_attn_b_in['Wpq'], 'L0_attn_b_bpq': _L0_attn_b_in['bpq'], 'L0_attn_b_rel_emb': _L0_attn_b_in['rel_emb'], 'L0_ffn_Wg': _L0_ffn_in['Wg'], 'L0_ffn_bg': _L0_ffn_in['bg'], 'L0_ffn_We': _L0_ffn_in['We'], 'L0_ffn_be': _L0_ffn_in['be'], 'L1_attn_a_Wq': _L1_attn_a_in['Wq'], 'L1_attn_a_bq': _L1_attn_a_in['bq'], 'L1_attn_a_Wk': _L1_attn_a_in['Wk'], 'L1_attn_a_bk': _L1_attn_a_in['bk'], 'L1_attn_a_Wv': _L1_attn_a_in['Wv'], 'L1_attn_a_bv': _L1_attn_a_in['bv'], 'L1_attn_a_Wo': _L1_attn_a_in['Wo'], 'L1_attn_a_bo': _L1_attn_a_in['bo'], 'L1_attn_b_wq': _L1_attn_b_in['wq'], 'L1_attn_b_wk': _L1_attn_b_in['wk'], 'L1_attn_b_wv': _L1_attn_b_in['wv'], 'L1_attn_b_in_proj_w': _L1_attn_b_in['in_proj_w'], 'L1_attn_b_in_proj_b': _L1_attn_b_in['in_proj_b'], 'L1_attn_b_out_w': _L1_attn_b_in['out_w'], 'L1_attn_b_out_b': _L1_attn_b_in['out_b'], 'L1_ffn_gate_w': _L1_ffn_in['gate_w'], 'L1_ffn_w_gate': _L1_ffn_in['w_gate'], 'L1_ffn_w_up': _L1_ffn_in['w_up'], 'L1_ffn_w_down': _L1_ffn_in['w_down']}
    _x0 = _d['L0_attn_a_x']
    _d['L0_attn_a_x'] = jax.random.normal(jax.random.fold_in(jax.random.key(seed), 1), (8, 512, 128), dtype=_x0.dtype)
    del _x0
    return _d

def reference(L0_attn_a_x, L0_attn_a_W_DQ, L0_attn_a_W_UQ, L0_attn_a_W_QR, L0_attn_a_W_DKV, L0_attn_a_W_UK, L0_attn_a_W_UV, L0_attn_a_W_KR, L0_attn_a_W_O, L0_attn_b_Wq, L0_attn_b_bq, L0_attn_b_Wk, L0_attn_b_bk, L0_attn_b_Wv, L0_attn_b_bv, L0_attn_b_Wo, L0_attn_b_bo, L0_attn_b_Wpk, L0_attn_b_bpk, L0_attn_b_Wpq, L0_attn_b_bpq, L0_attn_b_rel_emb, L0_ffn_Wg, L0_ffn_bg, L0_ffn_We, L0_ffn_be, L1_attn_a_Wq, L1_attn_a_bq, L1_attn_a_Wk, L1_attn_a_bk, L1_attn_a_Wv, L1_attn_a_bv, L1_attn_a_Wo, L1_attn_a_bo, L1_attn_b_wq, L1_attn_b_wk, L1_attn_b_wv, L1_attn_b_in_proj_w, L1_attn_b_in_proj_b, L1_attn_b_out_w, L1_attn_b_out_b, L1_ffn_gate_w, L1_ffn_w_gate, L1_ffn_w_up, L1_ffn_w_down):

    def _L0_attn_a_ref(x, W_DQ, W_UQ, W_QR, W_DKV, W_UK, W_UV, W_KR, W_O):
        import jax, jax.numpy as jnp
        import numpy as np
        D_MODEL, N_HEADS = (128, 16)
        D_H = D_MODEL // N_HEADS
        D_HR = D_H // 2
        D_LATENT = 32
        THETA = 10000.0

        def rope(x, theta=THETA):
            S, d = (x.shape[-2], x.shape[-1])
            inv = theta ** (-jnp.arange(0, d, 2, dtype=jnp.float32) / d)
            ang = jnp.arange(S, dtype=jnp.float32)[:, None] * inv
            cos, sin = (jnp.cos(ang), jnp.sin(ang))
            x1, x2 = (x[..., 0::2], x[..., 1::2])
            r1 = x1 * cos - x2 * sin
            r2 = x1 * sin + x2 * cos
            return jnp.stack([r1, r2], axis=-1).reshape(x.shape)
        B, S, _ = x.shape
        d_qk = D_H + D_HR
        c_q = x @ W_DQ
        Qc = (c_q @ W_UQ).reshape(B, S, N_HEADS, D_H).transpose(0, 2, 1, 3)
        Qr = (c_q @ W_QR).reshape(B, S, N_HEADS, D_HR).transpose(0, 2, 1, 3)
        Qr = rope(Qr)
        c_kv = x @ W_DKV
        Kc = (c_kv @ W_UK).reshape(B, S, N_HEADS, D_H).transpose(0, 2, 1, 3)
        Kr = rope((x @ W_KR)[:, None, :, :])
        Kr = jnp.broadcast_to(Kr, (B, N_HEADS, S, D_HR))
        V = (c_kv @ W_UV).reshape(B, S, N_HEADS, D_H).transpose(0, 2, 1, 3)
        Q = jnp.concatenate([Qc, Qr], axis=-1)
        K = jnp.concatenate([Kc, Kr], axis=-1)
        scores = jnp.einsum('bhqd,bhkd->bhqk', Q, K)
        scores = jnp.clip(scores, -80.0, 80.0)
        causal = jnp.tril(jnp.ones((S, S), dtype=bool))
        scores = jnp.where(causal, scores, -jnp.inf)
        weights = jax.nn.softmax(scores / jnp.sqrt(jnp.float32(d_qk)), axis=-1)
        attn = jnp.einsum('bhqk,bhkd->bhqd', weights, V)
        attn = attn.transpose(0, 2, 1, 3).reshape(B, S, N_HEADS * D_H)
        return attn @ W_O

    def _L0_attn_b_ref(x, Wq, bq, Wk, bk, Wv, bv, Wo, bo, Wpk, bpk, Wpq, bpq, rel_emb):
        import jax, jax.numpy as jnp
        import numpy as np
        D_MODEL = 128
        N_HEADS = 16
        D_K = D_MODEL // N_HEADS
        MAX_POS = 64
        ATT_SPAN = MAX_POS
        B, T = (4, 128)
        SCALE_FACTOR = 3

        def _heads(y):
            b, t, _ = y.shape
            return y.reshape(b, t, N_HEADS, D_K).transpose(0, 2, 1, 3)
        b, t, c = x.shape
        scale = 1.0 / jnp.sqrt(jnp.asarray(D_K * SCALE_FACTOR, x.dtype))
        Q = _heads(x @ Wq.T + bq)
        K = _heads(x @ Wk.T + bk)
        V = _heads(x @ Wv.T + bv)
        rel = jnp.arange(t)[None, :] - jnp.arange(t)[:, None]
        rel_pos = jnp.clip(rel + ATT_SPAN, 0, 2 * ATT_SPAN - 1)
        p2c_pos = jnp.clip(-rel + ATT_SPAN, 0, 2 * ATT_SPAN - 1)
        scores = jnp.einsum('bhqd,bhkd->bhqk', Q, K) * scale
        pos_key = (rel_emb @ Wpk.T + bpk).reshape(2 * ATT_SPAN, N_HEADS, D_K)
        c2p = jnp.einsum('bhqd,shd->bhqs', Q, pos_key) * scale
        c2p = jnp.take_along_axis(c2p, rel_pos[None, None, :, :], axis=-1)
        pos_query = (rel_emb @ Wpq.T + bpq).reshape(2 * ATT_SPAN, N_HEADS, D_K)
        p2c = jnp.einsum('bhkd,shd->bhks', K, pos_query) * scale
        p2c = jnp.take_along_axis(p2c, p2c_pos[None, None, :, :], axis=-1)
        p2c = jnp.swapaxes(p2c, -1, -2)
        scores = scores + c2p + p2c
        probs = jax.nn.softmax(scores, axis=-1)
        ctx = jnp.einsum('bhqk,bhkd->bhqd', probs, V)
        ctx = ctx.transpose(0, 2, 1, 3).reshape(b, t, c)
        return ctx @ Wo.T + bo

    def _L0_ffn_ref(x, Wg, bg, We, be):
        import jax, jax.numpy as jnp
        import numpy as np
        IN_DIM = 128
        OUT_DIM = 128
        NUM_EXPERTS = 8
        TOP_K = 2
        gate = jax.nn.softmax(x @ Wg + bg, axis=-1)
        topk_vals, topk_idx = jax.lax.top_k(gate, TOP_K)
        onehot = jax.nn.one_hot(topk_idx, NUM_EXPERTS, dtype=gate.dtype)
        gate_sparse = jnp.einsum('bsk,bske->bse', topk_vals, onehot)
        gate_sparse = gate_sparse / jnp.sum(gate_sparse, axis=-1, keepdims=True)
        y = jnp.einsum('bsi,eoi->bseo', x, We) + be[None, None, :, :].transpose(0, 1, 2, 3)
        out = jnp.einsum('bseo,bse->bso', y, gate_sparse)
        return out

    def _L1_attn_a_ref(x, Wq, bq, Wk, bk, Wv, bv, Wo, bo):
        import jax, jax.numpy as jnp
        import numpy as np
        B, T, D = (2, 256, 128)
        H = 16
        DH = D // H
        EPS = 1e-06

        def _feature_map(x):
            return jax.nn.elu(x) + 1.0
        b, t, d = x.shape
        q = (x @ Wq.T + bq).reshape(b, t, H, DH).transpose(0, 2, 1, 3)
        k = (x @ Wk.T + bk).reshape(b, t, H, DH).transpose(0, 2, 1, 3)
        v = (x @ Wv.T + bv).reshape(b, t, H, DH).transpose(0, 2, 1, 3)
        q = _feature_map(q)
        k = _feature_map(k)
        kv = jnp.einsum('bhtd,bhte->bhtde', k, v)
        kv_cum = jnp.cumsum(kv, axis=2)
        numerator = jnp.einsum('bhtd,bhtde->bhte', q, kv_cum)
        k_cum = jnp.cumsum(k, axis=2)
        denominator = jnp.einsum('bhtd,bhtd->bht', q, k_cum)
        denominator = jnp.maximum(denominator, EPS)[..., None]
        out = numerator / denominator
        out = out.transpose(0, 2, 1, 3).reshape(b, t, d)
        return out @ Wo.T + bo

    def _L1_attn_b_ref(x, wq, wk, wv, in_proj_w, in_proj_b, out_w, out_b):
        import jax, jax.numpy as jnp
        import numpy as np
        B, M, D, H = (2, 256, 128, 16)

        def _rope(x):
            b, m, d = x.shape
            i = jnp.arange(d // 2, dtype=jnp.float32)
            theta = 10000.0 ** (-2.0 * (i - 1.0) / d)
            ang = jnp.arange(m, dtype=jnp.float32)[:, None] * theta[None, :]
            c, s = (jnp.cos(ang), jnp.sin(ang))
            xe, xo = (x[..., 0::2], x[..., 1::2])
            ye = xe * c + xo * s
            yo = -xe * s + xo * c
            return jnp.stack([ye, yo], axis=-1).reshape(b, m, d)
        b, m, d = x.shape
        h = H
        hd = d // h
        q = _rope(x @ wq.T)
        k = _rope(x @ wk.T)
        v = _rope(x @ wv.T)
        wqi, wki, wvi = jnp.split(in_proj_w, 3, axis=0)
        bqi, bki, bvi = jnp.split(in_proj_b, 3, axis=0)
        qh = (q @ wqi.T + bqi).reshape(b, m, h, hd)
        kh = (k @ wki.T + bki).reshape(b, m, h, hd)
        vh = (v @ wvi.T + bvi).reshape(b, m, h, hd)
        scores = jnp.einsum('bqhd,bkhd->bhqk', qh, kh) / jnp.sqrt(jnp.float32(hd))
        causal = jnp.tril(jnp.ones((m, m), dtype=bool))
        scores = jnp.where(causal, scores, jnp.float32(-jnp.inf))
        attn = jax.nn.softmax(scores, axis=-1)
        o = jnp.einsum('bhqk,bkhd->bqhd', attn, vh).reshape(b, m, d)
        return o @ out_w.T + out_b

    def _L1_ffn_ref(x, gate_w, w_gate, w_up, w_down):
        import jax, jax.numpy as jnp
        import numpy as np
        CAPACITY = 2
        B, S, D = x.shape
        E = gate_w.shape[0]
        k = S // E * CAPACITY
        logits = jnp.einsum('bsd,ed->bse', x, gate_w)
        affinity = jax.nn.softmax(logits, axis=-1)
        affinity = jnp.transpose(affinity, (0, 2, 1))
        gating, idx = jax.lax.top_k(affinity, k)
        bidx = jnp.arange(B)[:, None, None]
        x_in = x[bidx, idx]
        h = jax.nn.silu(jnp.einsum('bekd,eid->beki', x_in, w_gate)) * jnp.einsum('bekd,eid->beki', x_in, w_up)
        x_e = jnp.einsum('beki,edi->bekd', h, w_down)
        out = jnp.zeros_like(x).at[bidx, idx].add(gating[..., None] * x_e)
        return out
    x = L0_attn_a_x
    x = x + _L0_attn_a_ref(_layernorm(x, axis=-1), L0_attn_a_W_DQ, L0_attn_a_W_UQ, L0_attn_a_W_QR, L0_attn_a_W_DKV, L0_attn_a_W_UK, L0_attn_a_W_UV, L0_attn_a_W_KR, L0_attn_a_W_O)
    x = x + _L0_ffn_ref(_layernorm(x, axis=-1), L0_ffn_Wg, L0_ffn_bg, L0_ffn_We, L0_ffn_be)
    x = x + _L0_attn_b_ref(_layernorm(x, axis=-1), L0_attn_b_Wq, L0_attn_b_bq, L0_attn_b_Wk, L0_attn_b_bk, L0_attn_b_Wv, L0_attn_b_bv, L0_attn_b_Wo, L0_attn_b_bo, L0_attn_b_Wpk, L0_attn_b_bpk, L0_attn_b_Wpq, L0_attn_b_bpq, L0_attn_b_rel_emb)
    x = x + _L0_ffn_ref(_layernorm(x, axis=-1), L0_ffn_Wg, L0_ffn_bg, L0_ffn_We, L0_ffn_be)
    x = x + _L1_attn_a_ref(_layernorm(x, axis=-1), L1_attn_a_Wq, L1_attn_a_bq, L1_attn_a_Wk, L1_attn_a_bk, L1_attn_a_Wv, L1_attn_a_bv, L1_attn_a_Wo, L1_attn_a_bo)
    x = x + _L1_ffn_ref(_layernorm(x, axis=-1), L1_ffn_gate_w, L1_ffn_w_gate, L1_ffn_w_up, L1_ffn_w_down)
    x = x + _L1_attn_b_ref(_layernorm(x, axis=-1), L1_attn_b_wq, L1_attn_b_wk, L1_attn_b_wv, L1_attn_b_in_proj_w, L1_attn_b_in_proj_b, L1_attn_b_out_w, L1_attn_b_out_b)
    x = x + _L1_ffn_ref(_layernorm(x, axis=-1), L1_ffn_gate_w, L1_ffn_w_gate, L1_ffn_w_up, L1_ffn_w_down)
    return x

_drawn_inputs = setup_inputs


def setup_inputs(seed=0):
    import zlib

    import numpy as np

    out = dict(_drawn_inputs(seed))
    spreads = {'L0_attn_b_bq': (0.0, 0.8),
     'L0_attn_b_bk': (0.0, 0.8),
     'L0_attn_b_bv': (0.0, 0.1),
     'L0_attn_b_bo': (0.0, 0.1),
     'L0_attn_b_bpk': (0.0, 2.0),
     'L0_attn_b_bpq': (0.0, 0.8),
     'L0_ffn_bg': (0.0, 0.1),
     'L1_attn_a_bq': (0.0, 0.8),
     'L1_attn_a_bk': (0.0, 0.8),
     'L1_attn_a_bv': (0.0, 0.45),
     'L1_attn_a_bo': (0.0, 0.1)}
    factors = {'L0_attn_b_Wq': 8.0,
     'L0_attn_b_Wk': 8.0,
     'L0_attn_b_Wv': 3.3,
     'L0_attn_b_Wpk': 8.0,
     'L0_attn_b_Wpq': 8.0,
     'L0_attn_b_rel_emb': 8.0,
     'L1_attn_a_Wq': 8.0,
     'L1_attn_a_Wk': 8.0,
     'L1_attn_a_Wv': 5.548,
     'L1_attn_a_Wo': 2.878,
     'L1_attn_b_wq': 8.0,
     'L1_attn_b_wk': 8.0,
     'L1_attn_b_wv': 8.0,
     'L1_attn_b_in_proj_w': 8.0,
     'L1_attn_b_in_proj_b': 8.0,
     'L1_attn_b_out_w': 8.0,
     'L1_attn_b_out_b': 14.035}
    for name, (base, spread) in spreads.items():
        noise = np.random.default_rng([zlib.crc32(name.encode()), seed]).standard_normal(out[name].shape)
        drawn = base * np.exp(spread * noise) if base else spread * noise
        out[name] = jnp.asarray(drawn.astype(out[name].dtype))
    for name, factor in factors.items():
        out[name] = (out[name] * factor).astype(out[name].dtype)
    return out
```

```python
from contextlib import ExitStack

import numpy as np

import concourse.bass as bass
from concourse import mybir

F32 = mybir.dt.float32
BF16 = mybir.dt.bfloat16
ALU = mybir.AluOpType
ACT = mybir.ActivationFunctionType
AX = mybir.AxisListType.X

P = 128
B, S, D = 8, 512, 128
NT = S // P
H, DH = 16, 8
DR, DL = 4, 32
E = 8
FI = 512
KTOP = S // E * 2
REL = 64
LPART = (0, 0, 1, 0, 1, 2)
RPART = (0, 1, 0, 2, 1, 0)
NC6 = len(LPART)
LN_EPS = 1e-5
FAR = S - 3 * REL
EXT = 3 * P
TW = 2 * EXT + 2 * P
VW = 32


class Net:

    def __init__(self, nc, aps, ctx):
        self.nc, self.aps, self.ctx = nc, aps, ctx
        sb = lambda name, shape, dt=F32: ctx.enter_context(nc.sbuf_tensor(name, shape, dt))
        self.X = sb("X", [P, B * NT, D])
        self.V = sb("V", [P, B * H, NT, DH])
        self.idf = sb("idf", [P, P])
        self.idb = sb("idb", [P, P], BF16)
        self.negb = sb("negb", [P, P], BF16)
        self.half = sb("half", [P, NT])
        self.ones = sb("ones", [1, S])
        self.constants = ctx.enter_context(nc.semaphore("constants"))
        self.carrier = ctx.enter_context(nc.semaphore("carrier"))
        scratch = lambda name, shape, dt: nc.dram_tensor(name, shape, dt, kind="Internal").ap()
        rows = NC6 * (DH + DR)
        self.QS = scratch("QS", (B * H, rows, S), BF16)
        self.KS = scratch("KS", (B * H, rows, S), BF16)
        self.KLS = scratch("KLS", (B * H, NC6 * DH, FAR), BF16)
        self.KHS = scratch("KHS", (B * H, NC6 * DH, FAR), BF16)
        self.TB = scratch("TB", (H, NC6 * DH, TW), BF16)
        self.aff = sb("aff", [P, NT, B * E])
        self.slot = sb("slot", [P, NT, B * E])
        self.CU = scratch("CU", (B * H, 2 * DH, S), F32)


class Phase:

    def __init__(self, net, tag):
        self.net, self.nc, self.tag, self.ctx, self.sems = net, net.nc, tag, ExitStack(), []

    def __enter__(self):
        return self

    def __exit__(self, *a):
        if a[0] is None:
            for s in self.sems:
                self.nc.gpsimd.sem_clear(s)
            self.nc.all_engine_barrier()
        self.ctx.close()

    def sb(self, name, shape, dt=F32):
        return self.ctx.enter_context(self.nc.sbuf_tensor(f"{self.tag}_{name}", shape, dt))

    def ps(self, name, shape, dt=F32):
        return self.ctx.enter_context(self.nc.psum_tensor(f"{self.tag}_{name}", shape, dt))

    def sem(self, name):
        s = self.ctx.enter_context(self.nc.semaphore(f"{self.tag}_{name}"))
        self.sems.append(s)
        return s


def waited(net, eng, *waits):
    for sem, value in waits:
        eng.wait_ge(sem, value)
    eng.sem_inc(net.carrier, 1)


def over(ap, dim, n):
    shape = list(ap.shape)
    shape.insert(dim, n)
    return ap.unsqueeze(dim).broadcast_to(shape)


def setup(net):
    nc = net.nc
    with Phase(net, "setup") as ph:
        loaded, made = ph.sem("loaded"), ph.sem("made")
        with nc.Block() as block:
            @block.sync
            def _(sp):
                sp.dma_start(net.X[:, :, :], net.aps["L0_attn_a_x"].rearrange("b (j p) d -> p (b j) d", p=P)).then_inc(loaded, 16)
                sp.wait_ge(loaded, 16)

            @block.vector
            def _(v):
                v.memset(net.half[:, :], -0.5)
                v.memset(net.ones[:, :], 1.0)

            @block.gpsimd
            def _(g):
                g.memset(net.idf[:, :], 0.0)
                g.memset(net.negb[:, :], 0.0).then_inc(made, 1)
                g.wait_ge(made, 1)
                g.affine_select(out=net.idf[:, :], in_=net.idf[:, :], compare_op=ALU.not_equal, fill=1.0, base=0,
                                pattern=[[-1, P]], channel_multiplier=1).then_inc(made, 1)
                g.affine_select(out=net.negb[:, :], in_=net.negb[:, :], compare_op=ALU.is_ge, fill=-1e30, base=0,
                                pattern=[[-1, P]], channel_multiplier=1).then_inc(made, 1)
                g.wait_ge(made, 3)
                g.tensor_copy(net.idb[:, :], net.idf[:, :]).then_inc(net.constants, 1)


class Norm:

    def __init__(self, ph, tag, psT, xn=None):
        self.net, self.psT = ph.net, psT
        self.xn = xn if xn is not None else ph.sb(tag + "xn", [P, NT, D])
        self.xT = ph.sb(tag + "xT", [P, S])
        self.st = ph.sb(tag + "st", [P, NT, 6])
        self.mv = ph.sb(tag + "mv", [P, NT, 2])
        self.ve = ph.sb(tag + "ve", [P, NT])
        self.rs = ph.sb(tag + "rs", [P, NT])
        s = lambda n: ph.sem(tag + n)
        self.stats, self.moments, self.shifted, self.inverse = s("stats"), s("moments"), s("shifted"), s("inverse")
        self.normed, self.turned, self.ready = s("normed"), s("turned"), s("ready")
        self.used = (self.turned, 1)

    def dve(self, v, b):
        net = self.net
        waited(net, v, (self.inverse, b))
        for j in range(NT):
            v.bn_stats(self.st[:, j, :], net.X[:, bass.ds(b * NT + j, 1), :].rearrange("p o d -> p (o d)")).then_inc(self.stats, 1)
        waited(net, v, (self.stats, NT * b + NT))
        for j in range(NT):
            v.bn_aggr(self.mv[:, j, :], self.st[:, j, :]).then_inc(self.moments, 1)
        v.wait_ge(self.inverse, b + 1)
        v.wait_ge(self.used[0], self.used[1] * b)
        for j in range(NT):
            v.tensor_scalar(self.xn[:, j, :], net.X[:, bass.ds(b * NT + j, 1), :].rearrange("p o d -> p (o d)"),
                            self.mv[:, j, 0:1], self.rs[:, j:j + 1], ALU.subtract, ALU.mult).then_inc(self.normed, 1)

    def pool(self, g, b):
        waited(self.net, g, (self.moments, NT * b + NT))
        g.tensor_scalar(self.ve[:, :], self.mv[:, :, 1], LN_EPS, None, ALU.add).then_inc(self.shifted, 1)
        g.wait_ge(self.shifted, b + 1)
        g.wait_ge(self.normed, NT * b)
        g.tensor_tensor(self.rs[:, :], self.ve[:, :], self.net.half[:, :], ALU.pow).then_inc(self.inverse, 1)

    def pe(self, pe, b):
        pe.wait_ge(self.normed, NT * b + NT)
        pe.wait_ge(self.ready, b)
        for j in range(NT):
            t = pe.transpose(self.psT[:, j * P:(j + 1) * P], self.xn[:, j, :], self.net.idf[:, :])
        t.then_inc(self.turned, 1)

    def act(self, a, b, free=None):
        a.wait_ge(self.turned, b + 1)
        if free is not None:
            a.wait_ge(*free)
        a.copy(self.xT[:, :], self.psT[:, :]).then_inc(self.ready, 1)


class Split:

    def __init__(self, ph, tag, n, src, cols=S):
        self.net, self.n, self.src = ph.net, n, src
        self.part = ph.sb(tag + "part", [n, 3, cols], BF16)
        self.r1 = ph.sb(tag + "r1", [n, cols])
        self.first, self.rest, self.second, self.third, self.kept = (
            ph.sem(tag + x) for x in ("first", "rest", "second", "third", "kept"))

    def act(self, a, b, have, stored):
        a.wait_ge(*have)
        a.wait_ge(self.kept, 16 * stored * b)
        a.copy(self.part[:, 0, :], self.src).then_inc(self.first, 1)

    def dve(self, v, b):
        v.wait_ge(self.first, b + 1)
        v.wait_ge(self.third, b)
        v.tensor_tensor(self.r1[:, :], self.src, self.part[:, 0, :], ALU.subtract).then_inc(self.rest, 1)

    def pool(self, g, b):
        waited(self.net, g, (self.rest, b + 1))
        g.tensor_copy(self.part[:, 1, :], self.r1[:, :]).then_inc(self.second, 1)
        g.wait_ge(self.second, b + 1)
        g.tensor_tensor(self.part[:, 2, :], self.r1[:, :], self.part[:, 1, :], ALU.subtract).then_inc(self.third, 1)

    def store(self, sp, b, dst, parts, width, at, per):
        sp.wait_ge(self.third, b + 1)
        for c, part in enumerate(parts):
            rows = dst[bass.ds(b * H, H), c * width + at:c * width + at + per, :]
            sp.dma_start(rows, self.part[:, part, :]).then_inc(self.kept, 16)


def mla_prep(net):
    nc, aps = net.nc, net.aps
    WD = DH + DR
    with Phase(net, "ma") as ph:
        w_down = ph.sb("w_down", [P, P])
        w_q = ph.sb("w_q", [DL, H * DH])
        w_qr = ph.sb("w_qr", [DL, 2 * H * DR])
        w_kv = ph.sb("w_kv", [2 * DL, 2 * H * DH])
        rot = ph.sb("rot", [P, S])
        lat = ph.sb("lat", [P, S])
        a1 = ph.sb("a1", [H * DR, S])
        a2 = ph.sb("a2", [H * DR, S])
        b1 = ph.sb("b1", [DR, S])
        b2 = ph.sb("b2", [DR, S])
        qr = ph.sb("qr", [H * DR, S])
        kr = ph.sb("kr", [DR, S])
        psT, psD, psQ, psR, psK, psV = (ph.ps(n, [P, S]) for n in ("psT", "psD", "psQ", "psR", "psK", "psV"))
        nm = Norm(ph, "n", psT)
        sq = Split(ph, "q", P, psQ[:, :])
        sk = Split(ph, "k", P, psK[:, :])
        sqr = Split(ph, "qr", H * DR, qr[:, :])
        skr = Split(ph, "kr", DR, kr[:, :])
        weights = ph.sem("weights")
        down, latent, up, rq, rqs, rk, rks, vals = (ph.sem(x) for x in
            ("down", "latent", "up", "rq", "rqs", "rk", "rks", "vals"))
        with nc.Block() as block:
            @block.sync
            def _(sp):
                sp.dma_start(w_down[:, :], aps["mla_down"]).then_inc(weights, 16)
                sp.dma_start(w_q[:, :], aps["L0_attn_a_W_UQ"]).then_inc(weights, 16)
                sp.dma_start(w_qr[:, :], aps["mla_qr"]).then_inc(weights, 16)
                sp.dma_start(w_kv[DL:2 * DL, 0:H * DH], aps["L0_attn_a_W_UK"]).then_inc(weights, 16)
                sp.dma_start(w_kv[DL:2 * DL, H * DH:], aps["L0_attn_a_W_UV"]).then_inc(weights, 16)
                sp.dma_start(rot[:, :], aps["mla_rot"]).then_inc(weights, 16)
                with sp.Fori(0, B) as b:
                    sq.store(sp, b, net.QS, LPART, WD, 0, DH)
                    sk.store(sp, b, net.KS, RPART, WD, 0, DH)
                    sqr.store(sp, b, net.QS, LPART, WD, DH, DR)
                    sp.wait_ge(skr.third, b + 1)
                    for c, part in enumerate(RPART):
                        rows = net.KS[bass.ds(b * H, H), c * WD + DH:(c + 1) * WD, :].rearrange("h r s -> r h s")
                        src = skr.part[:, part, :].unsqueeze(1).broadcast_to([DR, H, S])
                        sp.dma_start(rows, src).then_inc(skr.kept, 16)
                for s in (sq, sk, sqr):
                    sp.wait_ge(s.kept, 16 * NC6 * B)
                sp.wait_ge(skr.kept, 16 * NC6 * B)

            @block.tensor
            def _(pe):
                pe.wait_ge(weights, 16 * 6)
                with pe.Fori(0, B) as b:
                    nm.pe(pe, b)
                    pe.wait_ge(nm.ready, b + 1)
                    pe.wait_ge(latent, b)
                    pe.wait_ge(rk, 2 * b)
                    pe.matmul(psD[:, :], w_down[:, :], nm.xT[:, :], start=True, stop=True).then_inc(down, 1)
                    pe.wait_ge(latent, b + 1)
                    pe.wait_ge(sq.rest, b)
                    pe.wait_ge(sk.rest, b)
                    pe.wait_ge(rq, 2 * b)
                    pe.wait_ge(vals, b)
                    pe.matmul(psQ[:, :], w_q[:, :], lat[0:DL, :], start=True, stop=True).then_inc(up, 1)
                    pe.matmul(psR[:, :], w_qr[:, :], lat[0:DL, :], start=True, stop=True).then_inc(up, 1)
                    pe.matmul(psK[:, :], w_kv[DL:2 * DL, 0:P], lat[DL:2 * DL, :], start=True, stop=True).then_inc(up, 1)
                    for j in range(NT):
                        m = pe.matmul(psV[:, j * P:(j + 1) * P], lat[DL:2 * DL, j * P:(j + 1) * P],
                                      w_kv[DL:2 * DL, P:], start=True, stop=True)
                    m.then_inc(up, 1)

            @block.scalar
            def _(a):
                with a.Fori(0, B) as b:
                    nm.act(a, b, free=(down, b))
                    a.wait_ge(down, b + 1)
                    a.wait_ge(up, 4 * b)
                    a.copy(lat[0:2 * DL, :], psD[0:2 * DL, :]).then_inc(latent, 1)
                    sq.act(a, b, (up, 4 * b + 1), NC6)
                    sk.act(a, b, (up, 4 * b + 3), NC6)
                    a.wait_ge(up, 4 * b + 4)
                    a.copy(net.V[:, bass.ds(b * H, H), :, :].rearrange("p h j d -> p j h d"),
                           psV[:, :].rearrange("p (j h d) -> p j h d", j=NT, h=H)).then_inc(vals, 1)
                    sqr.act(a, b, (rqs, b + 1), NC6)
                    skr.act(a, b, (rks, b + 1), NC6)

            @block.vector
            def _(v):
                v.wait_ge(weights, 16 * 6)
                with v.Fori(0, B) as b:
                    nm.dve(v, b)
                    v.wait_ge(down, b + 1)
                    v.wait_ge(rks, b)
                    v.tensor_tensor(b1[:, :], psD[2 * DL:2 * DL + DR, :], rot[0:DR, :], ALU.mult).then_inc(rk, 1)
                    v.tensor_tensor(b2[:, :], psD[3 * DL:3 * DL + DR, :], rot[H * DR:H * DR + DR, :], ALU.mult).then_inc(rk, 1)
                    v.wait_ge(rk, 2 * b + 2)
                    v.wait_ge(skr.rest, b)
                    v.tensor_tensor(kr[:, :], b1[:, :], b2[:, :], ALU.add).then_inc(rks, 1)
                    v.wait_ge(up, 4 * b + 2)
                    v.wait_ge(rqs, b)
                    v.tensor_tensor(a1[:, :], psR[0:H * DR, :], rot[0:H * DR, :], ALU.mult).then_inc(rq, 1)
                    v.tensor_tensor(a2[:, :], psR[H * DR:, :], rot[H * DR:, :], ALU.mult).then_inc(rq, 1)
                    v.wait_ge(rq, 2 * b + 2)
                    v.wait_ge(sqr.rest, b)
                    v.tensor_tensor(qr[:, :], a1[:, :], a2[:, :], ALU.add).then_inc(rqs, 1)
                    sq.dve(v, b)
                    sk.dve(v, b)
                    sqr.dve(v, b)
                    skr.dve(v, b)

            @block.gpsimd
            def _(g):
                with g.Fori(0, B) as b:
                    nm.pool(g, b)
                    sq.pool(g, b)
                    sk.pool(g, b)
                    sqr.pool(g, b)
                    skr.pool(g, b)


U = 4


DIAG = (0, 512, 1024, 896)
CAUSAL = 1280


def heads_t(net, tag, width, clip, scale):
    nc = net.nc
    rows = NC6 * width
    N = B * H
    with Phase(net, tag) as ph:
        q = ph.sb("q", [rows, U, S], BF16)
        k = ph.sb("k", [rows, U, S], BF16)
        v1 = ph.sb("v1", [P, U, NT, VW])
        c = ph.sb("c", [P, 2, CAUSAL])
        w = ph.sb("w", [P, 2, CAUSAL])
        o = ph.sb("o", [P, S])
        sc = [ph.ps(f"sc{i}", [P, 3 * S]) for i in range(2)]
        po = ph.ps("po", [P, S])
        ld = [ph.sem(f"ld{u}") for u in range(U)]
        scored, clipped, weighed, masked, summed, copied, valued, stored, made = (
            ph.sem(x) for x in ("scored", "clipped", "weighed", "masked", "summed", "copied", "valued", "stored", "made"))
        READY = 2
        with nc.Block() as block:
            @block.sync
            def _(sp):
                with sp.Fori(0, N // U) as i:
                    for u in range(U):
                        sp.wait_ge(scored, U * i + u + 1)
                        sp.dma_start(q[:, u, :], net.QS[bass.ds(U * i + u, 1), 0:rows, :]).then_inc(ld[u], 16)
                        sp.dma_start(k[:, u, :], net.KS[bass.ds(U * i + u, 1), 0:rows, :]).then_inc(ld[u], 16)

            def scores(pe, i, u, n):
                s = sc[u % 2]
                pe.wait_ge(ld[u], 32 * i + 32)
                if clip is None:
                    pe.wait_ge(weighed, n + 1)
                else:
                    pe.wait_ge(clipped, n + 1)
                for J in range(NT):
                    m = pe.matmul(s[:, DIAG[J]:DIAG[J] + S - J * P], k[:, u, J * P:(J + 1) * P],
                                  q[:, u, J * P:], start=True, stop=True)
                m.then_inc(scored, 1)

            def context(pe, i, u, n):
                x = w[:, u % 2, :]
                pe.wait_ge(masked, n + 1)
                pe.wait_ge(valued, n + 1)
                if u == 0:
                    pe.wait_ge(copied, i)
                for J in range(NT):
                    m = pe.matmul(po[VW * u:VW * (u + 1), J * P:], v1[:, u, J, :], x[:, DIAG[J]:DIAG[J] + S - J * P],
                                  start=J == 0, stop=J == NT - 1)
                m.then_inc(summed, 1)

            @block.tensor
            def _(pe):
                pe.sem_inc(scored, U)
                pe.sem_inc(summed, U)
                scores(pe, 0, 0, 0)
                scores(pe, 0, 1, 1)
                with pe.Fori(0, N // U - 1) as i:
                    for u in range(U):
                        t = u + 2
                        scores(pe, i + t // U, t % U, U * i + t)
                        context(pe, i, u, U * i + u)
                for u in range(U):
                    if u + 2 < U:
                        scores(pe, N // U - 1, u + 2, N - U + u + 2)
                    context(pe, N // U - 1, u, N - U + u)

            @block.vector
            def _(v):
                if clip is not None:
                    v.sem_inc(clipped, 2)
                    with v.Fori(0, N // U) as i:
                        for u in range(U):
                            n = U * i + u
                            v.wait_ge(scored, n + U + 1)
                            v.wait_ge(weighed, n + 1)
                            v.tensor_scalar(c[:, u % 2, :], sc[u % 2][:, 0:CAUSAL], clip, -clip, ALU.min, ALU.max)\
                                .then_inc(clipped, 1)

            @block.scalar
            def _(a):
                a.sem_inc(weighed, 2)
                with a.Fori(0, N // U) as i:
                    for u in range(U):
                        n = U * i + u
                        a.wait_ge(summed, n + U - 1)
                        if clip is not None:
                            a.wait_ge(clipped, n + 3)
                            a.activation(w[:, u % 2, :], c[:, u % 2, :], ACT.Exp, scale=scale).then_inc(weighed, 1)
                        else:
                            a.wait_ge(scored, n + U + 1)
                            a.copy(w[:, u % 2, :], sc[u % 2][:, 0:CAUSAL]).then_inc(weighed, 1)
                    a.wait_ge(summed, U * i + 2 * U)
                    a.wait_ge(stored, 16 * U * i)
                    a.copy(o[:, :], po[:, :]).then_inc(copied, 1)
                    a.wait_ge(copied, i + 1)
                    for u in range(U):
                        a.dma_start(net.CU[bass.ds(U * i + u, 1), :, :], o[VW * u:VW * u + 2 * DH, :]).then_inc(stored, 16)
                a.wait_ge(stored, 16 * N)

            @block.gpsimd
            def _(g):
                g.memset(v1[:, :, :, :], 0.0).then_inc(made, 1)
                g.wait_ge(made, 1)
                g.memset(v1[:, :, :, DH:2 * DH], 1.0).then_inc(made, 1)
                g.wait_ge(made, 2)
                with g.Fori(0, N // U) as i:
                    for u in range(U):
                        n = U * i + u
                        waited(net, g, (summed, n + 1))
                        g.tensor_copy(v1[:, u, :, 0:DH], net.V[:, bass.ds(n, 1), :, :].rearrange("p o j d -> p (o j) d"))\
                            .then_inc(valued, 1)
                        waited(net, g, (weighed, n + 3))
                        for J in range(NT):
                            x = w[:, u % 2, DIAG[J]:DIAG[J] + P]
                            m = g.affine_select(out=x, in_=x, compare_op=ALU.is_ge, fill=0.0, base=0,
                                                pattern=[[1, P]], channel_multiplier=-1)
                        m.then_inc(masked, 1)



class Attended:

    def __init__(self, ph, psY, wo, bo=None, floor=None):
        self.net, self.psY, self.wo_dram, self.bo_dram, self.floor = ph.net, psY, wo, bo, floor
        self.wo = ph.sb("wo", [P, D])
        self.bo = ph.sb("bo", [1, D])
        self.num = ph.sb("num", [P, S])
        self.den = ph.sb("den", [P, S])
        self.ctx = ph.sb("ctxT", [P, S])
        self.w, self.loaded, self.floored, self.inverted, self.divided, self.out, self.added = (
            ph.sem("at_" + x) for x in ("w", "loaded", "floored", "inverted", "divided", "out", "added"))

    def weights(self, sp):
        sp.dma_start(self.wo[:, :], self.wo_dram).then_inc(self.w, 16)
        if self.bo_dram is not None:
            sp.dma_start(self.bo[:, :], self.bo_dram.unsqueeze(0)).then_inc(self.w, 16)

    def load(self, sp, b):
        sp.wait_ge(self.divided, b)
        for dst, r in ((self.num, 0), (self.den, DH)):
            sp.dma_start(dst[:, :], self.net.CU[bass.ds(b * H, H), r:r + DH, :]).then_inc(self.loaded, 16)

    def dve_divide(self, v, b):
        v.wait_ge(self.loaded, 32 * b + 32)
        if self.floor is not None:
            v.tensor_scalar(self.den[:, :], self.den[:, :], self.floor, None, ALU.max).then_inc(self.floored, 1)
            v.wait_ge(self.floored, b + 1)
        v.reciprocal(self.den[:, :], self.den[:, :]).then_inc(self.inverted, 1)
        v.wait_ge(self.inverted, b + 1)
        v.wait_ge(self.out, b)
        v.tensor_tensor(self.ctx[:, :], self.num[:, :], self.den[:, :], ALU.mult).then_inc(self.divided, 1)

    def pe(self, pe, b):
        pe.wait_ge(self.w, 32 if self.bo_dram is not None else 16)
        pe.wait_ge(self.divided, b + 1)
        pe.wait_ge(self.added, b)
        for j in range(NT):
            y = self.psY[:, j * P:(j + 1) * P]
            m = pe.matmul(y, self.ctx[:, j * P:(j + 1) * P], self.wo[:, :], start=True, stop=self.bo_dram is None)
            if self.bo_dram is not None:
                m = pe.matmul(y, self.net.ones[:, 0:P], self.bo[:, :], start=False, stop=True)
        m.then_inc(self.out, 1)

    def dve_add(self, v, b):
        x = self.net.X[:, bass.ds(b * NT, NT), :]
        v.wait_ge(self.out, b + 1)
        v.tensor_tensor(x, x, self.psY[:, :].rearrange("p (j d) -> p j d", j=NT), ALU.add).then_inc(self.added, 1)
        v.wait_ge(self.added, b + 1)


def moe_top2(net, tag, attended):
    nc, aps = net.nc, net.aps
    with Phase(net, tag) as ph:
        psT, psY, psG, psB = (ph.ps(n, [P, S]) for n in ("psT", "psY", "psG", "psB"))
        psE = [[ph.ps(f"psE{r}{x}", [P, S]) for x in range(2)] for r in range(2)]
        at = Attended(ph, psY, *attended)
        nm = Norm(ph, "n", psT)
        wg = ph.sb("wg", [D, E])
        bg = ph.sb("bg", [1, E])
        we = ph.sb("we", [D, E * D])
        be = ph.sb("be", [E, D])
        small = lambda n, shape: ph.sb(n, [P, NT] + shape)
        mx, z, ex, sm, pr, gt, eq, cnt, gate = (small(n, x) for n, x in (
            ("mx", []), ("z", [E]), ("ex", [E]), ("sm", []), ("pr", [E]), ("gt", [E, E]), ("eq", [E, E]), ("cnt", [E]), ("gate", [E])))
        before = ph.sb("before", [P, E, E])
        gT = ph.sb("gT", [E, S])
        acc = ph.sb("acc", [P, 2, D])
        weights, made, logits, shifted, powered, gated, turned, gready, biased, mixed, summed, step, astep = (ph.sem(x) for x in
            ("weights", "made", "logits", "shifted", "powered", "gated", "turned", "gready", "biased", "mixed", "summed", "step", "astep"))
        STEPS, ASTEPS = 11, NT * (E + 1)

        with nc.Block() as block:
            @block.sync
            def _(sp):
                at.weights(sp)
                sp.dma_start(wg[:, :], aps["L0_ffn_Wg"]).then_inc(weights, 16)
                sp.dma_start(bg[:, :], aps["L0_ffn_bg"].unsqueeze(0)).then_inc(weights, 16)
                sp.dma_start(we[:, :], aps["WeT"]).then_inc(weights, 16)
                sp.dma_start(be[:, :], aps["L0_ffn_be"]).then_inc(weights, 16)
                with sp.Fori(0, B) as b:
                    at.load(sp, b)

            @block.tensor
            def _(pe):
                pe.wait_ge(weights, 64)
                with pe.Fori(0, B) as b:
                    at.pe(pe, b)
                    nm.pe(pe, b)
                    pe.wait_ge(nm.ready, b + 1)
                    pe.wait_ge(shifted, b)
                    for j in range(NT):
                        g = psG[:, j * E:(j + 1) * E]
                        pe.matmul(g, nm.xT[:, j * P:(j + 1) * P], wg[:, :], start=True, stop=False)
                        m = pe.matmul(g, net.ones[:, 0:P], bg[:, :], start=False, stop=True)
                    m.then_inc(logits, 1)

                    def experts(j):
                        t = NT * b + j
                        pe.wait_ge(summed, t + 1)
                        for x in range(2):
                            m = pe.matmul(psE[j % 2][x][:, :], nm.xT[:, j * P:(j + 1) * P], we[:, x * S:(x + 1) * S],
                                          start=True, stop=True)
                        m.then_inc(mixed, 1)

                    experts(0)
                    experts(1)
                    pe.wait_ge(gated, b + 1)
                    pe.wait_ge(nm.ready, b + 1)
                    for j in range(NT):
                        m = pe.transpose(psT[0:E, j * P:(j + 1) * P], gate[:, j, :], net.idf[:, :])
                    m.then_inc(turned, 1)
                    pe.wait_ge(gready, b + 1)
                    pe.wait_ge(summed, NT * b + 2)
                    for j in range(NT):
                        m = pe.matmul(psB[:, j * P:(j + 1) * P], gT[:, j * P:(j + 1) * P], be[:, :], start=True, stop=True)
                    m.then_inc(biased, 1)
                    experts(2)
                    experts(3)

            @block.scalar
            def _(a):
                with a.Fori(0, B) as b:
                    nm.act(a, b, free=(mixed, NT * b))
                    a.wait_ge(shifted, b + 1)
                    a.activation(ex[:, :, :], z[:, :, :], ACT.Exp).then_inc(powered, 1)
                    a.wait_ge(turned, b + 1)
                    a.wait_ge(biased, b)
                    a.copy(gT[:, :], psT[0:E, :]).then_inc(gready, 1)

            @block.vector
            def _(v):
                v.sem_inc(summed, 2)
                v.wait_ge(made, 2)
                with v.Fori(0, B) as b:
                    done = [0]

                    def then(ins, sem=None):
                        done[0] += 1
                        ins.then_inc(step, 1)
                        v.wait_ge(step, STEPS * b + done[0])

                    at.dve_divide(v, b)
                    at.dve_add(v, b)
                    nm.dve(v, b)
                    v.wait_ge(logits, b + 1)
                    pg = psG[:, 0:NT * E].rearrange("p (j e) -> p j e", j=NT)
                    then(v.tensor_reduce(mx[:, :], pg, AX, ALU.max))
                    v.tensor_tensor(z[:, :, :], pg, over(mx[:, :], 2, E), ALU.subtract).then_inc(shifted, 1)
                    v.wait_ge(powered, b + 1)
                    then(v.reduce_sum(sm[:, :], ex[:, :, :], AX))
                    then(v.reciprocal(sm[:, :], sm[:, :]))
                    then(v.tensor_tensor(pr[:, :, :], ex[:, :, :], over(sm[:, :], 2, E), ALU.mult))
                    v.tensor_tensor(gt[:, :, :, :], over(pr[:, :, :], 2, E), over(pr[:, :, :], 3, E), ALU.is_gt)
                    then(v.tensor_tensor(eq[:, :, :, :], over(pr[:, :, :], 2, E), over(pr[:, :, :], 3, E), ALU.is_equal))
                    then(v.tensor_tensor(eq[:, :, :, :], eq[:, :, :, :], over(before[:, :, :], 1, NT), ALU.mult))
                    then(v.tensor_tensor(gt[:, :, :, :], gt[:, :, :, :], eq[:, :, :, :], ALU.add))
                    then(v.reduce_sum(cnt[:, :, :], gt[:, :, :, :], AX))
                    v.wait_ge(turned, b)
                    then(v.scalar_tensor_tensor(gate[:, :, :], cnt[:, :, :], 1.5, pr[:, :, :], ALU.is_lt, ALU.mult))
                    then(v.reduce_sum(sm[:, :], gate[:, :, :], AX))
                    then(v.reciprocal(mx[:, :], sm[:, :]))
                    v.tensor_tensor(gate[:, :, :], gate[:, :, :], over(mx[:, :], 2, E), ALU.mult).then_inc(gated, 1)
                    v.wait_ge(gated, b + 1)
                    v.wait_ge(biased, b + 1)
                    n = 0
                    for j in range(NT):
                        x = net.X[:, bass.ds(b * NT + j, 1), :].rearrange("p o d -> p (o d)")
                        v.tensor_tensor(acc[:, 0, :], psB[:, j * P:(j + 1) * P], x, ALU.add).then_inc(astep, 1)
                        n += 1
                        v.wait_ge(mixed, NT * b + j + 1)
                        for e in range(E):
                            v.wait_ge(astep, ASTEPS * b + n)
                            m = v.scalar_tensor_tensor(x if e == E - 1 else acc[:, (e + 1) % 2, :],
                                                       psE[j % 2][e // 4][:, (e % 4) * P:(e % 4 + 1) * P],
                                                       gate[:, j, e:e + 1], acc[:, e % 2, :], ALU.mult, ALU.add)
                            if e == E - 1:
                                m.then_inc(summed, 1)
                                v.wait_ge(summed, NT * b + j + 3)
                                v.sem_inc(astep, 1)
                            else:
                                m.then_inc(astep, 1)
                            n += 1

            @block.gpsimd
            def _(g):
                g.memset(before[:, :, :], 1.0).then_inc(made, 1)
                g.wait_ge(made, 1)
                g.affine_select(out=before[:, :, :], in_=before[:, :, :], compare_op=ALU.is_gt, fill=0.0, base=0,
                                pattern=[[1, E], [-1, E]], channel_multiplier=0).then_inc(made, 1)
                with g.Fori(0, B) as b:
                    nm.pool(g, b)



def biased(pe, net, out, lhsT, rhs, row, bias_on_rows):
    pe.matmul(out, lhsT, rhs, start=True, stop=False)
    if bias_on_rows:
        return pe.matmul(out, row, net.ones[:, 0:S], start=False, stop=True)
    return pe.matmul(out, net.ones[:, 0:P], row, start=False, stop=True)


def values_out(net, a, psV, b):
    return a.copy(net.V[:, bass.ds(b * H, H), :, :].rearrange("p h j d -> p j h d"),
                  psV[:, :].rearrange("p (j h d) -> p j h d", j=NT, h=H))


def linear_prep(net):
    nc, aps = net.nc, net.aps
    with Phase(net, "la") as ph:
        w = ph.sb("w", [D, 3, D])
        bias = ph.sb("bias", [1, 3, D])
        low, ex, f = ph.sb("low", [P, 2, S]), ph.sb("ex", [P, 2, S]), ph.sb("f", [P, 2, S])
        psT, psQ, psK, psV = (ph.ps(n, [P, S]) for n in ("psT", "psQ", "psK", "psV"))
        nm = Norm(ph, "n", psT)
        sp_q = Split(ph, "q", P, f[:, 0, :])
        sp_k = Split(ph, "k", P, f[:, 1, :])
        weights, proj, clipped, powered, mapped, vals = (ph.sem(x) for x in
            ("weights", "proj", "clipped", "powered", "mapped", "vals"))
        with nc.Block() as block:
            @block.sync
            def _(sp):
                for n, x in enumerate("qkv"):
                    sp.dma_start(w[:, n, :], aps[f"L1a_W{x}T"]).then_inc(weights, 16)
                    sp.dma_start(bias[:, n, :], aps[f"L1_attn_a_b{x}"].unsqueeze(0)).then_inc(weights, 16)
                with sp.Fori(0, B) as b:
                    sp_q.store(sp, b, net.QS, LPART, DH, 0, DH)
                    sp_k.store(sp, b, net.KS, RPART, DH, 0, DH)
                for s in (sp_q, sp_k):
                    sp.wait_ge(s.kept, 16 * NC6 * B)

            @block.tensor
            def _(pe):
                pe.wait_ge(weights, 16 * 6)
                with pe.Fori(0, B) as b:
                    nm.pe(pe, b)
                    pe.wait_ge(nm.ready, b + 1)
                    pe.wait_ge(mapped, 2 * b)
                    pe.wait_ge(vals, b)
                    biased(pe, net, psQ[:, :], w[:, 0, :], nm.xT[:, :], bias[:, 0, :], True).then_inc(proj, 1)
                    biased(pe, net, psK[:, :], w[:, 1, :], nm.xT[:, :], bias[:, 1, :], True).then_inc(proj, 1)
                    for j in range(NT):
                        m = biased(pe, net, psV[:, j * P:(j + 1) * P], nm.xT[:, j * P:(j + 1) * P], w[:, 2, :],
                                   bias[:, 2, :], False)
                    m.then_inc(proj, 1)

            @block.scalar
            def _(a):
                with a.Fori(0, B) as b:
                    nm.act(a, b, free=(proj, 3 * b))
                    for n in range(2):
                        a.wait_ge(clipped, 2 * b + n + 1)
                        a.wait_ge(mapped, 2 * b)
                        a.activation(ex[:, n, :], low[:, n, :], ACT.Exp).then_inc(powered, 1)
                    a.wait_ge(proj, 3 * b + 3)
                    values_out(net, a, psV, b).then_inc(vals, 1)
                    sp_q.act(a, b, (mapped, 2 * b + 1), NC6)
                    sp_k.act(a, b, (mapped, 2 * b + 2), NC6)

            @block.vector
            def _(v):
                with v.Fori(0, B) as b:
                    nm.dve(v, b)
                    v.wait_ge(powered, 2 * b)
                    for n, ps in enumerate((psQ, psK)):
                        v.wait_ge(proj, 3 * b + n + 1)
                        v.tensor_scalar(low[:, n, :], ps[:, :], 0.0, None, ALU.min).then_inc(clipped, 1)
                    for n, (ps, s) in enumerate(((psQ, sp_q), (psK, sp_k))):
                        v.wait_ge(powered, 2 * b + n + 1)
                        v.wait_ge(s.rest, b)
                        v.scalar_tensor_tensor(f[:, n, :], ps[:, :], 0.0, ex[:, n, :], ALU.max, ALU.add).then_inc(mapped, 1)
                    sp_q.dve(v, b)
                    sp_k.dve(v, b)

            @block.gpsimd
            def _(g):
                with g.Fori(0, B) as b:
                    nm.pool(g, b)
                    sp_q.pool(g, b)
                    sp_k.pool(g, b)


def relative_tables(net, keep):
    nc, aps = net.nc, net.aps
    with Phase(net, "rt") as ph:
        w = ph.sb("w", [D, 2, D])
        bias = ph.sb("bias", [1, 2, D])
        rel = ph.sb("rel", [D, 2, P])
        tab = ph.sb("tab", [P, TW])
        r1 = ph.sb("r1", [P, TW])
        part = ph.sb("part", [P, 3, TW], BF16)
        zero = ph.sb("zero", [P, P])
        psP, psQ = ph.ps("psP", [P, P]), ph.ps("psQ", [P, P])
        weights, proj, filled, first, rest, second, third, kept, zeroed = (ph.sem(x) for x in
            ("weights", "proj", "filled", "first", "rest", "second", "third", "kept", "zeroed"))
        with nc.Block() as block:
            @block.sync
            def _(sp):
                for n, x in enumerate(("k", "q")):
                    sp.dma_start(w[:, n, :], aps[f"L0b_Wp{x}T"]).then_inc(weights, 16)
                    sp.dma_start(bias[:, n, :], aps[f"L0_attn_b_bp{x}"].unsqueeze(0)).then_inc(weights, 16)
                sp.dma_start(rel[:, 0, :], aps["relT"]).then_inc(weights, 16)
                sp.dma_start(rel[:, 1, :], aps["relT_reversed"]).then_inc(weights, 16)
                sp.wait_ge(third, 1)
                for c in range(NC6):
                    r = net.TB[:, c * DH:(c + 1) * DH, :]
                    sp.dma_start(r[:, :, 0:EXT], part[:, RPART[c], 0:EXT]).then_inc(kept, 16)
                    sp.dma_start(r[:, :, EXT:], part[:, LPART[c], EXT:]).then_inc(kept, 16)
                sp.wait_ge(kept, 32 * NC6)

            @block.tensor
            def _(pe):
                pe.wait_ge(weights, 16 * 6)
                for n, ps in enumerate((psP, psQ)):
                    pe.matmul(ps[:, :], w[:, n, :], rel[:, n, :], start=True, stop=False)
                    pe.matmul(ps[:, :], bias[:, n, :], net.ones[:, 0:P], start=False, stop=True).then_inc(proj, 1)

            @block.vector
            def _(v):
                v.memset(zero[:, :], 0.0).then_inc(zeroed, 1)
                v.wait_ge(zeroed, 1)
                v.wait_ge(proj, 2)
                z = zero[:, :]
                fill = lambda lo, hi, col: v.tensor_scalar(tab[:, lo:hi], zero[:, 0:hi - lo], col, None, ALU.add).then_inc(filled, 1)
                first_k, last_k, first_q, last_q = psP[:, 0:1], psP[:, P - 1:P], psQ[:, P - 1:P], psQ[:, 0:1]
                fill(0, P - 1, first_k)
                v.tensor_copy(tab[:, P - 1:2 * P - 1], psP[:, :]).then_inc(filled, 1)
                fill(2 * P - 1, 3 * P - 1, last_k)
                fill(3 * P - 1, 3 * P, last_k)
                fill(EXT, EXT + P, last_q)
                v.tensor_copy(tab[:, EXT + P:EXT + 2 * P], psQ[:, :]).then_inc(filled, 1)
                fill(EXT + 2 * P, 2 * EXT, first_q)
                fill(2 * EXT, 2 * EXT + P, first_q)
                fill(2 * EXT + P, TW, last_q)
                v.wait_ge(filled, 9)
                v.tensor_copy(keep[:, 0:1], tab[:, 0:1])
                v.tensor_copy(keep[:, 1:2], tab[:, EXT - 1:EXT])
                v.tensor_copy(part[:, 0, :], tab[:, :]).then_inc(first, 1)
                v.wait_ge(first, 1)
                v.tensor_tensor(r1[:, :], tab[:, :], part[:, 0, :], ALU.subtract).then_inc(rest, 1)
                v.wait_ge(rest, 1)
                v.tensor_copy(part[:, 1, :], r1[:, :]).then_inc(second, 1)
                v.wait_ge(second, 1)
                v.tensor_tensor(part[:, 2, :], r1[:, :], part[:, 1, :], ALU.subtract).then_inc(third, 1)


def relative_prep(net, keep):
    nc, aps = net.nc, net.aps
    with Phase(net, "ra") as ph:
        w = ph.sb("w", [D, 3, D])
        bias = ph.sb("bias", [1, 3, D])
        far = ph.sb("far", [P, 2, FAR])
        psT, psQ, psK, psV = (ph.ps(n, [P, S]) for n in ("psT", "psQ", "psK", "psV"))
        nm = Norm(ph, "n", psT)
        sp_q = Split(ph, "q", P, psQ[:, :])
        sp_k = Split(ph, "k", P, psK[:, :])
        sp_l = Split(ph, "l", P, far[:, 0, :], FAR)
        sp_h = Split(ph, "h", P, far[:, 1, :], FAR)
        weights, proj, shifted, vals = (ph.sem(x) for x in ("weights", "proj", "shifted", "vals"))
        with nc.Block() as block:
            @block.sync
            def _(sp):
                for n, x in enumerate("qkv"):
                    sp.dma_start(w[:, n, :], aps[f"L0b_W{x}T"]).then_inc(weights, 16)
                    sp.dma_start(bias[:, n, :], aps[f"L0_attn_b_b{x}"].unsqueeze(0)).then_inc(weights, 16)
                with sp.Fori(0, B) as b:
                    sp_q.store(sp, b, net.QS, LPART, DH, 0, DH)
                    sp_k.store(sp, b, net.KS, RPART, DH, 0, DH)
                    sp_l.store(sp, b, net.KLS, RPART, DH, 0, DH)
                    sp_h.store(sp, b, net.KHS, RPART, DH, 0, DH)
                for s in (sp_q, sp_k, sp_l, sp_h):
                    sp.wait_ge(s.kept, 16 * NC6 * B)

            @block.tensor
            def _(pe):
                pe.wait_ge(weights, 16 * 6)
                with pe.Fori(0, B) as b:
                    nm.pe(pe, b)
                    pe.wait_ge(nm.ready, b + 1)
                    pe.wait_ge(sp_q.rest, b)
                    pe.wait_ge(sp_k.rest, b)
                    pe.wait_ge(shifted, 2 * b)
                    pe.wait_ge(vals, b)
                    biased(pe, net, psQ[:, :], w[:, 0, :], nm.xT[:, :], bias[:, 0, :], True).then_inc(proj, 1)
                    biased(pe, net, psK[:, :], w[:, 1, :], nm.xT[:, :], bias[:, 1, :], True).then_inc(proj, 1)
                    for j in range(NT):
                        m = biased(pe, net, psV[:, j * P:(j + 1) * P], nm.xT[:, j * P:(j + 1) * P], w[:, 2, :],
                                   bias[:, 2, :], False)
                    m.then_inc(proj, 1)

            @block.scalar
            def _(a):
                with a.Fori(0, B) as b:
                    nm.act(a, b, free=(proj, 3 * b))
                    sp_q.act(a, b, (proj, 3 * b + 1), NC6)
                    sp_k.act(a, b, (proj, 3 * b + 2), NC6)
                    a.wait_ge(proj, 3 * b + 3)
                    values_out(net, a, psV, b).then_inc(vals, 1)
                    sp_l.act(a, b, (shifted, 2 * b + 1), NC6)
                    sp_h.act(a, b, (shifted, 2 * b + 2), NC6)

            @block.vector
            def _(v):
                with v.Fori(0, B) as b:
                    nm.dve(v, b)
                    sp_q.dve(v, b)
                    sp_k.dve(v, b)
                    v.wait_ge(sp_k.rest, b + 1)
                    for n, s in enumerate((sp_l, sp_h)):
                        v.wait_ge(s.rest, b)
                        v.tensor_scalar(far[:, n, :], psK[:, n * (S - FAR):n * (S - FAR) + FAR], keep[:, n:n + 1], None, ALU.add)\
                            .then_inc(shifted, 1)
                    sp_l.dve(v, b)
                    sp_h.dve(v, b)

            @block.gpsimd
            def _(g):
                with g.Fori(0, B) as b:
                    nm.pool(g, b)
                    for s in (sp_q, sp_k, sp_l, sp_h):
                        s.pool(g, b)



def rotary_prep(net):
    nc, aps = net.nc, net.aps
    with Phase(net, "ya") as ph:
        w = ph.sb("w", [D, 6, D])
        wi = ph.sb("wi", [D, 3, D])
        bias = ph.sb("bias", [1, 3, D])
        rot = ph.sb("rot", [D, 2, S])
        t = ph.sb("t", [D, 2, S])
        turned = ph.sb("turned", [D, 3, S])
        psT, psQ, psK, psV, psA, psB = (ph.ps(n, [P, S]) for n in ("psT", "psQ", "psK", "psV", "psA", "psB"))
        nm = Norm(ph, "n", psT)
        sp_q = Split(ph, "q", P, psQ[:, :])
        sp_k = Split(ph, "k", P, psK[:, :])
        weights, first, products, rotated, proj, vals = (ph.sem(x) for x in
            ("weights", "first", "products", "rotated", "proj", "vals"))
        with nc.Block() as block:
            @block.sync
            def _(sp):
                sp.dma_start(w[:, :, :], aps["L1b_w"]).then_inc(weights, 16)
                sp.dma_start(wi[:, :, :], aps["L1b_in"]).then_inc(weights, 16)
                sp.dma_start(bias[:, :, :], aps["L1_attn_b_in_proj_b"].rearrange("(o n d) -> o n d", o=1, n=3)).then_inc(weights, 16)
                sp.dma_start(rot[:, :, :], aps["L1b_rot"]).then_inc(weights, 16)
                with sp.Fori(0, B) as b:
                    sp_q.store(sp, b, net.QS, LPART, DH, 0, DH)
                    sp_k.store(sp, b, net.KS, RPART, DH, 0, DH)
                for s in (sp_q, sp_k):
                    sp.wait_ge(s.kept, 16 * NC6 * B)

            @block.tensor
            def _(pe):
                pe.wait_ge(weights, 64)
                with pe.Fori(0, B) as b:
                    nm.pe(pe, b)
                    pe.wait_ge(nm.ready, b + 1)
                    for n in range(3):
                        pe.wait_ge(products, 6 * b + 2 * n)
                        pe.matmul(psA[:, :], w[:, 2 * n, :], nm.xT[:, :], start=True, stop=True)
                        pe.matmul(psB[:, :], w[:, 2 * n + 1, :], nm.xT[:, :], start=True, stop=True).then_inc(first, 1)
                    pe.wait_ge(sp_q.rest, b)
                    pe.wait_ge(sp_k.rest, b)
                    pe.wait_ge(vals, b)
                    for n, ps in enumerate((psQ, psK)):
                        pe.wait_ge(rotated, 3 * b + n + 1)
                        biased(pe, net, ps[:, :], wi[:, n, :], turned[:, n, :], bias[:, n, :], True).then_inc(proj, 1)
                    pe.wait_ge(rotated, 3 * b + 3)
                    for j in range(NT):
                        m = biased(pe, net, psV[:, j * P:(j + 1) * P], turned[:, 2, j * P:(j + 1) * P], wi[:, 2, :],
                                   bias[:, 2, :], False)
                    m.then_inc(proj, 1)

            @block.scalar
            def _(a):
                with a.Fori(0, B) as b:
                    nm.act(a, b, free=(first, 3 * b))
                    sp_q.act(a, b, (proj, 3 * b + 1), NC6)
                    sp_k.act(a, b, (proj, 3 * b + 2), NC6)
                    a.wait_ge(proj, 3 * b + 3)
                    values_out(net, a, psV, b).then_inc(vals, 1)

            @block.vector
            def _(v):
                v.wait_ge(weights, 64)
                with v.Fori(0, B) as b:
                    nm.dve(v, b)
                    v.wait_ge(proj, 3 * b)
                    for n in range(3):
                        v.wait_ge(first, 3 * b + n + 1)
                        v.wait_ge(rotated, 3 * b + n)
                        for i, ps in enumerate((psA, psB)):
                            v.tensor_tensor(t[:, i, :], ps[:, :], rot[:, i, :], ALU.mult).then_inc(products, 1)
                        v.wait_ge(products, 6 * b + 2 * n + 2)
                        v.tensor_tensor(turned[:, n, :], t[:, 0, :], t[:, 1, :], ALU.add).then_inc(rotated, 1)
                    sp_q.dve(v, b)
                    sp_k.dve(v, b)

            @block.gpsimd
            def _(g):
                with g.Fori(0, B) as b:
                    nm.pool(g, b)
                    sp_q.pool(g, b)
                    sp_k.pool(g, b)


QDIAG = (896, 1024, 512, 0)


def heads_max(net, tag, scale):
    nc = net.nc
    rows, N = NC6 * DH, B * H
    with Phase(net, tag) as ph:
        q = ph.sb("q", [rows, U, S], BF16)
        k = ph.sb("k", [rows, U, S], BF16)
        v1 = ph.sb("v1", [P, U, NT, VW])
        mx = ph.sb("mx", [P, 2, NT])
        nm = ph.sb("nm", [P, 2, NT])
        e = ph.sb("e", [P, 2, CAUSAL])
        w = ph.sb("w", [P, 2, CAUSAL])
        o = ph.sb("o", [P, S])
        sc = ph.ps("sc", [P, 3 * S])
        tr = ph.ps("tr", [P, 3 * S])
        po = ph.ps("po", [P, S])
        ld = [ph.sem(f"ld{u}") for u in range(U)]
        scored, found, negated, powered, turned, weighed, summed, copied, valued, stored, made = (ph.sem(x) for x in
            ("scored", "found", "negated", "powered", "turned", "weighed", "summed", "copied", "valued", "stored", "made"))
        with nc.Block() as block:
            @block.sync
            def _(sp):
                with sp.Fori(0, N // U) as i:
                    for u in range(U):
                        sp.wait_ge(scored, U * i + u + 1)
                        sp.dma_start(q[:, u, :], net.QS[bass.ds(U * i + u, 1), 0:rows, :]).then_inc(ld[u], 16)
                        sp.dma_start(k[:, u, :], net.KS[bass.ds(U * i + u, 1), 0:rows, :]).then_inc(ld[u], 16)

            def scores(pe, i, u, n):
                pe.wait_ge(ld[u], 32 * i + 32)
                pe.wait_ge(powered, NT * n)
                for I in reversed(range(NT)):
                    at, width = QDIAG[I], (I + 1) * P
                    pe.matmul(sc[:, at:at + width], q[:, u, I * P:width], k[:, u, 0:width], start=True, stop=False)
                    m = pe.matmul(sc[:, at + I * P:at + width], net.idb[:, :], net.negb[:, :], start=False, stop=True)
                m.then_inc(scored, 1)

            def turn(pe, u, n):
                pe.wait_ge(powered, NT * n + NT)
                pe.wait_ge(weighed, n)
                for J in range(NT):
                    for I in range(J, NT):
                        at, to = QDIAG[I] + J * P, DIAG[J] + (I - J) * P
                        m = pe.transpose(tr[:, to:to + P], e[:, u % 2, at:at + P], net.idf[:, :])
                m.then_inc(turned, 1)

            def context(pe, i, u, n):
                pe.wait_ge(weighed, n + 1)
                pe.wait_ge(valued, n + 1)
                if u == 0:
                    pe.wait_ge(copied, i)
                for J in range(NT):
                    m = pe.matmul(po[VW * u:VW * (u + 1), J * P:], v1[:, u, J, :],
                                  w[:, u % 2, DIAG[J]:DIAG[J] + S - J * P], start=J == 0, stop=J == NT - 1)
                m.then_inc(summed, 1)

            @block.tensor
            def _(pe):
                pe.sem_inc(scored, U)
                pe.sem_inc(summed, U)
                scores(pe, 0, 0, 0)
                turn(pe, 0, 0)
                with pe.Fori(0, N // U - 1) as i:
                    for u in range(U):
                        t = u + 1
                        scores(pe, i + t // U, t % U, U * i + t)
                        context(pe, i, u, U * i + u)
                        turn(pe, t, U * i + t)
                for u in range(U):
                    if u + 1 < U:
                        scores(pe, N // U - 1, u + 1, N - U + u + 1)
                    context(pe, N // U - 1, u, N - U + u)
                    if u + 1 < U:
                        turn(pe, u + 1, N - U + u + 1)

            @block.vector
            def _(v):
                with v.Fori(0, N // U) as i:
                    for u in range(U):
                        n = U * i + u
                        v.wait_ge(scored, n + U + 1)
                        for I in range(NT):
                            m = v.tensor_reduce(mx[:, u % 2, I:I + 1], sc[:, QDIAG[I]:QDIAG[I] + (I + 1) * P], AX, ALU.max)
                        m.then_inc(found, 1)
                        v.wait_ge(found, n + 1)
                        v.tensor_scalar(nm[:, u % 2, :], mx[:, u % 2, :], -scale, None, ALU.mult).then_inc(negated, 1)
                        v.wait_ge(turned, n + 1)
                        v.wait_ge(summed, n + U - 1)
                        v.tensor_copy(w[:, u % 2, :], tr[:, 0:CAUSAL]).then_inc(weighed, 1)

            @block.scalar
            def _(a):
                with a.Fori(0, N // U) as i:
                    for u in range(U):
                        n = U * i + u
                        a.wait_ge(negated, n + 1)
                        if u >= 2:
                            a.wait_ge(turned, n - 1)
                        else:
                            a.wait_ge(turned, U * i)
                        for I in range(NT):
                            a.activation(e[:, u % 2, QDIAG[I]:QDIAG[I] + (I + 1) * P], sc[:, QDIAG[I]:QDIAG[I] + (I + 1) * P],
                                         ACT.Exp, bias=nm[:, u % 2, I:I + 1], scale=scale).then_inc(powered, 1)
                    a.wait_ge(summed, U * i + 2 * U)
                    a.wait_ge(stored, 16 * U * i)
                    a.copy(o[:, :], po[:, :]).then_inc(copied, 1)
                    a.wait_ge(copied, i + 1)
                    for u in range(U):
                        a.dma_start(net.CU[bass.ds(U * i + u, 1), :, :], o[VW * u:VW * u + 2 * DH, :]).then_inc(stored, 16)
                a.wait_ge(stored, 16 * N)

            @block.gpsimd
            def _(g):
                g.memset(v1[:, :, :, :], 0.0).then_inc(made, 1)
                g.wait_ge(made, 1)
                g.memset(v1[:, :, :, DH:2 * DH], 1.0).then_inc(made, 1)
                g.wait_ge(made, 2)
                with g.Fori(0, N // U) as i:
                    for u in range(U):
                        n = U * i + u
                        waited(net, g, (summed, n + 1))
                        g.tensor_copy(v1[:, u, :, 0:DH], net.V[:, bass.ds(n, 1), :, :].rearrange("p o j d -> p (o j) d"))\
                            .then_inc(valued, 1)


C1, C2 = NT * P, (NT - 1) * P


def heads_relative(net, tag, scale):
    nc = net.nc
    rows = NC6 * DH
    G = 16
    with Phase(net, tag) as ph:
        q = ph.sb("q", [rows, B, S], BF16)
        k = ph.sb("k", [rows, B, S], BF16)
        kl = ph.sb("kl", [rows, B, FAR], BF16)
        kh = ph.sb("kh", [rows, B, FAR], BF16)
        tb = ph.sb("tb", [rows, TW], BF16)
        c0 = ph.sb("c0", [P, B, NT, P])
        c1 = ph.sb("c1", [P, B, NT - 1, P])
        d0 = ph.sb("d0", [P, B, NT, P])
        d1 = ph.sb("d1", [P, B, NT - 1, P])
        bf = ph.sb("bf", [P, NT * (S + P)])
        v1 = ph.sb("v1", [P, B, NT, VW])
        mx = ph.sb("mx", [P, NT])
        nm = ph.sb("nm", [P, NT])
        ss = ph.sb("ss", [P, NT, S])
        e = ph.sb("e", [P, NT, S])
        w = ph.sb("w", [P, 2, S])
        o = ph.sb("o", [P, S])
        sc = [ph.ps(f"sc{i}", [P, S]) for i in range(2)]
        pc = [ph.ps(f"pc{i}", [P, S]) for i in range(2)]
        tr = [ph.ps(f"tr{i}", [P, S]) for i in range(2)]
        po = ph.ps("po", [P, S])
        names = ("stacks", "tabled", "ctab", "dtab", "turned", "biased", "scored", "full", "negated", "powered",
                 "blocks", "weighed", "summed", "copied", "valued", "stored", "made", "placed")
        (stacks, tabled, ctab, dtab, turned, biased_, scored, full, negated, powered, blocks, weighed, summed, copied,
         valued, stored, made, placed) = (ph.sem(x) for x in names)
        keysF, keysL, posF, posL = 0, EXT, 2 * EXT, 2 * EXT + P
        CH = P // G

        with nc.Block() as block:
            @block.sync
            def _(sp):
                heads = lambda t: t.rearrange("(b h) r s -> h r b s", b=B)
                with sp.Fori(0, H) as h:
                    sp.wait_ge(scored, NT * B * h)
                    for dst, src in ((q, net.QS[:, 0:rows, :]), (k, net.KS[:, 0:rows, :]), (kl, net.KLS), (kh, net.KHS)):
                        sp.dma_start(dst[:, :, :], heads(src)[bass.ds(h, 1), :, :, :].rearrange("o r b s -> (o r) b s"))\
                            .then_inc(stacks, 16)
                    sp.dma_start(tb[:, :], net.TB[bass.ds(h, 1), :, :].rearrange("o r s -> (o r) s")).then_inc(stacks, 16)

            @block.tensor
            def _(pe):
                with pe.Fori(0, H) as h:
                    pe.wait_ge(stacks, 80 * h + 80)
                    qv = q[:, :, :].rearrange("r b (i s) -> r s b i", i=NT)
                    kv = k[:, :, :].rearrange("r b (i s) -> r s b i", i=NT)
                    pe.wait_ge(copied, 2 * h)
                    for c in range(CH):
                        if c:
                            pe.wait_ge(ctab, 2 * CH * h + 2 * c)
                        for s in range(G):
                            x = G * c + s
                            full_, part = sc[0][:, 32 * s:32 * s + 32], sc[1][:, 24 * s:24 * s + 24]
                            at = 191 - x
                            pe.matmul(full_, tb[:, at:at + P], qv[:, x, :, :], start=True, stop=True)
                            pe.matmul(part[64:128], tb[:, at - 64:at], qv[:, x, :, 1:NT], start=True, stop=True)
                            m = pe.matmul(part[0:64], tb[:, at + P:at + P + 64], qv[:, x, :, 0:NT - 1], start=True, stop=True)
                        m.then_inc(tabled, 1)
                        if c:
                            pe.wait_ge(dtab, 2 * CH * h + 2 * c)
                        for s in range(G):
                            x = G * c + s
                            full_, part = tr[0][:, 32 * s:32 * s + 32], tr[1][:, 24 * s:24 * s + 24]
                            at = keysL + 191 - x
                            pe.matmul(full_, tb[:, at:at + P], kv[:, x, :, :], start=True, stop=True)
                            if x >= REL:
                                m = pe.matmul(part, tb[:, at + P:at + 2 * P], kv[:, x, :, 0:NT - 1], start=True, stop=True)
                            else:
                                m = pe.matmul(part, tb[:, at - P:at], kv[:, x, :, 1:NT], start=True, stop=True)
                        m.then_inc(tabled, 1)
                    pe.wait_ge(ctab, 2 * CH * h + 2 * CH)
                    pe.wait_ge(dtab, 2 * CH * h + 2 * CH)
                    for b in range(B):
                        n = B * h + b
                        pe.wait_ge(biased_, 3 * n)
                        for i in range(NT):
                            pe.transpose(pc[0][:, i * P:(i + 1) * P], c0[:, b, i, :], net.idf[:, :])
                        for i in range(NT - 1):
                            m = pe.transpose(pc[1][:, i * P:(i + 1) * P], c1[:, b, i, :], net.idf[:, :])
                        m.then_inc(turned, 1)
                        for I in range(NT):
                            s = sc[I % 2]
                            pe.wait_ge(full, NT * n + max(I - 1, 0))
                            lo, hi = max(0, I * P - REL), min(S, I * P + P + REL)
                            qi = q[:, b, I * P:(I + 1) * P]
                            if lo:
                                pe.matmul(s[:, 0:lo], qi, kl[:, b, 0:lo], start=True, stop=False)
                                pe.matmul(s[:, 0:lo], tb[:, posF:posF + P], k[:, b, 0:lo], start=False, stop=True)
                            if hi < S:
                                pe.matmul(s[:, hi:S], qi, kh[:, b, hi - (S - FAR):FAR], start=True, stop=False)
                                pe.matmul(s[:, hi:S], tb[:, posL:posL + P], k[:, b, hi:S], start=False, stop=True)
                            pe.matmul(s[:, lo:hi], qi, k[:, b, lo:hi], start=True, stop=True).then_inc(scored, 1)
                        pe.wait_ge(powered, NT * n + NT)
                        pe.wait_ge(valued, h + 1)
                        if b % U == 0:
                            pe.wait_ge(copied, 2 * h + b // U)

                        def turn(J):
                            pe.wait_ge(weighed, NT * n + max(J - 1, 0))
                            for I in range(NT):
                                m = pe.transpose(tr[J % 2][:, I * P:(I + 1) * P], e[:, I, J * P:(J + 1) * P], net.idf[:, :])
                            m.then_inc(blocks, 1)

                        turn(0)
                        turn(1)
                        for J in range(NT):
                            pe.wait_ge(weighed, NT * n + J + 1)
                            m = pe.matmul(po[VW * (b % U):VW * (b % U + 1), :], v1[:, b, J, :], w[:, J % 2, :],
                                          start=J == 0, stop=J == NT - 1)
                            m.then_inc(summed, 1)
                            if J + 2 < NT:
                                turn(J + 2)

            @block.vector
            def _(v):
                v.memset(bf[:, :], 0.0).then_inc(placed, 1)
                v.wait_ge(placed, 1)

                def window(first, n, width):
                    run = bf[:, first:first + n * (S + P)]
                    return run.rearrange("p (n w) -> p n w", n=n)[:, :, 0:width]

                with v.Fori(0, H) as h:
                    for c in range(CH):
                        v.wait_ge(tabled, 2 * CH * h + 2 * c + 1)
                        v.tensor_copy(c0[:, :, :, G * c:G * c + G],
                                      sc[0][:, :].rearrange("p (s b i) -> p b i s", s=G, b=B)).then_inc(ctab, 1)
                        v.tensor_copy(c1[:, :, :, G * c:G * c + G],
                                      sc[1][:, 0:24 * G].rearrange("p (s b i) -> p b i s", s=G, b=B)).then_inc(ctab, 1)
                    v.wait_ge(dtab, 2 * CH * h + 2 * CH)
                    for b in range(B):
                        n = B * h + b
                        v.wait_ge(turned, n + 1)
                        v.wait_ge(full, NT * n)
                        v.tensor_tensor(window(0, NT, P), pc[0][:, :].rearrange("p (i k) -> p i k", i=NT), d0[:, b, :, :],
                                        ALU.add).then_inc(biased_, 1)
                        side = pc[1][:, 0:C2].rearrange("p (i k) -> p i k", i=NT - 1)
                        v.tensor_tensor(window(S + REL, NT - 1, REL), side[:, :, REL:P], d1[:, b, :, REL:P],
                                        ALU.add).then_inc(biased_, 1)
                        v.tensor_tensor(window(P, NT - 1, REL), side[:, :, 0:REL], d1[:, b, :, 0:REL],
                                        ALU.add).then_inc(biased_, 1)
                        v.wait_ge(biased_, 3 * n + 3)
                        v.wait_ge(powered, NT * n)
                        for I in range(NT):
                            v.wait_ge(scored, NT * n + I + 1)
                            waited(net, v)
                            v.tensor_tensor_reduce(ss[:, I, :], sc[I % 2][:, :], bf[:, I * S:(I + 1) * S], 1.0, -3e38,
                                                   ALU.add, ALU.max, mx[:, I:I + 1]).then_inc(full, 1)
                        v.wait_ge(full, NT * n + NT)
                        v.tensor_scalar(nm[:, :], mx[:, :], -scale, None, ALU.mult).then_inc(negated, 1)
                        for J in (0, 2):
                            v.wait_ge(blocks, NT * n + J + 1)
                            v.wait_ge(weighed, NT * n + J)
                            v.wait_ge(summed, NT * n + max(J - 1, 0))
                            v.tensor_copy(w[:, J % 2, :], tr[J % 2][:, :]).then_inc(weighed, 1)

            @block.scalar
            def _(a):
                with a.Fori(0, H) as h:
                    for c in range(CH):
                        a.wait_ge(tabled, 2 * CH * h + 2 * c + 2)
                        a.copy(d0[:, :, :, G * c:G * c + G],
                               tr[0][:, :].rearrange("p (s b i) -> p b i s", s=G, b=B)).then_inc(dtab, 1)
                        a.copy(d1[:, :, :, G * c:G * c + G],
                               tr[1][:, 0:24 * G].rearrange("p (s b i) -> p b i s", s=G, b=B)).then_inc(dtab, 1)
                    for b in range(B):
                        n = B * h + b
                        a.wait_ge(negated, n + 1)
                        a.wait_ge(blocks, NT * n)
                        for I in range(NT):
                            a.activation(e[:, I, :], ss[:, I, :], ACT.Exp, bias=nm[:, I:I + 1], scale=scale).then_inc(powered, 1)
                        for J in (1, 3):
                            a.wait_ge(blocks, NT * n + J + 1)
                            a.wait_ge(weighed, NT * n + J)
                            a.wait_ge(summed, NT * n + max(J - 1, 0))
                            a.copy(w[:, J % 2, :], tr[J % 2][:, :]).then_inc(weighed, 1)
                        if b % U == U - 1:
                            t = 2 * h + b // U
                            a.wait_ge(summed, NT * n + NT)
                            a.wait_ge(stored, 16 * U * t)
                            a.copy(o[:, :], po[:, :]).then_inc(copied, 1)
                            a.wait_ge(copied, t + 1)
                            for u in range(U):
                                bh = (b - U + 1 + u) * H + h
                                a.dma_start(net.CU[bass.ds(bh, 1), :, :], o[VW * u:VW * u + 2 * DH, :]).then_inc(stored, 16)
                a.wait_ge(stored, 16 * B * H)

            @block.gpsimd
            def _(g):
                g.memset(v1[:, :, :, :], 0.0).then_inc(made, 1)
                g.wait_ge(made, 1)
                g.memset(v1[:, :, :, DH:2 * DH], 1.0).then_inc(made, 1)
                g.wait_ge(made, 2)
                heads = net.V[:, :, :, :].rearrange("p (b h) j d -> p h b (j d)", b=B)
                with g.Fori(0, H) as h:
                    waited(net, g, (summed, NT * B * h))
                    for j in range(NT):
                        m = g.tensor_copy(v1[:, :, j, 0:DH],
                                          heads[:, bass.ds(h, 1), :, j * DH:(j + 1) * DH].rearrange("p o b d -> p (o b) d"))
                    m.then_inc(valued, 1)


def expert_affinity(net, tag, attended):
    nc, aps = net.nc, net.aps
    with Phase(net, tag) as ph:
        psT, psY, psG = (ph.ps(n, [P, S]) for n in ("psT", "psY", "psG"))
        at = Attended(ph, psY, *attended)
        nm = Norm(ph, "n", psT)
        wg = ph.sb("wg", [D, E])
        mx, sm = ph.sb("mx", [P, NT]), ph.sb("sm", [P, NT])
        z, ex = ph.sb("z", [P, NT, E]), ph.sb("ex", [P, NT, E])
        weights, logits, shifted, powered, step, done_ = (ph.sem(x) for x in
            ("weights", "logits", "shifted", "powered", "step", "done"))
        with nc.Block() as block:
            @block.sync
            def _(sp):
                at.weights(sp)
                sp.dma_start(wg[:, :], aps["L1f_gateT"]).then_inc(weights, 16)
                with sp.Fori(0, B) as b:
                    at.load(sp, b)

            @block.tensor
            def _(pe):
                pe.wait_ge(weights, 16)
                with pe.Fori(0, B) as b:
                    at.pe(pe, b)
                    nm.pe(pe, b)
                    pe.wait_ge(nm.ready, b + 1)
                    pe.wait_ge(shifted, b)
                    for j in range(NT):
                        m = pe.matmul(psG[:, j * E:(j + 1) * E], nm.xT[:, j * P:(j + 1) * P], wg[:, :], start=True, stop=True)
                    m.then_inc(logits, 1)

            @block.scalar
            def _(a):
                with a.Fori(0, B) as b:
                    nm.act(a, b, free=(logits, b))
                    a.wait_ge(shifted, b + 1)
                    a.wait_ge(done_, b)
                    a.activation(ex[:, :, :], z[:, :, :], ACT.Exp).then_inc(powered, 1)

            @block.vector
            def _(v):
                with v.Fori(0, B) as b:
                    at.dve_divide(v, b)
                    at.dve_add(v, b)
                    nm.dve(v, b)
                    v.wait_ge(logits, b + 1)
                    pg = psG[:, 0:NT * E].rearrange("p (j e) -> p j e", j=NT)
                    v.tensor_reduce(mx[:, :], pg, AX, ALU.max).then_inc(step, 1)
                    v.wait_ge(step, 3 * b + 1)
                    v.tensor_tensor(z[:, :, :], pg, over(mx[:, :], 2, E), ALU.subtract).then_inc(shifted, 1)
                    v.wait_ge(powered, b + 1)
                    v.reduce_sum(sm[:, :], ex[:, :, :], AX).then_inc(step, 1)
                    v.wait_ge(step, 3 * b + 2)
                    v.reciprocal(sm[:, :], sm[:, :]).then_inc(step, 1)
                    v.wait_ge(step, 3 * b + 3)
                    v.tensor_tensor(net.aff[:, :, bass.ds(b * E, E)], ex[:, :, :], over(sm[:, :], 2, E), ALU.mult)\
                        .then_inc(done_, 1)

            @block.gpsimd
            def _(g):
                with g.Fori(0, B) as b:
                    nm.pool(g, b)


def expert_choice(net, tag):
    nc = net.nc
    L = B * E
    with Phase(net, tag) as ph:
        work = ph.sb("work", [L, S])
        best = ph.sb("best", [L, 8])
        taken = ph.sb("taken", [L, S])
        ones = ph.sb("ones", [L, S])
        count = ph.sb("count", [L, S])
        place = ph.sb("place", [L, S])
        psA, psB = ph.ps("psA", [L, S]), ph.ps("psB", [P, NT * L])
        turned, ready, top, replaced, last, placed, back = (ph.sem(x) for x in
            ("turned", "ready", "top", "replaced", "last", "placed", "back"))
        with nc.Block() as block:
            @block.tensor
            def _(pe):
                for j in range(NT):
                    m = pe.transpose(psA[:, j * P:(j + 1) * P], net.aff[:, j, :], net.idf[:, :])
                m.then_inc(turned, 1)
                pe.wait_ge(placed, 1)
                for j in range(NT):
                    m = pe.transpose(psB[:, j * L:(j + 1) * L], place[:, j * P:(j + 1) * P], net.idf[0:L, 0:L])
                m.then_inc(back, 1)

            @block.vector
            def _(v):
                v.memset(ones[:, :], 1.0)
                v.wait_ge(turned, 1)
                v.tensor_copy(work[:, :], psA[:, :]).then_inc(ready, 1)
                v.wait_ge(ready, 1)
                with v.Fori(0, KTOP // 8) as i:
                    waited(net, v, (replaced, i))
                    v.max(best[:, :], work[:, :]).then_inc(top, 1)
                    waited(net, v, (top, i + 1))
                    v.match_replace(work[:, :], best[:, :], work[:, :], -1.0).then_inc(replaced, 1)
                v.wait_ge(replaced, KTOP // 8)
                v.tensor_scalar(taken[:, :], work[:, :], 0.0, None, ALU.is_lt).then_inc(last, 1)
                v.wait_ge(last, 1)
                v.tensor_tensor_scan(count[:, :], ones[:, :], taken[:, :], 0.0, ALU.mult, ALU.add).then_inc(last, 1)
                v.wait_ge(last, 2)
                v.tensor_tensor(count[:, :], count[:, :], taken[:, :], ALU.mult).then_inc(last, 1)
                v.wait_ge(last, 3)
                v.tensor_scalar(place[:, :], count[:, :], -1.0, None, ALU.add).then_inc(placed, 1)
                v.wait_ge(back, 1)
                v.tensor_copy(net.slot[:, :, :], psB[:, :].rearrange("p (j l) -> p j l", j=NT)).then_inc(last, 1)


def expert_ffn(net, tag):
    nc, aps = net.nc, net.aps
    FT = FI // P
    with Phase(net, tag) as ph:
        w_gate, w_up = ph.sb("w_gate", [D, E, FI]), ph.sb("w_up", [D, E, FI])
        w_down = ph.sb("w_down", [P, E, FT, D])
        nm = Norm(ph, "n", None)
        iota = ph.sb("iota", [P, P])
        aff, slot = ph.sb("aff", [P, NT, E]), ph.sb("slot", [P, NT, E])
        pick = ph.sb("pick", [P, 2, NT, P])
        pickT = ph.sb("pickT", [P, S])
        xg = ph.sb("xg", [P, P])
        weight = ph.sb("weight", [P, 1])
        act_ = ph.sb("act", [P, FI])
        hid = ph.sb("hid", [P, FI])
        y = ph.sb("y", [P, D])
        psX, psP, psG, psU, psD, psO = (ph.ps(n, [P, S]) for n in ("psX", "psP", "psG", "psU", "psD", "psO"))
        (weights, made, copied, picked, gathered, turned, got, gotT, inner, silu, hidden, down, scaled, scattered, added) = (
            ph.sem(x) for x in ("weights", "made", "copied", "picked", "gathered", "turned", "got", "gotT", "inner",
                                "silu", "hidden", "down", "scaled", "scattered", "added"))
        nm.used = (turned, E)
        with nc.Block() as block:
            @block.sync
            def _(sp):
                for dst, x in ((w_gate, "L1f_gate"), (w_up, "L1f_up")):
                    sp.dma_start(dst[:, :, :], aps[x]).then_inc(weights, 16)
                sp.dma_start(w_down[:, :, :, :], aps["L1f_down"]).then_inc(weights, 16)

            @block.tensor
            def _(pe):
                pe.wait_ge(weights, 48)

                def gather(b, e):
                    n = E * b + e
                    g = pick[:, e % 2, :, :]
                    pe.wait_ge(picked, n + 1)
                    if e == 0:
                        pe.wait_ge(nm.normed, NT * b + NT)
                    pe.wait_ge(got, 2 * n)
                    for j in range(NT):
                        pe.matmul(psX[:, 0:P], nm.xn[:, j, :], g[:, j, :], start=j == 0, stop=j == NT - 1)
                    for j in range(NT):
                        m = pe.matmul(psX[:, P:P + 1], g[:, j, :], aff[:, j, e:e + 1], start=j == 0, stop=j == NT - 1)
                    m.then_inc(gathered, 1)
                    pe.wait_ge(gotT, n)
                    for j in range(NT):
                        m = pe.transpose(psP[:, j * P:(j + 1) * P], g[:, j, :], net.idf[:, :])
                    m.then_inc(turned, 1)

                def up(b, e):
                    n = E * b + e
                    pe.wait_ge(got, 2 * n + 1)
                    pe.wait_ge(hidden, n)
                    for ps, w in ((psG, w_gate), (psU, w_up)):
                        for i in range(FT):
                            m = pe.matmul(ps[:, i * P:(i + 1) * P], w[:, e, i * P:(i + 1) * P], xg[:, :], start=True, stop=True)
                    m.then_inc(inner, 1)

                def project(b, e):
                    n = E * b + e
                    pe.wait_ge(hidden, n + 1)
                    pe.wait_ge(scaled, n)
                    for i in range(FT):
                        m = pe.matmul(psD[:, 0:D], hid[:, i * P:(i + 1) * P], w_down[:, e, i, :], start=i == 0, stop=i == FT - 1)
                    m.then_inc(down, 1)

                def scatter(b, e):
                    n = E * b + e
                    pe.wait_ge(scaled, n + 1)
                    pe.wait_ge(gotT, n + 1)
                    if e == 0:
                        pe.wait_ge(added, b)
                    for j in range(NT):
                        m = pe.matmul(psO[:, j * P:(j + 1) * P], pickT[:, j * P:(j + 1) * P], y[:, :],
                                      start=e == 0 and j == 0, stop=e == E - 1 and j == NT - 1, skip_group_check=True)
                    m.then_inc(scattered, 1)

                with pe.Fori(0, B) as b:
                    gather(b, 0)
                    up(b, 0)
                    for e in range(E):
                        if e + 1 < E:
                            gather(b, e + 1)
                        project(b, e)
                        if e + 1 < E:
                            up(b, e + 1)
                        scatter(b, e)

            @block.scalar
            def _(a):
                with a.Fori(0, B) as b:
                    for e in range(E):
                        n = E * b + e
                        a.wait_ge(gathered, n + 1)
                        a.wait_ge(inner, n)
                        a.copy(xg[:, :], psX[:, 0:P]).then_inc(got, 1)
                        a.wait_ge(scaled, n)
                        a.copy(weight[:, :], psX[:, P:P + 1]).then_inc(got, 1)
                        a.wait_ge(inner, n + 1)
                        a.wait_ge(hidden, n)
                        a.activation(act_[:, :], psG[:, :], ACT.Silu).then_inc(silu, 1)
                        a.wait_ge(turned, n + 1)
                        a.wait_ge(scattered, n)
                        a.copy(pickT[:, :], psP[:, :]).then_inc(gotT, 1)

            @block.vector
            def _(v):
                with v.Fori(0, B) as b:
                    nm.dve(v, b)
                    for e in range(E):
                        n = E * b + e
                        v.wait_ge(silu, n + 1)
                        v.wait_ge(down, n)
                        v.tensor_tensor(hid[:, :], act_[:, :], psU[:, :], ALU.mult).then_inc(hidden, 1)
                        v.wait_ge(down, n + 1)
                        v.wait_ge(got, 2 * n + 2)
                        v.wait_ge(scattered, n)
                        v.tensor_scalar(y[:, :], psD[:, 0:D], weight[:, 0:1], None, ALU.mult).then_inc(scaled, 1)
                    v.wait_ge(scattered, E * b + E)
                    x = net.X[:, bass.ds(b * NT, NT), :]
                    v.tensor_tensor(x, x, psO[:, :].rearrange("p (j d) -> p j d", j=NT), ALU.add).then_inc(added, 1)
                    v.wait_ge(added, b + 1)

            @block.gpsimd
            def _(g):
                g.iota(iota[:, :], pattern=[[1, P]], base=0, channel_multiplier=0,
                       allow_small_or_imprecise_dtypes=True).then_inc(made, 1)
                g.wait_ge(made, 1)
                with g.Fori(0, B) as b:
                    nm.pool(g, b)
                    waited(net, g, (turned, E * b))
                    g.tensor_copy(aff[:, :, :], net.aff[:, :, bass.ds(b * E, E)]).then_inc(copied, 1)
                    g.tensor_copy(slot[:, :, :], net.slot[:, :, bass.ds(b * E, E)]).then_inc(copied, 1)
                    g.wait_ge(copied, 2 * b + 2)
                    for e in range(E):
                        n = E * b + e
                        waited(net, g, (turned, n - 1 if e else n))
                        for j in range(NT):
                            m = g.tensor_scalar(pick[:, e % 2, j, :], iota[:, :], slot[:, j, e:e + 1], None, ALU.is_equal)
                        m.then_inc(picked, 1)


def dump(net, out, what):
    nc = net.nc
    with Phase(net, "dump") as ph:
        done = ph.sem("done")
        with nc.Block() as block:
            @block.sync
            def _(sp):
                sp.dma_start(out.rearrange("b (j p) d -> p (b j) d", p=P), net.X[:, :, :]).then_inc(done, 16)
                sp.wait_ge(done, 16)


def attention_out(net, tag, args):
    nc = net.nc
    with Phase(net, tag) as ph:
        at = Attended(ph, ph.ps("psY", [P, S]), *args)
        with nc.Block() as block:
            @block.sync
            def _(sp):
                at.weights(sp)
                with sp.Fori(0, B) as b:
                    at.load(sp, b)

            @block.tensor
            def _(pe):
                with pe.Fori(0, B) as b:
                    at.pe(pe, b)

            @block.vector
            def _(v):
                with v.Fori(0, B) as b:
                    at.dve_divide(v, b)
                    at.dve_add(v, b)


STAGES = 99
START = 0


def program(nc, aps, out):
    run = lambda n: START < n <= STAGES
    with ExitStack() as ctx:
        net = Net(nc, aps, ctx)
        setup(net)
        if run(2):
            mla_prep(net)
            heads_t(net, "mh", DH + DR, 80.0, float(1.0 / np.sqrt(np.float32(DH + DR))))
            moe_top2(net, "m1", (aps["L0_attn_a_W_O"],))
        if run(3):
            with net.nc.sbuf_tensor("far_keys", [P, 2], F32) as keep:
                relative_tables(net, keep)
                relative_prep(net, keep)
            heads_relative(net, "rh", float(1.0 / np.sqrt(np.float32(DH * 3))))
            if STAGES == 3:
                attention_out(net, "ro", (aps["L0b_WoT"], aps["L0_attn_b_bo"]))
            else:
                moe_top2(net, "m2", (aps["L0b_WoT"], aps["L0_attn_b_bo"]))
        if run(5):
            linear_prep(net)
            heads_t(net, "lh", DH, None, None)
            expert_affinity(net, "lo", (aps["L1a_WoT"], aps["L1_attn_a_bo"], 1e-6))
            expert_choice(net, "lc")
            expert_ffn(net, "lf")
        if run(7):
            rotary_prep(net)
            heads_max(net, "yh", float(1.0 / np.sqrt(np.float32(DH))))
            expert_affinity(net, "yo", (aps["L1b_WoT"], aps["L1_attn_b_out_b"]))
            expert_choice(net, "yc")
            expert_ffn(net, "yf")
        dump(net, out, "X")


def rotary_mla():
    inv = np.float32(10000.0) ** (-np.arange(0, DR, 2, dtype=np.float32) / np.float32(DR))
    ang = (np.arange(S, dtype=np.float32)[:, None] * inv.astype(np.float32)).astype(np.float64)
    cos, sin = np.cos(ang).T, np.sin(ang).T
    c4 = np.repeat(cos, 2, 0)
    s4 = np.stack([-sin, sin], 1).reshape(DR, S)
    rot = np.zeros((P, S), np.float32)
    rot[:H * DR] = np.tile(c4, (H, 1))
    rot[H * DR:] = np.tile(s4, (H, 1))
    return rot


def rotary_full():
    i = np.arange(D // 2, dtype=np.float32)
    theta = (np.float32(10000.0) ** (np.float32(-2.0) * (i - np.float32(1.0)) / np.float32(D))).astype(np.float32)
    ang = (np.arange(S, dtype=np.float32)[:, None] * theta[None, :]).astype(np.float64)
    cos, sin = np.cos(ang).T, np.sin(ang).T
    return np.stack([np.repeat(cos, 2, 0), np.stack([sin, -sin], 1).reshape(D, S)], 1).astype(np.float32)


def host_layout(inputs):
    a = {k: np.ascontiguousarray(v) for k, v in inputs.items()}
    out = dict(a)
    swap = lambda w: np.ascontiguousarray(w.reshape(w.shape[0], -1, 2)[:, :, ::-1].reshape(w.shape))
    down = np.zeros((D, P), a["L0_attn_a_W_DQ"].dtype)
    down[:, 0:DL] = a["L0_attn_a_W_DQ"]
    down[:, DL:2 * DL] = a["L0_attn_a_W_DKV"]
    down[:, 2 * DL:2 * DL + DR] = a["L0_attn_a_W_KR"]
    down[:, 3 * DL:3 * DL + DR] = swap(a["L0_attn_a_W_KR"])
    out["mla_down"] = down
    out["mla_qr"] = np.concatenate([a["L0_attn_a_W_QR"], swap(a["L0_attn_a_W_QR"])], 1)
    out["mla_rot"] = rotary_mla()
    turned = lambda w: np.ascontiguousarray(w.T)
    for x in "qkvo":
        out[f"L0b_W{x}T"] = turned(a[f"L0_attn_b_W{x}"])
        out[f"L1a_W{x}T"] = turned(a[f"L1_attn_a_W{x}"])
    for x in "kq":
        out[f"L0b_Wp{x}T"] = turned(a[f"L0_attn_b_Wp{x}"])
    each = [turned(a[f"L1_attn_b_w{x}"]) for x in "qkv"]
    out["L1b_w"] = np.ascontiguousarray(np.stack([y for w in each for y in (w, swap(w))], 1))
    out["L1b_in"] = np.ascontiguousarray(np.stack([turned(w) for w in np.split(a["L1_attn_b_in_proj_w"], 3, 0)], 1))
    out["L1b_rot"] = rotary_full()
    out["L1b_WoT"] = turned(a["L1_attn_b_out_w"])
    out["relT"] = turned(a["L0_attn_b_rel_emb"])
    out["relT_reversed"] = turned(a["L0_attn_b_rel_emb"][::-1])
    out["WeT"] = np.ascontiguousarray(a["L0_ffn_We"].transpose(2, 0, 1).reshape(D, E * D))
    out["L1f_gateT"] = turned(a["L1_ffn_gate_w"])
    for x in ("gate", "up"):
        out[f"L1f_{x}"] = np.ascontiguousarray(a[f"L1_ffn_w_{x}"].transpose(2, 0, 1))
    down = a["L1_ffn_w_down"].reshape(E, D, FI // P, P)
    out["L1f_down"] = np.ascontiguousarray(down.transpose(3, 0, 2, 1))
    return out



def kernel(**inputs):
    import concourse.bacc as _bacc
    from concourse.bass_utils import run_bass_kernel_spmd as _run

    nc = _bacc.Bacc("TRN2", target_bir_lowering=False, num_devices=1)
    arrays, aps = {}, {}
    for name, a in host_layout(inputs).items():
        arrays[f"in_{name}"] = a
        aps[name] = nc.dram_tensor(f"in_{name}", a.shape, mybir.dt.from_np(a.dtype), kind="ExternalInput").ap()
    out = nc.dram_tensor("out", (B, S, D), F32, kind="ExternalOutput").ap()
    program(nc, aps, out)
    r = _run(nc, [arrays], core_ids=[0])
    return r.results[0]["out"]
```

```python
from contextlib import ExitStack

import numpy as np

import concourse.bass as bass
from concourse import mybir

F32 = mybir.dt.float32
BF16 = mybir.dt.bfloat16
ALU = mybir.AluOpType
ACT = mybir.ActivationFunctionType
AX = mybir.AxisListType.X

P = 128
B, S, D = 8, 512, 128
NT = S // P
H, DH = 16, 8
DR, DL = 4, 32
E = 8
FI = 512
KTOP = S // E * 2
REL = 64
LPART = (0, 0, 0, 1, 1, 2)
RPART = (0, 1, 2, 0, 1, 0)
NC6 = len(LPART)
RUNS = ((0, 3), (3, 5), (5, 6))
BASE = 4
LN_EPS = 1e-5
FAR = S - 3 * REL
EXT = 3 * P
TW = 2 * EXT + 2 * P
VW = 32


class Net:

    def __init__(self, nc, aps, ctx):
        self.nc, self.aps, self.ctx = nc, aps, ctx
        sb = lambda name, shape, dt=F32: ctx.enter_context(nc.sbuf_tensor(name, shape, dt))
        self.X = sb("X", [P, B * NT, D])
        self.V = sb("V", [P, B * H, NT, DH])
        self.idf = sb("idf", [P, P])
        self.idb = sb("idb", [P, P], BF16)
        self.negb = sb("negb", [P, P], BF16)
        self.half = sb("half", [P, NT])
        self.ones = sb("ones", [1, S])
        self.constants = ctx.enter_context(nc.semaphore("constants"))
        self.carrier = ctx.enter_context(nc.semaphore("carrier"))
        scratch = lambda name, shape, dt: nc.dram_tensor(name, shape, dt, kind="Internal").ap()
        self.QS = scratch("QS", (B * H, NC6 * DH, S), BF16)
        self.KS = scratch("KS", (B * H, NC6 * DH, S), BF16)
        self.QM = scratch("QM", (B * H, NC6 * (DH + DR), S), BF16)
        self.KM = scratch("KM", (B * H, NC6 * (DH + DR), S), BF16)
        self.KLS = scratch("KLS", (B * H, NC6 * DH, FAR), BF16)
        self.KHS = scratch("KHS", (B * H, NC6 * DH, FAR), BF16)
        self.TB = scratch("TB", (H, NC6 * DH, TW), BF16)
        self.aff = sb("aff", [P, NT, B * E])
        self.slot = sb("slot", [P, NT, B * E])
        self.CU = scratch("CU", (B * H, DH + 1, S), F32)
        self.RD = scratch("RD", (B * H, S), F32)


class Phase:

    def __init__(self, net, tag):
        self.net, self.nc, self.tag, self.ctx, self.sems = net, net.nc, tag, ExitStack(), []

    def __enter__(self):
        return self

    def __exit__(self, *a):
        if a[0] is None:
            for s in self.sems:
                self.nc.gpsimd.sem_clear(s)
            self.nc.all_engine_barrier()
        self.ctx.close()

    def start(self):
        engines = (self.nc.gpsimd, self.nc.vector, self.nc.scalar, self.nc.tensor, self.nc.sync)
        for i, s in enumerate(self.sems):
            engines[i % len(engines)].sem_inc(s, BASE)
        self.nc.all_engine_barrier()
        return self.nc.Block()

    def sb(self, name, shape, dt=F32):
        return self.ctx.enter_context(self.nc.sbuf_tensor(f"{self.tag}_{name}", shape, dt))

    def ps(self, name, shape, dt=F32):
        return self.ctx.enter_context(self.nc.psum_tensor(f"{self.tag}_{name}", shape, dt))

    def sem(self, name):
        s = self.ctx.enter_context(self.nc.semaphore(f"{self.tag}_{name}"))
        self.sems.append(s)
        return s


def waited(net, eng, *waits):
    for sem, value in waits:
        eng.wait_ge(sem, BASE + value)
    eng.sem_inc(net.carrier, 1)


def over(ap, dim, n):
    shape = list(ap.shape)
    shape.insert(dim, n)
    return ap.unsqueeze(dim).broadcast_to(shape)


def setup(net):
    nc = net.nc
    with Phase(net, "setup") as ph:
        loaded, made = ph.sem("loaded"), ph.sem("made")
        with ph.start() as block:
            @block.sync
            def _(sp):
                sp.dma_start(net.X[:, :, :], net.aps["L0_attn_a_x"].rearrange("b (j p) d -> p (b j) d", p=P)).then_inc(loaded, 16)
                sp.wait_ge(loaded, BASE + 16)

            @block.vector
            def _(v):
                v.memset(net.half[:, :], -0.5)
                v.memset(net.ones[:, :], 1.0)

            @block.gpsimd
            def _(g):
                g.memset(net.idf[:, :], 0.0)
                g.memset(net.negb[:, :], 0.0).then_inc(made, 1)
                g.wait_ge(made, BASE + 1)
                g.affine_select(out=net.idf[:, :], in_=net.idf[:, :], compare_op=ALU.not_equal, fill=1.0, base=0,
                                pattern=[[-1, P]], channel_multiplier=1).then_inc(made, 1)
                g.affine_select(out=net.negb[:, :], in_=net.negb[:, :], compare_op=ALU.is_ge, fill=-1e30, base=0,
                                pattern=[[-1, P]], channel_multiplier=1).then_inc(made, 1)
                g.wait_ge(made, BASE + 3)
                g.tensor_copy(net.idb[:, :], net.idf[:, :]).then_inc(net.constants, 1)


class Norm:

    def __init__(self, ph, tag, psT, used=None):
        self.net, self.psT = ph.net, psT
        self.xn = ph.sb(tag + "xn", [P, NT, D])
        self.xT = ph.sb(tag + "xT", [P, S])
        self.st = ph.sb(tag + "st", [P, NT, 6])
        self.mv = ph.sb(tag + "mv", [P, NT, 2])
        self.ve = ph.sb(tag + "ve", [P, NT])
        self.rs = ph.sb(tag + "rs", [P, NT])
        s = lambda n: ph.sem(tag + n)
        self.stats_, self.moments, self.shifted, self.inverse = s("stats"), s("moments"), s("shifted"), s("inverse")
        self.normed, self.turned, self.ready = s("normed"), s("turned"), s("ready")
        self.used = used or (self.turned, 1)

    def tile(self, b, j):
        return self.net.X[:, bass.ds(b * NT + j, 1), :].rearrange("p o d -> p (o d)")

    def stats(self, v, b):
        waited(self.net, v, (self.inverse, b))
        for j in range(NT):
            v.bn_stats(self.st[:, j, :], self.tile(b, j)).then_inc(self.stats_, 1)
        waited(self.net, v, (self.stats_, NT * b + NT))
        for j in range(NT):
            v.bn_aggr(self.mv[:, j, :], self.st[:, j, :]).then_inc(self.moments, 1)

    def power(self, g, b):
        waited(self.net, g, (self.moments, NT * b + NT))
        g.tensor_scalar(self.ve[:, :], self.mv[:, :, 1], LN_EPS, None, ALU.add).then_inc(self.shifted, 1)
        g.wait_ge(self.shifted, BASE + b + 1)
        g.wait_ge(self.normed, BASE + NT * b)
        g.tensor_tensor(self.rs[:, :], self.ve[:, :], self.net.half[:, :], ALU.pow).then_inc(self.inverse, 1)

    def norm(self, v, b):
        v.wait_ge(self.inverse, BASE + b + 1)
        v.wait_ge(self.used[0], BASE + self.used[1] * b)
        for j in range(NT):
            v.tensor_scalar(self.xn[:, j, :], self.tile(b, j), self.mv[:, j, 0:1], self.rs[:, j:j + 1],
                            ALU.subtract, ALU.mult).then_inc(self.normed, 1)

    def turn(self, pe, b):
        pe.wait_ge(self.normed, BASE + NT * b + NT)
        pe.wait_ge(self.ready, BASE + b)
        for j in range(NT):
            t = pe.transpose(self.psT[:, j * P:(j + 1) * P], self.xn[:, j, :], self.net.idf[:, :])
        t.then_inc(self.turned, 1)

    def keep(self, a, b, free):
        a.wait_ge(self.turned, BASE + b + 1)
        a.wait_ge(free[0], BASE + free[1])
        a.copy(self.xT[:, :], self.psT[:, :]).then_inc(self.ready, 1)


def batches(eng, before, body):
    before()
    with eng.Fori(0, B - 1) as b:
        body(b, True)
    body(B - 1, False)


class Split:

    def __init__(self, ph, tag, n, src, cols=S, bias=None, dmas=len(RUNS)):
        self.net, self.n, self.src, self.bias, self.dmas = ph.net, n, src, bias, dmas
        self.part = ph.sb(tag + "part", [n, 3, cols], BF16)
        self.r1 = ph.sb(tag + "r1", [n, cols])
        self.first, self.rest, self.second, self.third, self.kept = (
            ph.sem(tag + x) for x in ("first", "rest", "second", "third", "kept"))

    def act(self, a, b, have):
        a.wait_ge(have[0], BASE + have[1])
        a.wait_ge(self.kept, BASE + 16 * self.dmas * b)
        if self.bias is None:
            a.copy(self.part[:, 0, :], self.src).then_inc(self.first, 1)
        else:
            a.activation(self.part[:, 0, :], self.src, ACT.Identity, bias=self.bias).then_inc(self.first, 1)

    def dve(self, v, b):
        v.wait_ge(self.first, BASE + b + 1)
        v.wait_ge(self.third, BASE + b)
        if self.bias is None:
            v.tensor_tensor(self.r1[:, :], self.src, self.part[:, 0, :], ALU.subtract).then_inc(self.rest, 1)
        else:
            v.scalar_tensor_tensor(self.r1[:, :], self.src, self.bias, self.part[:, 0, :], ALU.add, ALU.subtract)\
                .then_inc(self.rest, 1)

    def pool(self, g, b):
        waited(self.net, g, (self.rest, b + 1))
        g.tensor_copy(self.part[:, 1, :], self.r1[:, :]).then_inc(self.second, 1)
        g.wait_ge(self.second, BASE + b + 1)
        g.tensor_tensor(self.part[:, 2, :], self.r1[:, :], self.part[:, 1, :], ALU.subtract).then_inc(self.third, 1)

    def store(self, sp, b, dst, left, at=0, shared=False):
        sp.wait_ge(self.third, BASE + b + 1)
        per = self.n if shared else self.n // H
        copies = dst[bass.ds(b * H, H), :, :].rearrange("h (w c) s -> h w c s", c=NC6)[:, at:at + per, :, :]
        for i, (lo, hi) in enumerate(RUNS):
            if left and self.dmas == len(RUNS):
                src = over(self.part[:, i, :], 1, hi - lo)
                sp.dma_start(copies[:, :, lo:hi, :].rearrange("h r c s -> (h r) c s"), src).then_inc(self.kept, 16)
            elif left:
                for c in range(lo, hi):
                    sp.dma_start(copies[:, :, c, :], self.part[:, i, :]).then_inc(self.kept, 16)
            else:
                rows, src = copies[:, :, lo:hi, :].rearrange("h r c s -> h r (c s)"), self.part[:, 0:hi - lo, :].rearrange("p c s -> p (c s)")
                if shared:
                    rows, src = rows.rearrange("h r x -> r h x"), over(src, 1, H)
                sp.dma_start(rows, src).then_inc(self.kept, 16)

    def end(self, sp):
        sp.wait_ge(self.kept, BASE + 16 * self.dmas * B)


def mla_prep(net):
    nc, aps = net.nc, net.aps
    WD = DH + DR
    with Phase(net, "ma") as ph:
        w_down = ph.sb("w_down", [P, P])
        w_q = ph.sb("w_q", [DL, H * DH])
        w_qr = ph.sb("w_qr", [DL, 2 * H * DR])
        w_kv = ph.sb("w_kv", [2 * DL, 2 * H * DH])
        rot = ph.sb("rot", [P, S])
        lat = ph.sb("lat", [P, S])
        a1 = ph.sb("a1", [H * DR, S])
        a2 = ph.sb("a2", [H * DR, S])
        b1 = ph.sb("b1", [DR, S])
        b2 = ph.sb("b2", [DR, S])
        qr = ph.sb("qr", [H * DR, S])
        kr = ph.sb("kr", [DR, S])
        psT, psD, psQ, psR, psK, psV = (ph.ps(n, [P, S]) for n in ("psT", "psD", "psQ", "psR", "psK", "psV"))
        nm = Norm(ph, "n", psT)
        sq = Split(ph, "q", P, psQ[:, :], dmas=NC6)
        sk = Split(ph, "k", P, psK[:, :])
        sqr = Split(ph, "qr", H * DR, qr[:, :], dmas=NC6)
        skr = Split(ph, "kr", DR, kr[:, :])
        weights = ph.sem("weights")
        down, latent, up, rq, rqs, rk, rks, vals = (ph.sem(x) for x in
            ("down", "latent", "up", "rq", "rqs", "rk", "rks", "vals"))
        with ph.start() as block:
            @block.sync
            def _(sp):
                sp.dma_start(w_down[:, :], aps["mla_down"]).then_inc(weights, 16)
                sp.dma_start(w_q[:, :], aps["L0_attn_a_W_UQ"]).then_inc(weights, 16)
                sp.dma_start(w_qr[:, :], aps["mla_qr"]).then_inc(weights, 16)
                sp.dma_start(w_kv[DL:2 * DL, 0:H * DH], aps["L0_attn_a_W_UK"]).then_inc(weights, 16)
                sp.dma_start(w_kv[DL:2 * DL, H * DH:], aps["L0_attn_a_W_UV"]).then_inc(weights, 16)
                sp.dma_start(rot[:, :], aps["mla_rot"]).then_inc(weights, 16)
                with sp.Fori(0, B) as b:
                    sq.store(sp, b, net.QM, True)
                    sk.store(sp, b, net.KM, False)
                    skr.store(sp, b, net.KM, False, DH, shared=True)
                    sqr.store(sp, b, net.QM, True, DH)
                for s in (sq, sk, sqr, skr):
                    s.end(sp)

            @block.tensor
            def _(pe):
                pe.wait_ge(weights, BASE + 16 * 6)

                def body(b, more):
                    pe.wait_ge(nm.ready, BASE + b + 1)
                    pe.wait_ge(latent, BASE + b)
                    pe.wait_ge(rk, BASE + 2 * b)
                    pe.matmul(psD[:, :], w_down[:, :], nm.xT[:, :], start=True, stop=True).then_inc(down, 1)
                    if more:
                        nm.turn(pe, b + 1)
                    pe.wait_ge(latent, BASE + b + 1)
                    pe.wait_ge(rq, BASE + 2 * b)
                    pe.matmul(psR[:, :], w_qr[:, :], lat[0:DL, :], start=True, stop=True).then_inc(up, 1)
                    pe.wait_ge(sq.rest, BASE + b)
                    pe.matmul(psQ[:, :], w_q[:, :], lat[0:DL, :], start=True, stop=True).then_inc(up, 1)
                    pe.wait_ge(sk.rest, BASE + b)
                    pe.matmul(psK[:, :], w_kv[DL:2 * DL, 0:P], lat[DL:2 * DL, :], start=True, stop=True).then_inc(up, 1)
                    pe.wait_ge(vals, BASE + b)
                    for j in range(NT):
                        m = pe.matmul(psV[:, j * P:(j + 1) * P], lat[DL:2 * DL, j * P:(j + 1) * P],
                                      w_kv[DL:2 * DL, P:], start=True, stop=True)
                    m.then_inc(up, 1)

                batches(pe, lambda: nm.turn(pe, 0), body)

            @block.scalar
            def _(a):
                def body(b, more):
                    a.wait_ge(down, BASE + b + 1)
                    a.wait_ge(up, BASE + 4 * b)
                    a.copy(lat[0:2 * DL, :], psD[0:2 * DL, :]).then_inc(latent, 1)
                    skr.act(a, b, (rks, b + 1))
                    if more:
                        nm.keep(a, b + 1, (down, b + 1))
                    sq.act(a, b, (up, 4 * b + 2))
                    sk.act(a, b, (up, 4 * b + 3))
                    sqr.act(a, b, (rqs, b + 1))
                    a.wait_ge(up, BASE + 4 * b + 4)
                    values_out(net, a, psV, b).then_inc(vals, 1)

                batches(a, lambda: nm.keep(a, 0, (down, 0)), body)

            @block.vector
            def _(v):
                v.wait_ge(weights, BASE + 16 * 6)

                def before():
                    nm.stats(v, 0)
                    nm.norm(v, 0)

                def body(b, more):
                    if more:
                        nm.stats(v, b + 1)
                    v.wait_ge(down, BASE + b + 1)
                    v.wait_ge(rks, BASE + b)
                    v.tensor_tensor(b1[:, :], psD[2 * DL:2 * DL + DR, :], rot[0:DR, :], ALU.mult).then_inc(rk, 1)
                    v.tensor_tensor(b2[:, :], psD[3 * DL:3 * DL + DR, :], rot[H * DR:H * DR + DR, :], ALU.mult).then_inc(rk, 1)
                    v.wait_ge(rk, BASE + 2 * b + 2)
                    v.wait_ge(skr.rest, BASE + b)
                    v.tensor_tensor(kr[:, :], b1[:, :], b2[:, :], ALU.add).then_inc(rks, 1)
                    skr.dve(v, b)
                    if more:
                        nm.norm(v, b + 1)
                    v.wait_ge(up, BASE + 4 * b + 1)
                    v.wait_ge(rqs, BASE + b)
                    v.tensor_tensor(a1[:, :], psR[0:H * DR, :], rot[0:H * DR, :], ALU.mult).then_inc(rq, 1)
                    v.tensor_tensor(a2[:, :], psR[H * DR:, :], rot[H * DR:, :], ALU.mult).then_inc(rq, 1)
                    v.wait_ge(rq, BASE + 2 * b + 2)
                    v.wait_ge(sqr.rest, BASE + b)
                    v.tensor_tensor(qr[:, :], a1[:, :], a2[:, :], ALU.add).then_inc(rqs, 1)
                    sq.dve(v, b)
                    sk.dve(v, b)
                    sqr.dve(v, b)

                batches(v, before, body)

            @block.gpsimd
            def _(g):
                def body(b, more):
                    if more:
                        nm.power(g, b + 1)
                    for s in (skr, sq, sk, sqr):
                        s.pool(g, b)

                batches(g, lambda: nm.power(g, 0), body)


U = 4
UT = 8
R = 4
AHEAD = 3


DIAG = (0, 512, 1024, 896)
CAUSAL = 1280
QDIAG = (896, 1024, 512, 0)


class HeadLoads:

    def __init__(self, ph, rows, queries, keys):
        self.net, self.rows, self.queries, self.keys = ph.net, rows, queries, keys
        self.q = ph.sb("q", [rows, R, S], BF16)
        self.k = ph.sb("k", [rows, R, S], BF16)
        self.v1 = ph.sb("v1", [P, R, NT, VW])
        self.o = ph.sb("o", [P, UT // R, S])
        self.po = [ph.ps(f"po{i}", [P, S]) for i in range(UT // R)]
        self.loaded = [ph.sem(f"loaded{r}") for r in range(R)]
        self.stored = [ph.sem(f"stored{i}") for i in range(UT // R)]
        self.made, self.valued, self.copied = ph.sem("made"), ph.sem("valued"), ph.sem("copied")

    def sync(self, sp, scored):
        turns = B * H // UT

        def store(i, x):
            sp.wait_ge(self.copied, BASE + UT // R * i + x + 1)
            for r in range(R):
                sp.dma_start(self.net.CU[bass.ds(UT * i + R * x + r, 1), :, :], self.o[VW * r:VW * r + DH + 1, x, :])\
                    .then_inc(self.stored[x], 16)

        def turn(i, before):
            for u in range(UT):
                n, r = UT * i + u, u % R
                if before is not None or u >= R:
                    sp.wait_ge(scored, BASE + n - R + 1)
                sp.dma_start(self.q[:, r, :], self.queries[bass.ds(n, 1), :, :]).then_inc(self.loaded[r], 16)
                sp.dma_start(self.k[:, r, :], self.keys[bass.ds(n, 1), :, :]).then_inc(self.loaded[r], 16)
                if r == R - 1 and before is not None:
                    store(before, u // R)

        turn(0, None)
        with sp.Fori(0, turns - 1) as i:
            turn(i + 1, i)
        for x in range(UT // R):
            store(turns - 1, x)
        for s in self.stored:
            sp.wait_ge(s, BASE + 16 * R * turns)

    def wait_loaded(self, pe, i, u):
        pe.wait_ge(self.loaded[u % R], BASE + 32 * (UT // R * i + u // R + 1))

    def pool_start(self, g):
        g.memset(self.v1[:, :, :, :], 0.0).then_inc(self.made, 1)
        g.wait_ge(self.made, BASE + 1)
        g.memset(self.v1[:, :, :, DH:2 * DH], 1.0).then_inc(self.made, 1)
        g.wait_ge(self.made, BASE + 2)

    def pool_values(self, g, n, u, summed):
        waited(self.net, g, (summed, n - R + 1))
        g.tensor_copy(self.v1[:, u % R, :, 0:DH], self.net.V[:, bass.ds(n, 1), :, :].rearrange("p o j d -> p (o j) d"))\
            .then_inc(self.valued, 1)

    def context(self, pe, i, u, n, w, ready, summed):
        pe.wait_ge(ready, BASE + n + 1)
        pe.wait_ge(self.valued, BASE + n + 1)
        if u % R == 0:
            pe.wait_ge(self.copied, BASE + UT // R * i + u // R - 1)
        at = VW * (u % R)
        for J in range(NT):
            m = pe.matmul(self.po[u // R][at:at + VW, J * P:], self.v1[:, u % R, J, :],
                          w[:, DIAG[J]:DIAG[J] + S - J * P], start=J == 0, stop=J == NT - 1)
        m.then_inc(summed, 1)

    def act_copy(self, a, i, x, summed):
        a.wait_ge(summed, BASE + UT * i + R * (x + 1))
        a.wait_ge(self.stored[x], BASE + 16 * R * i)
        a.copy(self.o[:, x, :], self.po[x][:, :]).then_inc(self.copied, 1)

    def act(self, a, item, summed):
        turns = B * H // UT

        def turn(i, before):
            for u in range(UT):
                item(u, UT * i + u)
                if u % R == 1 and (u > R or before is not None):
                    self.act_copy(a, i if u > R else before, 0 if u > R else UT // R - 1, summed)

        turn(0, None)
        with a.Fori(0, turns - 1) as i:
            turn(i + 1, i)
        self.act_copy(a, turns - 1, UT // R - 1, summed)


def heads_t(net, tag, width, queries, keys, clip, scale):
    nc = net.nc
    N = B * H
    with Phase(net, tag) as ph:
        hl = HeadLoads(ph, NC6 * width, queries, keys)
        c = ph.sb("c", [P, R, CAUSAL])
        w = ph.sb("w", [P, R, CAUSAL])
        sc = [ph.ps(f"sc{i}", [P, 3 * S]) for i in range(2)]
        scored, clipped, weighed, masked, summed = (ph.sem(x) for x in ("scored", "clipped", "weighed", "masked", "summed"))
        read = weighed if clip is None else clipped
        with ph.start() as block:
            @block.sync
            def _(sp):
                hl.sync(sp, scored)

            def scores(pe, i, u, n):
                hl.wait_loaded(pe, i, u)
                pe.wait_ge(read, BASE + n - 1)
                for J in range(NT):
                    m = pe.matmul(sc[u % 2][:, DIAG[J]:DIAG[J] + S - J * P], hl.k[:, u % R, J * P:(J + 1) * P],
                                  hl.q[:, u % R, J * P:], start=True, stop=True)
                m.then_inc(scored, 1)

            @block.tensor
            def _(pe):
                def step(i, u, last):
                    t = u + AHEAD
                    if not last or t < UT:
                        scores(pe, i + t // UT, t % UT, UT * i + t)
                    hl.context(pe, i, u, UT * i + u, w[:, u % R, :], masked, summed)

                for u in range(AHEAD):
                    scores(pe, 0, u, u)
                with pe.Fori(0, N // UT - 1) as i:
                    for u in range(UT):
                        step(i, u, False)
                for u in range(UT):
                    step(N // UT - 1, u, True)

            @block.vector
            def _(v):
                if clip is not None:
                    with v.Fori(0, N // UT) as i:
                        for u in range(UT):
                            n = UT * i + u
                            v.wait_ge(scored, BASE + n + 1)
                            v.wait_ge(weighed, BASE + n - R + 1)
                            v.tensor_scalar(c[:, u % R, :], sc[u % 2][:, 0:CAUSAL], clip, -clip, ALU.min, ALU.max)\
                                .then_inc(clipped, 1)

            @block.scalar
            def _(a):
                def item(u, n):
                    a.wait_ge(summed, BASE + n - R + 1)
                    if clip is not None:
                        a.wait_ge(clipped, BASE + n + 1)
                        a.activation(w[:, u % R, :], c[:, u % R, :], ACT.Exp, scale=scale).then_inc(weighed, 1)
                    else:
                        a.wait_ge(scored, BASE + n + 1)
                        a.copy(w[:, u % R, :], sc[u % 2][:, 0:CAUSAL]).then_inc(weighed, 1)

                hl.act(a, item, summed)

            @block.gpsimd
            def _(g):
                hl.pool_start(g)
                with g.Fori(0, N // UT) as i:
                    for u in range(UT):
                        n = UT * i + u
                        hl.pool_values(g, n, u, summed)
                        waited(net, g, (weighed, n + 1))
                        for J in range(NT):
                            x = w[:, u % R, DIAG[J]:DIAG[J] + P]
                            m = g.affine_select(out=x, in_=x, compare_op=ALU.is_ge, fill=0.0, base=0,
                                                pattern=[[1, P]], channel_multiplier=-1)
                        m.then_inc(masked, 1)


class Attended:

    def __init__(self, ph, psT, psY, psG, wo, bo=None, floor=None, wg=None, hold=None):
        self.net, self.psY, self.psG, self.floor, self.hold = ph.net, psY, psG, floor, hold
        self.drams = [wo, wg] + ([bo.unsqueeze(0).broadcast_to([P, D])] if bo is not None else [])
        self.wo, self.wg, self.bo = ph.sb("wo", [P, D]), ph.sb("wg", [D, E]), ph.sb("bo", [P, D])
        self.den = ph.sb("den", [P, S])
        self.num = ph.sb("num", [P, S])
        self.inv = ph.sb("inv", [P, S])
        self.ctx = ph.sb("ctxT", [P, S])
        self.lg = ph.sb("lg", [P, B * NT, E])
        self.nm = Norm(ph, "n", psT)
        (self.w, self.dens, self.floored, self.inverted, self.kept, self.loaded, self.divided, self.out, self.added,
         self.logits, self.taken, self.held) = (ph.sem("at_" + x) for x in
            ("w", "dens", "floored", "inverted", "kept", "loaded", "divided", "out", "added", "logits", "taken", "held"))

    def sync(self, sp):
        net = self.net
        sp.dma_start(self.den[:, :], net.CU[:, DH, :]).then_inc(self.dens, 16)
        for dst, src in zip((self.wo, self.wg, self.bo), self.drams):
            sp.dma_start(dst[:, :], src).then_inc(self.w, 16)

    def sync_batches(self, sp):
        net = self.net
        sp.wait_ge(self.inverted, BASE + 1)
        sp.dma_start(net.RD, self.den[:, :]).then_inc(self.kept, 16)
        sp.wait_ge(self.kept, BASE + 16)
        with sp.Fori(0, B) as b:
            sp.wait_ge(self.divided, BASE + b)
            sp.dma_start(self.num[:, :], net.CU[bass.ds(b * H, H), 0:DH, :]).then_inc(self.loaded, 16)
            inv = over(net.RD[bass.ds(b * H, H), :], 1, DH)
            sp.dma_start(self.inv[:, :], inv).then_inc(self.loaded, 16)

    def pe(self, pe):
        nm = self.nm
        pe.wait_ge(self.w, BASE + 16 * len(self.drams))

        def output(b):
            pe.wait_ge(self.divided, BASE + b + 1)
            pe.wait_ge(self.added, BASE + b)
            for j in range(NT):
                m = pe.matmul(self.psY[:, j * P:(j + 1) * P], self.ctx[:, j * P:(j + 1) * P], self.wo[:, :], start=True, stop=True)
            m.then_inc(self.out, 1)

        def body(b, more):
            if more:
                output(b + 2)
            nm.turn(pe, b)
            pe.wait_ge(nm.ready, BASE + b + 1)
            pe.wait_ge(self.taken, BASE + b)
            for j in range(NT):
                m = pe.matmul(self.psG[:, j * E:(j + 1) * E], nm.xT[:, j * P:(j + 1) * P], self.wg[:, :], start=True, stop=True)
            m.then_inc(self.logits, 1)

        output(0)
        output(1)
        with pe.Fori(0, B - 2) as b:
            body(b, True)
        body(B - 2, False)
        body(B - 1, False)

    def act(self, a):
        nm = self.nm
        with a.Fori(0, B) as b:
            if self.hold is not None:
                a.wait_ge(self.held, BASE + b)
            nm.keep(a, b, (self.logits, b))
            if self.hold is not None:
                a.wait_ge(nm.ready, BASE + b + 1)
                a.copy(self.hold[:, bass.ds(b, 1), :].rearrange("p o s -> p (o s)"), nm.xT[:, :]).then_inc(self.held, 1)
            a.wait_ge(self.logits, BASE + b + 1)
            a.copy(self.lg[:, bass.ds(b * NT, NT), :].rearrange("p j e -> p (j e)"), self.psG[:, 0:NT * E]).then_inc(self.taken, 1)

    def dve(self, v):
        nm = self.nm
        v.wait_ge(self.dens, BASE + 16)
        if self.floor is not None:
            v.tensor_scalar(self.den[:, :], self.den[:, :], self.floor, None, ALU.max).then_inc(self.floored, 1)
            v.wait_ge(self.floored, BASE + 1)
        v.reciprocal(self.den[:, :], self.den[:, :]).then_inc(self.inverted, 1)
        if len(self.drams) == 3:
            v.wait_ge(self.w, BASE + 48)
            v.tensor_tensor(self.net.X[:, :, :], self.net.X[:, :, :], over(self.bo[:, :], 1, B * NT), ALU.add).then_inc(self.inverted, 1)
            v.wait_ge(self.inverted, BASE + 2)

        def add(b):
            x = self.net.X[:, bass.ds(b * NT, NT), :]
            v.wait_ge(self.out, BASE + b + 1)
            v.tensor_tensor(x, x, self.psY[:, :].rearrange("p (j d) -> p j d", j=NT), ALU.add).then_inc(self.added, 1)

        def stats(b):
            v.wait_ge(self.added, BASE + b + 1)
            nm.stats(v, b)

        def before():
            add(0)
            stats(0)

        def body(b, more):
            if more:
                add(b + 1)
            nm.norm(v, b)
            if more:
                stats(b + 1)

        batches(v, before, body)

    def pool(self, g):
        def divide(b):
            g.wait_ge(self.loaded, BASE + 32 * b + 32)
            g.wait_ge(self.out, BASE + b)
            g.tensor_tensor(self.ctx[:, :], self.num[:, :], self.inv[:, :], ALU.mult).then_inc(self.divided, 1)

        def body(b, more):
            if more:
                divide(b + 1)
            self.nm.power(g, b)

        batches(g, lambda: divide(0), body)


def softmax(v, at, step, count, mx, sm, ex, shifted, powered, bias=None):
    T = B * NT

    def then(ins):
        count[0] += 1
        ins.then_inc(step, 1)
        v.wait_ge(step, BASE + count[0])

    lg = at.lg[:, :, :]
    v.wait_ge(at.taken, BASE + B)
    if bias is not None:
        then(v.tensor_tensor(lg, lg, over(bias, 1, T), ALU.add))
    then(v.tensor_reduce(mx[:, :], lg, AX, ALU.max))
    v.tensor_tensor(lg, lg, over(mx[:, :], 2, E), ALU.subtract).then_inc(shifted, 1)
    v.wait_ge(powered, BASE + 1)
    then(v.reduce_sum(sm[:, :], ex[:, :, :], AX))
    then(v.reciprocal(sm[:, :], sm[:, :]))
    return then


def moe_top2(net, tag, attended):
    nc, aps = net.nc, net.aps
    T = B * NT
    with Phase(net, tag) as ph:
        psE = [[ph.ps(f"psE{r}{x}", [P, S]) for x in range(2)] for r in range(4)]
        xall = ph.sb("xall", [P, B, S])
        at = Attended(ph, psE[0][0], psE[0][1], psE[1][0], *attended, wg=aps["L0_ffn_Wg"], hold=xall)
        bg = ph.sb("bg", [P, E])
        we = ph.sb("we", [D, E * D])
        be = ph.sb("be", [1, E * D])
        rest = ph.sb("rest", [1, E * D])
        bparts = ph.sb("bparts", [1, 3, E * D], BF16)
        be3 = ph.sb("be3", [3, E * D], BF16)
        one3 = ph.sb("one3", [3, P], BF16)
        mx, sm = ph.sb("mx", [P, T]), ph.sb("sm", [P, T])
        ex, cnt, gate = ph.sb("ex", [P, T, E]), ph.sb("cnt", [P, T, E]), ph.sb("gate", [P, T, E])
        gt = ph.sb("gt", [P, T, E, E])
        xs = ph.sb("xs", [P, 2, S])
        gs = ph.sb("gs", [P, 2, NT * E])
        acc = ph.sb("acc", [P, 2, 2, D])
        weights, split, spread, made, shifted, powered, gated, fetched, gates, mixed, step, summed = (ph.sem(x) for x in
            ("weights", "split", "spread", "made", "shifted", "powered", "gated", "fetched", "gates", "mixed", "step", "summed"))
        PAIR = 2 * E

        with ph.start() as block:
            @block.sync
            def _(sp):
                at.sync(sp)
                sp.dma_start(be[:, :], aps["L0_ffn_be"].rearrange("(o e) d -> o (e d)", o=1)).then_inc(weights, 16)
                sp.dma_start(bg[:, :], aps["L0_ffn_bg"].unsqueeze(0).broadcast_to([P, E])).then_inc(weights, 16)
                sp.dma_start(we[:, :], aps["WeT"]).then_inc(weights, 16)
                at.sync_batches(sp)
                sp.wait_ge(split, BASE + 4)
                for i in range(3):
                    sp.dma_start(be3[i:i + 1, :], bparts[:, i, :]).then_inc(spread, 16)

            @block.tensor
            def _(pe):
                at.pe(pe)
                pe.wait_ge(weights, BASE + 48)
                pe.wait_ge(made, BASE + 2)
                pe.wait_ge(spread, BASE + 48)
                pe.wait_ge(at.nm.ready, BASE + B)
                pe.wait_ge(at.taken, BASE + B)
                pe.wait_ge(at.added, BASE + B)
                with pe.Fori(0, B // 2) as i:
                    for x in range(2):
                        b = 2 * i + x
                        pe.wait_ge(fetched, BASE + b + 1)
                        for j in range(NT):
                            if j % 2 == 0:
                                pe.wait_ge(summed, BASE + PAIR * (2 * b + j // 2 + 1))
                            for half in range(2):
                                out, at_ = psE[j][half][:, :], slice(half * S, (half + 1) * S)
                                pe.matmul(out, xs[:, x, j * P:(j + 1) * P], we[:, at_], start=True, stop=False)
                                m = pe.matmul(out, one3[:, :], be3[:, at_], start=False, stop=True)
                            m.then_inc(mixed, 1)

            @block.scalar
            def _(a):
                at.act(a)
                a.wait_ge(shifted, BASE + 1)
                a.activation(ex[:, :, :], at.lg[:, :, :], ACT.Exp).then_inc(powered, 1)
                a.wait_ge(at.held, BASE + B)
                with a.Fori(0, B // 2) as i:
                    for x in range(2):
                        b = 2 * i + x
                        a.wait_ge(mixed, BASE + NT * (b - 1))
                        a.copy(xs[:, x, :], xall[:, bass.ds(b, 1), :].rearrange("p o s -> p (o s)")).then_inc(fetched, 1)
                        a.wait_ge(gated, BASE + 1)
                        a.wait_ge(summed, BASE + PAIR * 2 * b)
                        a.copy(gs[:, x, :], gate[:, bass.ds(b * NT, NT), :].rearrange("p j e -> p (j e)")).then_inc(gates, 1)

            @block.vector
            def _(v):
                at.dve(v)
                v.sem_inc(summed, 2 * PAIR)
                v.wait_ge(weights, BASE + 48)
                count = [0]
                v.tensor_copy(bparts[:, 0, :], be[:, :]).then_inc(split, 1)
                v.wait_ge(split, BASE + 1)
                v.tensor_tensor(rest[:, :], be[:, :], bparts[:, 0, :], ALU.subtract).then_inc(split, 1)
                v.wait_ge(split, BASE + 2)
                v.tensor_copy(bparts[:, 1, :], rest[:, :]).then_inc(split, 1)
                v.wait_ge(split, BASE + 3)
                v.tensor_tensor(bparts[:, 2, :], rest[:, :], bparts[:, 1, :], ALU.subtract).then_inc(split, 1)
                then = softmax(v, at, step, count, mx, sm, ex, shifted, powered, bias=bg[:, :])
                pr = ex
                then(v.tensor_tensor(pr[:, :, :], ex[:, :, :], over(sm[:, :], 2, E), ALU.mult))
                v.wait_ge(made, BASE + 2)
                for f in range(E):
                    if f:
                        m = v.tensor_tensor(gt[:, :, 0:f, f], over(pr[:, :, f], 2, f), pr[:, :, 0:f], ALU.is_gt)
                    if f + 1 < E:
                        m = v.tensor_tensor(gt[:, :, f + 1:, f], over(pr[:, :, f], 2, E - 1 - f), pr[:, :, f + 1:], ALU.is_ge)
                then(m)
                then(v.reduce_sum(cnt[:, :, :], gt[:, :, :, :], AX))
                then(v.scalar_tensor_tensor(gate[:, :, :], cnt[:, :, :], 1.5, pr[:, :, :], ALU.is_lt, ALU.mult))
                then(v.reduce_sum(sm[:, :], gate[:, :, :], AX))
                then(v.reciprocal(mx[:, :], sm[:, :]))
                v.tensor_tensor(gate[:, :, :], gate[:, :, :], over(mx[:, :], 2, E), ALU.mult).then_inc(gated, 1)

                with v.Fori(0, B // 2) as i:
                    for x in range(2):
                        b = 2 * i + x
                        v.wait_ge(gates, BASE + b + 1)
                        for p in range(2):
                            v.wait_ge(mixed, BASE + NT * b + 2 * p + 2)
                            k = 0
                            for e in range(E):
                                for t in range(2):
                                    j = 2 * p + t
                                    tile = at.nm.tile(b, j)
                                    v.wait_ge(summed, BASE + PAIR * (2 * b + p + 2) + k - 1)
                                    v.scalar_tensor_tensor(tile if e == E - 1 else acc[:, t, e % 2, :],
                                                           psE[j][e // 4][:, (e % 4) * P:(e % 4 + 1) * P],
                                                           gs[:, x, j * E + e:j * E + e + 1],
                                                           acc[:, t, (e + 1) % 2, :] if e else tile,
                                                           ALU.mult, ALU.add).then_inc(summed, 1)
                                    k += 1

            @block.gpsimd
            def _(g):
                g.memset(one3[:, :], 1.0).then_inc(made, 1)
                g.memset(gt[:, :, :, :], 0.0).then_inc(made, 1)
                at.pool(g)


class Projections:

    def __init__(self, ph, bias_of):
        self.net, self.bias_of = ph.net, bias_of
        self.w = ph.sb("w", [D, 3, D])
        self.cols = ph.sb("bias_cols", [D, 2])
        self.row = ph.sb("bias_row", [P, D])
        self.loaded, self.vals = ph.sem("weights"), ph.sem("vals")

    def load(self, sp, weights):
        for n, x in enumerate(weights):
            sp.dma_start(self.w[:, n, :], x).then_inc(self.loaded, 16)
        for n in range(2):
            sp.dma_start(self.cols[:, n:n + 1], self.bias_of[n].unsqueeze(1)).then_inc(self.loaded, 16)
        sp.dma_start(self.row[:, :], self.bias_of[2].unsqueeze(0).broadcast_to([P, D])).then_inc(self.loaded, 16)

    def wait(self, eng):
        eng.wait_ge(self.loaded, BASE + 16 * 6)

    def values(self, pe, psV, x, w):
        for j in range(NT):
            m = pe.matmul(psV[:, j * P:(j + 1) * P], x[:, j * P:(j + 1) * P], w, start=True, stop=True)
        return m

    def dve_values(self, v, psV, b):
        v.tensor_tensor(self.net.V[:, bass.ds(b * H, H), :, :].rearrange("p h j d -> p j h d"),
                        psV[:, :].rearrange("p (j h d) -> p j h d", j=NT, h=H),
                        over(self.row[:, :].rearrange("p (h d) -> p h d", h=H), 1, NT), ALU.add).then_inc(self.vals, 1)


def values_out(net, a, psV, b):
    return a.copy(net.V[:, bass.ds(b * H, H), :, :].rearrange("p h j d -> p j h d"),
                  psV[:, :].rearrange("p (j h d) -> p j h d", j=NT, h=H))


def linear_prep(net):
    nc, aps = net.nc, net.aps
    with Phase(net, "la") as ph:
        pr = Projections(ph, [aps[f"L1_attn_a_b{x}"] for x in "qkv"])
        low, ex, f = ph.sb("low", [P, 2, S]), ph.sb("ex", [P, 2, S]), ph.sb("f", [P, 2, S])
        high = ph.sb("high", [P, 2, S])
        psT, psQ, psK, psV = (ph.ps(n, [P, S]) for n in ("psT", "psQ", "psK", "psV"))
        nm = Norm(ph, "n", psT)
        sp_q = Split(ph, "q", P, f[:, 0, :])
        sp_k = Split(ph, "k", P, f[:, 1, :])
        proj, clipped, powered, mapped = (ph.sem(x) for x in ("proj", "clipped", "powered", "mapped"))
        with ph.start() as block:
            @block.sync
            def _(sp):
                pr.load(sp, [aps[f"L1a_W{x}T"] for x in "qkv"])
                with sp.Fori(0, B) as b:
                    sp_q.store(sp, b, net.QS, True)
                    sp_k.store(sp, b, net.KS, False)
                for s in (sp_q, sp_k):
                    s.end(sp)

            @block.tensor
            def _(pe):
                pr.wait(pe)

                def body(b, more):
                    pe.wait_ge(nm.ready, BASE + b + 1)
                    pe.wait_ge(clipped, BASE + 4 * b)
                    pe.matmul(psQ[:, :], pr.w[:, 0, :], nm.xT[:, :], start=True, stop=True).then_inc(proj, 1)
                    pe.matmul(psK[:, :], pr.w[:, 1, :], nm.xT[:, :], start=True, stop=True).then_inc(proj, 1)
                    pe.wait_ge(pr.vals, BASE + b)
                    pr.values(pe, psV, nm.xT, pr.w[:, 2, :]).then_inc(proj, 1)
                    if more:
                        nm.turn(pe, b + 1)

                batches(pe, lambda: nm.turn(pe, 0), body)

            @block.scalar
            def _(a):
                def body(b, more):
                    for n in range(2):
                        a.wait_ge(clipped, BASE + 4 * b + 2 * n + 2)
                        a.wait_ge(mapped, BASE + 2 * b + n - 1)
                        a.activation(ex[:, n, :], low[:, n, :], ACT.Exp).then_inc(powered, 1)
                    if more:
                        nm.keep(a, b + 1, (proj, 3 * b + 3))
                    sp_q.act(a, b, (mapped, 2 * b + 1))
                    sp_k.act(a, b, (mapped, 2 * b + 2))

                batches(a, lambda: nm.keep(a, 0, (proj, 0)), body)

            @block.vector
            def _(v):
                pr.wait(v)

                def before():
                    nm.stats(v, 0)
                    nm.norm(v, 0)

                def body(b, more):
                    v.wait_ge(powered, BASE + 2 * b)
                    v.wait_ge(mapped, BASE + 2 * b)
                    for n, ps in enumerate((psQ, psK)):
                        v.wait_ge(proj, BASE + 3 * b + n + 1)
                        v.tensor_scalar(high[:, n, :], ps[:, :], pr.cols[:, n:n + 1], 0.0, ALU.add, ALU.max).then_inc(clipped, 1)
                        v.tensor_scalar(low[:, n, :], ps[:, :], pr.cols[:, n:n + 1], 0.0, ALU.add, ALU.min).then_inc(clipped, 1)
                    if more:
                        nm.stats(v, b + 1)
                    v.wait_ge(proj, BASE + 3 * b + 3)
                    pr.dve_values(v, psV, b)
                    for n, s in enumerate((sp_q, sp_k)):
                        v.wait_ge(powered, BASE + 2 * b + n + 1)
                        v.wait_ge(s.rest, BASE + b)
                        v.tensor_tensor(f[:, n, :], high[:, n, :], ex[:, n, :], ALU.add).then_inc(mapped, 1)
                    if more:
                        nm.norm(v, b + 1)
                    sp_q.dve(v, b)
                    sp_k.dve(v, b)

                batches(v, before, body)

            @block.gpsimd
            def _(g):
                def body(b, more):
                    if more:
                        nm.power(g, b + 1)
                    sp_q.pool(g, b)
                    sp_k.pool(g, b)

                batches(g, lambda: nm.power(g, 0), body)


def relative_tables(net, keep):
    nc, aps = net.nc, net.aps
    with Phase(net, "rt") as ph:
        w = ph.sb("w", [D, 2, D])
        bias = ph.sb("bias", [1, 2, D])
        rel = ph.sb("rel", [D, 2, P])
        tab = ph.sb("tab", [P, TW])
        r1 = ph.sb("r1", [P, TW])
        part = ph.sb("part", [P, 3, TW], BF16)
        zero = ph.sb("zero", [P, P])
        psP, psQ = ph.ps("psP", [P, P]), ph.ps("psQ", [P, P])
        weights, proj, filled, first, rest, second, third, kept, zeroed = (ph.sem(x) for x in
            ("weights", "proj", "filled", "first", "rest", "second", "third", "kept", "zeroed"))
        with ph.start() as block:
            @block.sync
            def _(sp):
                for n, x in enumerate(("k", "q")):
                    sp.dma_start(w[:, n, :], aps[f"L0b_Wp{x}T"]).then_inc(weights, 16)
                    sp.dma_start(bias[:, n, :], aps[f"L0_attn_b_bp{x}"].unsqueeze(0)).then_inc(weights, 16)
                sp.dma_start(rel[:, 0, :], aps["relT"]).then_inc(weights, 16)
                sp.dma_start(rel[:, 1, :], aps["relT_reversed"]).then_inc(weights, 16)
                sp.wait_ge(third, BASE + 1)
                copies = net.TB.rearrange("h (r c) x -> (h r) c x", c=NC6)
                for i, (lo, hi) in enumerate(RUNS):
                    sp.dma_start(copies[:, lo:hi, 0:EXT], part[:, 0:hi - lo, 0:EXT]).then_inc(kept, 16)
                    sp.dma_start(copies[:, lo:hi, EXT:], over(part[:, i, EXT:], 1, hi - lo)).then_inc(kept, 16)
                sp.wait_ge(kept, BASE + 32 * len(RUNS))

            @block.tensor
            def _(pe):
                pe.wait_ge(weights, BASE + 16 * 6)
                for n, ps in enumerate((psP, psQ)):
                    pe.matmul(ps[:, :], w[:, n, :], rel[:, n, :], start=True, stop=False)
                    pe.matmul(ps[:, :], bias[:, n, :], net.ones[:, 0:P], start=False, stop=True).then_inc(proj, 1)

            @block.vector
            def _(v):
                v.memset(zero[:, :], 0.0).then_inc(zeroed, 1)
                v.wait_ge(zeroed, BASE + 1)
                v.wait_ge(proj, BASE + 2)
                z = zero[:, :]
                fill = lambda lo, hi, col: v.tensor_scalar(tab[:, lo:hi], zero[:, 0:hi - lo], col, None, ALU.add).then_inc(filled, 1)
                first_k, last_k, first_q, last_q = psP[:, 0:1], psP[:, P - 1:P], psQ[:, P - 1:P], psQ[:, 0:1]
                fill(0, P - 1, first_k)
                v.tensor_copy(tab[:, P - 1:2 * P - 1], psP[:, :]).then_inc(filled, 1)
                fill(2 * P - 1, 3 * P - 1, last_k)
                fill(3 * P - 1, 3 * P, last_k)
                fill(EXT, EXT + P, last_q)
                v.tensor_copy(tab[:, EXT + P:EXT + 2 * P], psQ[:, :]).then_inc(filled, 1)
                fill(EXT + 2 * P, 2 * EXT, first_q)
                fill(2 * EXT, 2 * EXT + P, first_q)
                fill(2 * EXT + P, TW, last_q)
                v.wait_ge(filled, BASE + 9)
                v.tensor_copy(keep[:, 0:1], tab[:, 0:1])
                v.tensor_copy(keep[:, 1:2], tab[:, EXT - 1:EXT])
                v.tensor_copy(part[:, 0, :], tab[:, :]).then_inc(first, 1)
                v.wait_ge(first, BASE + 1)
                v.tensor_tensor(r1[:, :], tab[:, :], part[:, 0, :], ALU.subtract).then_inc(rest, 1)
                v.wait_ge(rest, BASE + 1)
                v.tensor_copy(part[:, 1, :], r1[:, :]).then_inc(second, 1)
                v.wait_ge(second, BASE + 1)
                v.tensor_tensor(part[:, 2, :], r1[:, :], part[:, 1, :], ALU.subtract).then_inc(third, 1)


def relative_prep(net, keep):
    nc, aps = net.nc, net.aps
    with Phase(net, "ra") as ph:
        pr = Projections(ph, [aps[f"L0_attn_b_b{x}"] for x in "qkv"])
        far = ph.sb("far", [P, 2, FAR])
        psT, psQ, psK, psV = (ph.ps(n, [P, S]) for n in ("psT", "psQ", "psK", "psV"))
        nm = Norm(ph, "n", psT)
        sp_q = Split(ph, "q", P, psQ[:, :], bias=pr.cols[:, 0:1])
        sp_k = Split(ph, "k", P, psK[:, :], bias=pr.cols[:, 1:2])
        sp_l = Split(ph, "l", P, far[:, 0, :], FAR)
        sp_h = Split(ph, "h", P, far[:, 1, :], FAR)
        proj, shifted = ph.sem("proj"), ph.sem("shifted")
        with ph.start() as block:
            @block.sync
            def _(sp):
                pr.load(sp, [aps[f"L0b_W{x}T"] for x in "qkv"])
                with sp.Fori(0, B) as b:
                    sp_q.store(sp, b, net.QS, True)
                    sp_k.store(sp, b, net.KS, False)
                    sp_l.store(sp, b, net.KLS, False)
                    sp_h.store(sp, b, net.KHS, False)
                for s in (sp_q, sp_k, sp_l, sp_h):
                    s.end(sp)

            @block.tensor
            def _(pe):
                pr.wait(pe)

                def body(b, more):
                    pe.wait_ge(nm.ready, BASE + b + 1)
                    pe.wait_ge(sp_q.rest, BASE + b)
                    pe.matmul(psQ[:, :], pr.w[:, 0, :], nm.xT[:, :], start=True, stop=True).then_inc(proj, 1)
                    pe.wait_ge(sp_k.rest, BASE + b)
                    pe.wait_ge(shifted, BASE + 2 * b)
                    pe.matmul(psK[:, :], pr.w[:, 1, :], nm.xT[:, :], start=True, stop=True).then_inc(proj, 1)
                    pe.wait_ge(pr.vals, BASE + b)
                    pr.values(pe, psV, nm.xT, pr.w[:, 2, :]).then_inc(proj, 1)
                    if more:
                        nm.turn(pe, b + 1)

                batches(pe, lambda: nm.turn(pe, 0), body)

            @block.scalar
            def _(a):
                def body(b, more):
                    sp_q.act(a, b, (proj, 3 * b + 1))
                    sp_k.act(a, b, (proj, 3 * b + 2))
                    if more:
                        nm.keep(a, b + 1, (proj, 3 * b + 3))
                    sp_l.act(a, b, (shifted, 2 * b + 1))
                    sp_h.act(a, b, (shifted, 2 * b + 2))

                batches(a, lambda: nm.keep(a, 0, (proj, 0)), body)

            @block.vector
            def _(v):
                pr.wait(v)

                def before():
                    nm.stats(v, 0)
                    nm.norm(v, 0)

                def body(b, more):
                    if more:
                        nm.stats(v, b + 1)
                    sp_q.dve(v, b)
                    sp_k.dve(v, b)
                    v.wait_ge(sp_k.rest, BASE + b + 1)
                    for n, s in enumerate((sp_l, sp_h)):
                        v.wait_ge(s.rest, BASE + b)
                        v.tensor_scalar(far[:, n, :], psK[:, n * (S - FAR):n * (S - FAR) + FAR], pr.cols[:, 1:2],
                                        keep[:, n:n + 1], ALU.add, ALU.add).then_inc(shifted, 1)
                    if more:
                        nm.norm(v, b + 1)
                    v.wait_ge(proj, BASE + 3 * b + 3)
                    pr.dve_values(v, psV, b)
                    sp_l.dve(v, b)
                    sp_h.dve(v, b)

                batches(v, before, body)

            @block.gpsimd
            def _(g):
                def body(b, more):
                    if more:
                        nm.power(g, b + 1)
                    for s in (sp_q, sp_k, sp_l, sp_h):
                        s.pool(g, b)

                batches(g, lambda: nm.power(g, 0), body)


def rotary_prep(net):
    nc, aps = net.nc, net.aps
    with Phase(net, "ya") as ph:
        wx = ph.sb("wx", [D, 6, D])
        bias = aps["L1_attn_b_in_proj_b"]
        pr = Projections(ph, [bias[n * D:(n + 1) * D] for n in range(3)])
        rot = ph.sb("rot", [D, 2, S])
        t = ph.sb("t", [D, 3, 2, S])
        turned = ph.sb("turned", [D, 3, S])
        psT, psQ, psK, psV = (ph.ps(n, [P, S]) for n in ("psT", "psQ", "psK", "psV"))
        ps = [[ph.ps(f"ps{i}{x}", [P, S]) for x in range(2)] for i in range(2)]
        nm = Norm(ph, "n", psT)
        sp_q = Split(ph, "q", P, psQ[:, :], bias=pr.cols[:, 0:1])
        sp_k = Split(ph, "k", P, psK[:, :], bias=pr.cols[:, 1:2])
        weights, first, products, rotated, proj = (ph.sem(x) for x in
            ("weights_x", "first", "products", "rotated", "proj"))
        with ph.start() as block:
            @block.sync
            def _(sp):
                sp.dma_start(wx[:, :, :], aps["L1b_w"]).then_inc(weights, 16)
                sp.dma_start(rot[:, :, :], aps["L1b_rot"]).then_inc(weights, 16)
                pr.load(sp, [aps["L1b_in"][:, n, :] for n in range(3)])
                with sp.Fori(0, B) as b:
                    sp_q.store(sp, b, net.QS, True)
                    sp_k.store(sp, b, net.KS, False)
                for s in (sp_q, sp_k):
                    s.end(sp)

            @block.tensor
            def _(pe):
                pe.wait_ge(weights, BASE + 32)
                pr.wait(pe)

                def turning(b, n):
                    m = 3 * b + n
                    pe.wait_ge(products, BASE + 2 * m - 2)
                    for x in range(2):
                        mm = pe.matmul(ps[n % 2][x][:, :], wx[:, 2 * n + x, :], nm.xT[:, :], start=True, stop=True)
                    mm.then_inc(first, 1)

                def projection(b, n):
                    pe.wait_ge(rotated, BASE + 3 * b + n + 1)
                    if n == 2:
                        pe.wait_ge(pr.vals, BASE + b)
                        pr.values(pe, psV, turned[:, 2, :], pr.w[:, 2, :]).then_inc(proj, 1)
                    else:
                        pe.wait_ge((sp_q, sp_k)[n].rest, BASE + b)
                        pe.matmul((psQ, psK)[n][:, :], pr.w[:, n, :], turned[:, n, :], start=True, stop=True).then_inc(proj, 1)

                def body(b, more):
                    pe.wait_ge(nm.ready, BASE + b + 1)
                    turning(b, 0)
                    turning(b, 1)
                    projection(b, 0)
                    turning(b, 2)
                    projection(b, 1)
                    if more:
                        nm.turn(pe, b + 1)
                    projection(b, 2)

                batches(pe, lambda: nm.turn(pe, 0), body)

            @block.scalar
            def _(a):
                def body(b, more):
                    sp_q.act(a, b, (proj, 3 * b + 1))
                    sp_k.act(a, b, (proj, 3 * b + 2))
                    if more:
                        nm.keep(a, b + 1, (first, 3 * b + 3))

                batches(a, lambda: nm.keep(a, 0, (first, 0)), body)

            @block.vector
            def _(v):
                v.wait_ge(weights, BASE + 32)
                pr.wait(v)

                def before():
                    nm.stats(v, 0)
                    nm.norm(v, 0)

                def body(b, more):
                    for n in range(3):
                        m = 3 * b + n
                        v.wait_ge(first, BASE + m + 1)
                        v.wait_ge(rotated, BASE + m - 2)
                        for x in range(2):
                            v.tensor_tensor(t[:, n, x, :], ps[n % 2][x][:, :], rot[:, x, :], ALU.mult).then_inc(products, 1)
                        if more and n == 0:
                            nm.stats(v, b + 1)
                        if n == 1:
                            sp_q.dve(v, b)
                        if n == 2:
                            sp_k.dve(v, b)
                    if more:
                        nm.norm(v, b + 1)
                    v.wait_ge(proj, BASE + 3 * b + 3)
                    pr.dve_values(v, psV, b)

                batches(v, before, body)

            @block.gpsimd
            def _(g):
                def body(b, more):
                    if more:
                        nm.power(g, b + 1)
                    for n in range(3):
                        m = 3 * b + n
                        g.wait_ge(products, BASE + 2 * m + 2)
                        g.wait_ge(proj, BASE + m - 2)
                        g.tensor_tensor(turned[:, n, :], t[:, n, 0, :], t[:, n, 1, :], ALU.add).then_inc(rotated, 1)
                    sp_q.pool(g, b)
                    sp_k.pool(g, b)

                batches(g, lambda: nm.power(g, 0), body)


QDIAG = (896, 1024, 512, 0)


def heads_max(net, tag, scale):
    nc = net.nc
    N = B * H
    ORDER = (3, 2, 0, 1)
    with Phase(net, tag) as ph:
        hl = HeadLoads(ph, NC6 * DH, net.QS, net.KS)
        mask = ph.sb("mask", [P, CAUSAL])
        mx = ph.sb("mx", [P, R, NT])
        nm = ph.sb("nm", [P, R, NT])
        e = ph.sb("e", [P, R, CAUSAL])
        w = ph.sb("w", [P, R, CAUSAL])
        sc = ph.ps("sc", [P, 3 * S])
        tr = ph.ps("tr", [P, 3 * S])
        masks, scored, found, negated, powered, turned, weighed, summed = (ph.sem(x) for x in
            ("masks", "scored", "found", "negated", "powered", "turned", "weighed", "summed"))
        with ph.start() as block:
            @block.sync
            def _(sp):
                hl.sync(sp, scored)

            def scores(pe, i, u, n):
                hl.wait_loaded(pe, i, u)
                for x, I in enumerate(ORDER):
                    at, width = QDIAG[I], (I + 1) * P
                    pe.wait_ge(found, BASE + NT * (n - 1) + (x + 1 if x != 1 else 3))
                    m = pe.matmul(sc[:, at:at + width], hl.q[:, u % R, I * P:width], hl.k[:, u % R, 0:width],
                                  start=True, stop=True)
                m.then_inc(scored, 1)

            def turn(pe, u, n):
                pe.wait_ge(powered, BASE + NT * n + NT)
                pe.wait_ge(weighed, BASE + n)
                for J in range(NT):
                    for I in range(J, NT):
                        at, to = QDIAG[I] + J * P, DIAG[J] + (I - J) * P
                        m = pe.transpose(tr[:, to:to + P], e[:, u % R, at:at + P], net.idf[:, :])
                m.then_inc(turned, 1)

            @block.tensor
            def _(pe):
                def step(i, u, last):
                    t = u + AHEAD
                    if not last or t < UT:
                        scores(pe, i + t // UT, t % UT, UT * i + t)
                    if not last or u + 1 < UT:
                        turn(pe, (u + 1) % UT, UT * i + u + 1)
                    hl.context(pe, i, u, UT * i + u, w[:, u % R, :], weighed, summed)

                for u in range(AHEAD):
                    scores(pe, 0, u, u)
                turn(pe, 0, 0)
                with pe.Fori(0, N // UT - 1) as i:
                    for u in range(UT):
                        step(i, u, False)
                for u in range(UT):
                    step(N // UT - 1, u, True)

            @block.vector
            def _(v):
                v.wait_ge(masks, BASE + 2)

                def find(u, n):
                    v.wait_ge(scored, BASE + n + 1)
                    waited(net, v, (turned, n - R + 1))
                    for I in ORDER:
                        part = slice(QDIAG[I], QDIAG[I] + (I + 1) * P)
                        v.tensor_tensor_reduce(e[:, u % R, part], sc[:, part], mask[:, part], 1.0, -3e38,
                                               ALU.add, ALU.max, mx[:, u % R, I:I + 1]).then_inc(found, 1)
                    v.wait_ge(found, BASE + NT * n + NT)
                    v.tensor_scalar(nm[:, u % R, :], mx[:, u % R, :], -scale, None, ALU.mult).then_inc(negated, 1)

                def keep(u, n):
                    v.wait_ge(turned, BASE + n + 1)
                    v.wait_ge(summed, BASE + n - R + 1)
                    v.tensor_copy(w[:, u % R, :], tr[:, 0:CAUSAL]).then_inc(weighed, 1)

                def step(i, u, last):
                    t = u + AHEAD
                    if not last or t < UT:
                        find(t % UT, UT * i + t)
                    if not last or u + 1 < UT:
                        keep((u + 1) % UT, UT * i + u + 1)

                for u in range(AHEAD):
                    find(u, u)
                keep(0, 0)
                with v.Fori(0, N // UT - 1) as i:
                    for u in range(UT):
                        step(i, u, False)
                for u in range(UT):
                    step(N // UT - 1, u, True)

            @block.scalar
            def _(a):
                def item(u, n):
                    a.wait_ge(negated, BASE + n + 1)
                    for I in ORDER:
                        part = slice(QDIAG[I], QDIAG[I] + (I + 1) * P)
                        a.activation(e[:, u % R, part], e[:, u % R, part], ACT.Exp, bias=nm[:, u % R, I:I + 1],
                                     scale=scale).then_inc(powered, 1)

                hl.act(a, item, summed)

            @block.gpsimd
            def _(g):
                g.memset(mask[:, :], 0.0).then_inc(masks, 1)
                hl.pool_start(g)
                for I in range(NT):
                    x = mask[:, QDIAG[I] + I * P:QDIAG[I] + (I + 1) * P]
                    m = g.affine_select(out=x, in_=x, compare_op=ALU.is_ge, fill=-1e30, base=0,
                                        pattern=[[-1, P]], channel_multiplier=1)
                m.then_inc(masks, 1)
                with g.Fori(0, N // UT) as i:
                    for u in range(UT):
                        hl.pool_values(g, UT * i + u, u, summed)


C1, C2 = NT * P, (NT - 1) * P


def heads_relative(net, tag, scale):
    nc = net.nc
    rows = NC6 * DH
    G = 16
    with Phase(net, tag) as ph:
        q = ph.sb("q", [rows, B, S], BF16)
        k = ph.sb("k", [rows, B, S], BF16)
        kl = ph.sb("kl", [rows, B, FAR], BF16)
        kh = ph.sb("kh", [rows, B, FAR], BF16)
        tb = ph.sb("tb", [rows, TW], BF16)
        c0 = ph.sb("c0", [P, B, NT, P])
        c1 = ph.sb("c1", [P, B, NT - 1, P])
        d0 = ph.sb("d0", [P, B, NT, P])
        d1 = ph.sb("d1", [P, B, NT - 1, P])
        bf = ph.sb("bf", [P, NT * (S + P)])
        v1 = ph.sb("v1", [P, B, NT, VW])
        mx = ph.sb("mx", [P, 2, NT])
        nm = ph.sb("nm", [P, 2, NT])
        ss = ph.sb("ss", [P, 2, NT, S])
        w = ph.sb("w", [P, NT, S])
        o = ph.sb("o", [P, 2, S])
        sc = [ph.ps(f"sc{i}", [P, S]) for i in range(2)]
        pc = [ph.ps(f"pc{i}", [P, S]) for i in range(2)]
        tr = [ph.ps(f"tr{i}", [P, S]) for i in range(2)]
        po = [ph.ps(f"po{i}", [P, S]) for i in range(2)]
        names = ("stacks", "fars", "tabled", "ctab", "dtab", "turned", "biased", "scored", "full", "negated", "powered",
                 "blocks", "summed", "copied", "valued", "made", "placed")
        (stacks, fars, tabled, ctab, dtab, turned, biased_, scored, full, negated, powered, blocks, summed, copied,
         valued, made, placed) = (ph.sem(x) for x in names)
        weighed = [ph.sem(f"weighed{i}") for i in range(2)]
        stored = [ph.sem(f"stored{i}") for i in range(2)]
        keysF, keysL, posF, posL = 0, EXT, 2 * EXT, 2 * EXT + P
        CH = P // G

        with ph.start() as block:
            @block.sync
            def _(sp):
                heads = lambda t: t.rearrange("(b h) r s -> h r b s", b=B)

                def load(h):
                    for dst, src, sem in ((q, net.QS, stacks), (k, net.KS, stacks),
                                          (kl, net.KLS, fars), (kh, net.KHS, fars)):
                        if dst is kl:
                            sp.dma_start(tb[:, :], net.TB[bass.ds(h, 1), :, :].rearrange("o r s -> (o r) s")).then_inc(stacks, 16)
                        sp.dma_start(dst[:, :, :], heads(src)[bass.ds(h, 1), :, :, :].rearrange("o r b s -> (o r) b s"))\
                            .then_inc(sem, 16)

                def store(h, g):
                    sp.wait_ge(copied, BASE + 2 * h + g + 1)
                    for u in range(U):
                        bh = (U * g + u) * H + h
                        sp.dma_start(net.CU[bass.ds(bh, 1), :, :], o[VW * u:VW * u + DH + 1, g, :]).then_inc(stored[g], 16)

                load(0)
                with sp.Fori(0, H - 1) as h:
                    store(h, 0)
                    sp.wait_ge(scored, BASE + NT * B * (h + 1))
                    load(h + 1)
                    store(h, 1)
                store(H - 1, 0)
                store(H - 1, 1)
                for x in stored:
                    sp.wait_ge(x, BASE + 16 * U * H)

            @block.tensor
            def _(pe):
                def tables(h):
                    pe.wait_ge(stacks, BASE + 48 * h + 48)
                    qv = q[:, :, :].rearrange("r b (i s) -> r s b i", i=NT)
                    kv = k[:, :, :].rearrange("r b (i s) -> r s b i", i=NT)
                    pe.wait_ge(full, BASE + NT * B * h)
                    for c in range(CH):
                        if c >= 2:
                            pe.wait_ge(ctab, BASE + 2 * CH * h + 2 * c - 2)
                        banks = pc if c % 2 else sc
                        for s in range(G):
                            x = G * c + s
                            full_, part = banks[0][:, 32 * s:32 * s + 32], banks[1][:, 24 * s:24 * s + 24]
                            at = 191 - x
                            pe.matmul(full_, tb[:, at:at + P], qv[:, x, :, :], start=True, stop=True)
                            pe.matmul(part[64:128], tb[:, at - 64:at], qv[:, x, :, 1:NT], start=True, stop=True)
                            m = pe.matmul(part[0:64], tb[:, at + P:at + P + 64], qv[:, x, :, 0:NT - 1], start=True, stop=True)
                        m.then_inc(tabled, 1)
                        if c:
                            pe.wait_ge(dtab, BASE + 2 * CH * h + 2 * c)
                        else:
                            for x in weighed:
                                pe.wait_ge(x, BASE + 2 * (B * h - 1))
                        for s in range(G):
                            x = G * c + s
                            full_, part = tr[0][:, 32 * s:32 * s + 32], tr[1][:, 24 * s:24 * s + 24]
                            at = keysL + 191 - x
                            pe.matmul(full_, tb[:, at:at + P], kv[:, x, :, :], start=True, stop=True)
                            if x >= REL:
                                m = pe.matmul(part, tb[:, at + P:at + 2 * P], kv[:, x, :, 0:NT - 1], start=True, stop=True)
                            else:
                                m = pe.matmul(part, tb[:, at - P:at], kv[:, x, :, 1:NT], start=True, stop=True)
                        m.then_inc(tabled, 1)
                    pe.wait_ge(ctab, BASE + 2 * CH * h + 2 * CH)
                    pe.wait_ge(dtab, BASE + 2 * CH * h + 2 * CH)
                    pe.wait_ge(fars, BASE + 32 * h + 32)

                def positions(h, b):
                    pe.wait_ge(biased_, BASE + 3 * (B * h + b))
                    for i in range(NT):
                        pe.transpose(pc[0][:, i * P:(i + 1) * P], c0[:, b, i, :], net.idf[:, :])
                    for i in range(NT - 1):
                        m = pe.transpose(pc[1][:, i * P:(i + 1) * P], c1[:, b, i, :], net.idf[:, :])
                    m.then_inc(turned, 1)

                def scores(h, b, I):
                    s = sc[I % 2]
                    pe.wait_ge(full, BASE + NT * (B * h + b) + I - 1)
                    lo, hi = max(0, I * P - REL), min(S, I * P + P + REL)
                    qi = q[:, b, I * P:(I + 1) * P]
                    if lo:
                        pe.matmul(s[:, 0:lo], qi, kl[:, b, 0:lo], start=True, stop=False)
                        pe.matmul(s[:, 0:lo], tb[:, posF:posF + P], k[:, b, 0:lo], start=False, stop=True)
                    if hi < S:
                        pe.matmul(s[:, hi:S], qi, kh[:, b, hi - (S - FAR):FAR], start=True, stop=False)
                        pe.matmul(s[:, hi:S], tb[:, posL:posL + P], k[:, b, hi:S], start=False, stop=True)
                    pe.matmul(s[:, lo:hi], qi, k[:, b, lo:hi], start=True, stop=True).then_inc(scored, 1)

                def turn(h, b, J):
                    n = B * h + b
                    if J == 0:
                        pe.wait_ge(powered, BASE + NT * n + NT)
                    pe.wait_ge(weighed[J % 2], BASE + 2 * n + J // 2)
                    for I in range(NT):
                        m = pe.transpose(tr[J % 2][:, I * P:(I + 1) * P], ss[:, b % 2, I, J * P:(J + 1) * P], net.idf[:, :])
                    m.then_inc(blocks, 1)

                def context(h, b, J):
                    n = B * h + b
                    if J == 0:
                        pe.wait_ge(valued, BASE + n + 1)
                        if b % U == 0:
                            pe.wait_ge(copied, BASE + 2 * h + b // U - 1)
                    pe.wait_ge(weighed[J % 2], BASE + 2 * n + J // 2 + 1)
                    pe.matmul(po[b // U][VW * (b % U):VW * (b % U + 1), :], v1[:, b, J, :], w[:, J, :],
                              start=J == 0, stop=J == NT - 1).then_inc(summed, 1)

                def front(h, b, back=None):
                    if b == 0:
                        positions(h, 0)
                    scores(h, b, 0)
                    scores(h, b, 1)
                    if back:
                        turn(*back, 0)
                        turn(*back, 1)
                    scores(h, b, 2)
                    scores(h, b, 3)
                    if back:
                        contexts(*back, ahead=(h, b + 1))
                    else:
                        positions(h, b + 1)

                def contexts(h, b, ahead=None):
                    context(h, b, 0)
                    turn(h, b, 2)
                    context(h, b, 1)
                    turn(h, b, 3)
                    if ahead and ahead[1] < B:
                        positions(*ahead)
                    context(h, b, 2)
                    context(h, b, 3)

                tables(0)
                front(0, 0)
                with pe.Fori(0, H - 1) as h:
                    for b in range(B - 1):
                        front(h, b + 1, (h, b))
                    tables(h + 1)
                    front(h + 1, 0, (h, B - 1))
                for b in range(B - 1):
                    front(H - 1, b + 1, (H - 1, b))
                turn(H - 1, B - 1, 0)
                turn(H - 1, B - 1, 1)
                contexts(H - 1, B - 1)

            @block.vector
            def _(v):
                v.memset(bf[:, :], 0.0).then_inc(placed, 1)
                v.wait_ge(placed, BASE + 1)

                def window(first, n, width):
                    run = bf[:, first:first + n * (S + P)]
                    return run.rearrange("p (n w) -> p n w", n=n)[:, :, 0:width]

                def tables(h):
                    for c in range(CH):
                        banks = pc if c % 2 else sc
                        v.wait_ge(tabled, BASE + 2 * CH * h + 2 * c + 1)
                        v.tensor_copy(c0[:, :, :, G * c:G * c + G],
                                      banks[0][:, :].rearrange("p (s b i) -> p b i s", s=G, b=B)).then_inc(ctab, 1)
                        v.tensor_copy(c1[:, :, :, G * c:G * c + G],
                                      banks[1][:, 0:24 * G].rearrange("p (s b i) -> p b i s", s=G, b=B)).then_inc(ctab, 1)
                    v.wait_ge(dtab, BASE + 2 * CH * h + 2 * CH)

                def keep(h, b, J):
                    n = B * h + b
                    v.wait_ge(blocks, BASE + NT * n + J + 1)
                    v.wait_ge(summed, BASE + NT * (n - 1) + J + 1)
                    v.tensor_copy(w[:, J, :], tr[0][:, :]).then_inc(weighed[0], 1)

                def bias(h, b):
                    n = B * h + b
                    v.wait_ge(turned, BASE + n + 1)
                    v.wait_ge(full, BASE + NT * n)
                    v.tensor_tensor(window(0, NT, P), pc[0][:, :].rearrange("p (i k) -> p i k", i=NT), d0[:, b, :, :],
                                    ALU.add).then_inc(biased_, 1)
                    side = pc[1][:, 0:C2].rearrange("p (i k) -> p i k", i=NT - 1)
                    v.tensor_tensor(window(S + REL, NT - 1, REL), side[:, :, REL:P], d1[:, b, :, REL:P],
                                    ALU.add).then_inc(biased_, 1)
                    v.tensor_tensor(window(P, NT - 1, REL), side[:, :, 0:REL], d1[:, b, :, 0:REL],
                                    ALU.add).then_inc(biased_, 1)

                def front(h, b, back=None):
                    n, x = B * h + b, b % 2
                    if b == 0:
                        bias(h, 0)
                    v.wait_ge(biased_, BASE + 3 * n + 3)
                    for I in range(NT):
                        waited(net, v, (scored, NT * n + I + 1), *([(blocks, NT * (n - 1))] if I == 0 else []))
                        v.tensor_tensor_reduce(ss[:, x, I, :], sc[I % 2][:, :], bf[:, I * S:(I + 1) * S], 1.0, -3e38,
                                               ALU.add, ALU.max, mx[:, x, I:I + 1]).then_inc(full, 1)
                        if I == 1 and back:
                            keep(*back, 0)
                    v.wait_ge(full, BASE + NT * n + NT)
                    v.wait_ge(powered, BASE + NT * (n - 1))
                    v.tensor_scalar(nm[:, x, :], mx[:, x, :], -scale, None, ALU.mult).then_inc(negated, 1)
                    if back:
                        keep(*back, 2)
                    if b + 1 < B:
                        bias(h, b + 1)

                tables(0)
                front(0, 0)
                with v.Fori(0, H - 1) as h:
                    for b in range(B - 1):
                        front(h, b + 1, (h, b))
                    tables(h + 1)
                    front(h + 1, 0, (h, B - 1))
                for b in range(B - 1):
                    front(H - 1, b + 1, (H - 1, b))
                keep(H - 1, B - 1, 0)
                keep(H - 1, B - 1, 2)

            @block.scalar
            def _(a):
                def tables(h):
                    for c in range(CH):
                        a.wait_ge(tabled, BASE + 2 * CH * h + 2 * c + 2)
                        a.copy(d0[:, :, :, G * c:G * c + G],
                               tr[0][:, :].rearrange("p (s b i) -> p b i s", s=G, b=B)).then_inc(dtab, 1)
                        a.copy(d1[:, :, :, G * c:G * c + G],
                               tr[1][:, 0:24 * G].rearrange("p (s b i) -> p b i s", s=G, b=B)).then_inc(dtab, 1)

                def keep(h, b, J):
                    n = B * h + b
                    a.wait_ge(blocks, BASE + NT * n + J + 1)
                    a.wait_ge(summed, BASE + NT * (n - 1) + J + 1)
                    a.copy(w[:, J, :], tr[1][:, :]).then_inc(weighed[1], 1)

                def power(h, b, I):
                    x = ss[:, b % 2, I, :]
                    a.activation(x, x, ACT.Exp, bias=nm[:, b % 2, I:I + 1], scale=scale).then_inc(powered, 1)

                def contexts(h, b):
                    g = b // U
                    a.wait_ge(summed, BASE + NT * (B * h + b) + NT)
                    a.wait_ge(stored[g], BASE + 16 * U * h)
                    a.copy(o[:, g, :], po[g][:, :]).then_inc(copied, 1)

                def front(h, b, back=None):
                    if back:
                        keep(*back, 1)
                    a.wait_ge(negated, BASE + B * h + b + 1)
                    power(h, b, 0)
                    power(h, b, 1)
                    if back:
                        keep(*back, 3)
                    power(h, b, 2)
                    power(h, b, 3)
                    if back and back[1] % U == U - 1:
                        contexts(*back)

                tables(0)
                front(0, 0)
                with a.Fori(0, H - 1) as h:
                    for b in range(B - 1):
                        front(h, b + 1, (h, b))
                    tables(h + 1)
                    front(h + 1, 0, (h, B - 1))
                for b in range(B - 1):
                    front(H - 1, b + 1, (H - 1, b))
                keep(H - 1, B - 1, 1)
                keep(H - 1, B - 1, 3)
                contexts(H - 1, B - 1)

            @block.gpsimd
            def _(g):
                g.memset(v1[:, :, :, :], 0.0).then_inc(made, 1)
                g.wait_ge(made, BASE + 1)
                g.memset(v1[:, :, :, DH:2 * DH], 1.0).then_inc(made, 1)
                g.wait_ge(made, BASE + 2)

                def values(h, b):
                    g.tensor_copy(v1[:, b, :, 0:DH], net.V[:, bass.ds(b * H + h, 1), :, :].rearrange("p o j d -> p (o j) d"))\
                        .then_inc(valued, 1)

                for b in range(B):
                    values(0, b)
                with g.Fori(0, H - 1) as h:
                    for b in range(B):
                        waited(net, g, (summed, NT * (B * h + b + 1)))
                        values(h + 1, b)


def expert_affinity(net, tag, attended):
    nc, aps = net.nc, net.aps
    T = B * NT
    with Phase(net, tag) as ph:
        at = Attended(ph, *(ph.ps(n, [P, S]) for n in ("psT", "psY", "psG")), *attended, wg=aps["L1f_gateT"])
        mx, sm = ph.sb("mx", [P, T]), ph.sb("sm", [P, T])
        ex = ph.sb("ex", [P, T, E])
        shifted, powered, step = (ph.sem(x) for x in ("shifted", "powered", "step"))
        with ph.start() as block:
            @block.sync
            def _(sp):
                at.sync(sp)
                at.sync_batches(sp)

            @block.tensor
            def _(pe):
                at.pe(pe)

            @block.scalar
            def _(a):
                at.act(a)
                a.wait_ge(shifted, BASE + 1)
                a.activation(ex[:, :, :], at.lg[:, :, :], ACT.Exp).then_inc(powered, 1)

            @block.vector
            def _(v):
                at.dve(v)
                softmax(v, at, step, [0], mx, sm, ex, shifted, powered)
                v.tensor_tensor(net.aff[:, :, :].rearrange("p j (b e) -> p b j e", b=B),
                                ex[:, :, :].rearrange("p (b j) e -> p b j e", b=B),
                                over(sm[:, :].rearrange("p (b j) -> p b j", b=B), 3, E), ALU.mult)

            @block.gpsimd
            def _(g):
                at.pool(g)


def expert_choice(net, tag):
    nc = net.nc
    L = B * E
    with Phase(net, tag) as ph:
        work = ph.sb("work", [L, S])
        best = ph.sb("best", [L, 8])
        taken = ph.sb("taken", [L, S])
        ones = ph.sb("ones", [L, S])
        count = ph.sb("count", [L, S])
        place = ph.sb("place", [L, S])
        psA, psB = ph.ps("psA", [L, S]), ph.ps("psB", [P, NT * L])
        turned, ready, top, replaced, last, placed, back = (ph.sem(x) for x in
            ("turned", "ready", "top", "replaced", "last", "placed", "back"))
        with ph.start() as block:
            @block.tensor
            def _(pe):
                for j in range(NT):
                    m = pe.transpose(psA[:, j * P:(j + 1) * P], net.aff[:, j, :], net.idf[:, :])
                m.then_inc(turned, 1)
                pe.wait_ge(placed, BASE + 1)
                for j in range(NT):
                    m = pe.transpose(psB[:, j * L:(j + 1) * L], place[:, j * P:(j + 1) * P], net.idf[0:L, 0:L])
                m.then_inc(back, 1)

            @block.vector
            def _(v):
                v.memset(ones[:, :], 1.0)
                v.wait_ge(turned, BASE + 1)
                v.tensor_copy(work[:, :], psA[:, :]).then_inc(ready, 1)
                v.wait_ge(ready, BASE + 1)
                with v.Fori(0, KTOP // 8) as i:
                    waited(net, v, (replaced, i))
                    v.max(best[:, :], work[:, :]).then_inc(top, 1)
                    waited(net, v, (top, i + 1))
                    v.match_replace(work[:, :], best[:, :], work[:, :], -1.0).then_inc(replaced, 1)
                v.wait_ge(replaced, BASE + KTOP // 8)
                v.tensor_scalar(taken[:, :], work[:, :], 0.0, None, ALU.is_lt).then_inc(last, 1)
                v.wait_ge(last, BASE + 1)
                v.tensor_tensor_scan(count[:, :], ones[:, :], taken[:, :], 0.0, ALU.mult, ALU.add).then_inc(last, 1)
                v.wait_ge(last, BASE + 2)
                v.tensor_tensor(count[:, :], count[:, :], taken[:, :], ALU.mult).then_inc(last, 1)
                v.wait_ge(last, BASE + 3)
                v.tensor_scalar(place[:, :], count[:, :], -1.0, None, ALU.add).then_inc(placed, 1)
                v.wait_ge(back, BASE + 1)
                v.tensor_copy(net.slot[:, :, :], psB[:, :].rearrange("p (j l) -> p j l", j=NT)).then_inc(last, 1)


def expert_ffn(net, tag):
    nc, aps = net.nc, net.aps
    FT = FI // P
    with Phase(net, tag) as ph:
        w_gate, w_up = ph.sb("w_gate", [D, E, FI]), ph.sb("w_up", [D, E, FI])
        w_down = ph.sb("w_down", [P, E, FT, D])
        iota = ph.sb("iota", [P, P])
        slot = ph.sb("slot", [P, 2, NT, E])
        af3 = ph.sb("af3", [P, NT, B * E, 3], BF16)
        afr = ph.sb("afr", [P, NT, B * E])
        xn3 = ph.sb("xn3", [P, 2, NT, 3, D], BF16)
        xr = ph.sb("xr", [P, NT, D])
        pick = ph.sb("pick", [P, 2, NT, P], BF16)
        pickT = ph.sb("pickT", [P, 2, S])
        xg = ph.sb("xg", [P, P])
        weight = ph.sb("weight", [P, 2])
        act_ = ph.sb("act", [P, FI])
        hid = ph.sb("hid", [P, FI])
        y = ph.sb("y", [P, D])
        psX, psG, psU, psD, psO, psO1, psW = (ph.ps(n, [P, S]) for n in ("psX", "psG", "psU", "psD", "psO", "psO1", "psW"))
        psP = ph.ps("psP", [P, S], BF16)
        psO = (psO, psO1)
        (weights, made, parted, copied, picked, gathered, turned, got, gotT, gotW, inner, silu, hidden, down, scaled, scattered,
         added, split) = (ph.sem(x) for x in ("weights", "made", "parted", "copied", "picked", "gathered", "turned", "got", "gotT", "gotW",
            "inner", "silu", "hidden", "down", "scaled", "scattered", "added", "split"))
        nm = Norm(ph, "n", None, used=(split, 4))

        def items(eng, item):
            with eng.Fori(0, B // 2 - 1) as i:
                for m in range(2 * E):
                    item(i, m, False)
            for m in range(2 * E):
                item(B // 2 - 1, m, m == 2 * E - 1)

        with ph.start() as block:
            @block.sync
            def _(sp):
                for dst, x in ((w_gate, "L1f_gate"), (w_up, "L1f_up")):
                    sp.dma_start(dst[:, :, :], aps[x]).then_inc(weights, 16)
                sp.dma_start(w_down[:, :, :, :], aps["L1f_down"]).then_inc(weights, 16)

            @block.tensor
            def _(pe):
                def gather(i, m):
                    n, e, x = 2 * E * i + m, m % E, m // E % 2
                    g = pick[:, m % 2, :, :]
                    pe.wait_ge(picked, BASE + n + 1)
                    if e == 0:
                        pe.wait_ge(split, BASE + 4 * (2 * i + m // E) + 4)
                    pe.wait_ge(got, BASE + n)
                    for j in range(NT):
                        for part in range(3):
                            mm = pe.matmul(psX[:, 0:P], xn3[:, x, j, part, :], g[:, j, :], start=j == 0 and part == 0,
                                           stop=j == NT - 1 and part == 2)
                    mm.then_inc(gathered, 1)
                    pe.wait_ge(gotW, BASE + n)
                    pe.wait_ge(gotT, BASE + n)
                    for j in range(NT):
                        pe.matmul(psW[:, 0:3], g[:, j, :], af3[:, j, bass.ds(n, 1), :].rearrange("p o c -> p (o c)"),
                                  start=j == 0, stop=j == NT - 1)
                    for j in range(NT):
                        mm = pe.transpose(psP[:, j * P:(j + 1) * P], g[:, j, :], net.idb[:, :])
                    mm.then_inc(turned, 1)

                def up(i, m):
                    n, e = 2 * E * i + m, m % E
                    pe.wait_ge(got, BASE + n + 1)
                    pe.wait_ge(hidden, BASE + n)
                    for ps, w in ((psG, w_gate), (psU, w_up)):
                        for t in range(FT):
                            mm = pe.matmul(ps[:, t * P:(t + 1) * P], w[:, e, t * P:(t + 1) * P], xg[:, :], start=True, stop=True)
                        mm.then_inc(inner, 1)

                def project(i, m):
                    n, e = 2 * E * i + m, m % E
                    pe.wait_ge(hidden, BASE + n + 1)
                    pe.wait_ge(scaled, BASE + n)
                    for t in range(FT):
                        mm = pe.matmul(psD[:, 0:D], hid[:, t * P:(t + 1) * P], w_down[:, e, t, :], start=t == 0, stop=t == FT - 1)
                    mm.then_inc(down, 1)

                def scatter(i, m):
                    n, e = 2 * E * i + m, m % E
                    pe.wait_ge(scaled, BASE + n + 1)
                    pe.wait_ge(gotT, BASE + n + 1)
                    if e == 0:
                        pe.wait_ge(added, BASE + 2 * i + m // E - 1)
                    out = psO[m // E]
                    for j in range(NT):
                        mm = pe.matmul(out[:, j * P:(j + 1) * P], pickT[:, m % 2, j * P:(j + 1) * P], y[:, :],
                                       start=e == 0 and j == 0, stop=e == E - 1 and j == NT - 1, skip_group_check=True)
                    mm.then_inc(scattered, 1)

                def item(i, m, last):
                    if not last:
                        gather(i, m + 1)
                    project(i, m)
                    if not last:
                        up(i, m + 1)
                    scatter(i, m)

                pe.wait_ge(parted, BASE + 4)
                gather(0, 0)
                pe.wait_ge(weights, BASE + 48)
                up(0, 0)
                items(pe, item)

            @block.scalar
            def _(a):
                def tokens(i, m):
                    n = 2 * E * i + m
                    a.wait_ge(gathered, BASE + n + 1)
                    a.wait_ge(inner, BASE + 2 * n)
                    a.copy(xg[:, :], psX[:, 0:P]).then_inc(got, 1)

                def item(i, m, last):
                    n = 2 * E * i + m
                    a.wait_ge(inner, BASE + 2 * n + 1)
                    a.wait_ge(hidden, BASE + n)
                    a.activation(act_[:, :], psG[:, :], ACT.Silu).then_inc(silu, 1)
                    if not last:
                        tokens(i, m + 1)

                tokens(0, 0)
                items(a, item)

            @block.vector
            def _(v):
                def parts(b, x, first=False):
                    full = lambda p: xn3[:, x, :, p, :]
                    v.wait_ge(nm.normed, BASE + NT * b + NT)
                    if not first:
                        v.wait_ge(gathered, BASE + E * (b - 1))
                    v.tensor_copy(full(0), nm.xn[:, :, :]).then_inc(split, 1)
                    v.wait_ge(split, BASE + 4 * b + 1)
                    v.tensor_tensor(xr[:, :, :], nm.xn[:, :, :], full(0), ALU.subtract).then_inc(split, 1)

                def rests(b, x):
                    full = lambda p: xn3[:, x, :, p, :]
                    v.wait_ge(split, BASE + 4 * b + 2)
                    v.tensor_copy(full(1), xr[:, :, :]).then_inc(split, 1)
                    v.wait_ge(split, BASE + 4 * b + 3)
                    v.tensor_tensor(full(2), xr[:, :, :], full(1), ALU.subtract).then_inc(split, 1)

                def picks(i, m):
                    n = 2 * E * i + m
                    v.wait_ge(turned, BASE + n + 1)
                    v.wait_ge(scattered, BASE + n - 1)
                    v.tensor_copy(pickT[:, m % 2, :], psP[:, :]).then_inc(gotT, 1)
                    v.wait_ge(scaled, BASE + n - 1)
                    v.reduce_sum(weight[:, m % 2:m % 2 + 1], psW[:, 0:3], AX).then_inc(gotW, 1)

                def item(i, m, last):
                    n, e, b = 2 * E * i + m, m % E, 2 * i + m // E
                    more = not last and (not isinstance(i, int) or b + 1 < B)
                    v.wait_ge(silu, BASE + n + 1)
                    v.wait_ge(inner, BASE + 2 * n + 2)
                    v.wait_ge(down, BASE + n)
                    v.tensor_tensor(hid[:, :], act_[:, :], psU[:, :], ALU.mult).then_inc(hidden, 1)
                    if not last:
                        picks(i, m + 1)
                    v.wait_ge(down, BASE + n + 1)
                    v.wait_ge(gotW, BASE + n + 1)
                    v.wait_ge(scattered, BASE + n)
                    v.tensor_scalar(y[:, :], psD[:, 0:D], weight[:, m % 2:m % 2 + 1], None, ALU.mult).then_inc(scaled, 1)
                    if more and e == 1:
                        nm.stats(v, b + 1)
                    if more and e == 3:
                        nm.norm(v, b + 1)
                    if more and e == 4:
                        parts(b + 1, (m // E + 1) % 2)
                    if more and e == 5:
                        rests(b + 1, (m // E + 1) % 2)
                    if e == E - 1:
                        v.wait_ge(scattered, BASE + n + 1)
                        tiles = net.X[:, bass.ds(b * NT, NT), :]
                        v.tensor_tensor(tiles, tiles, psO[m // E][:, :].rearrange("p (j d) -> p j d", j=NT), ALU.add).then_inc(added, 1)

                v.tensor_copy(af3[:, :, :, 0], net.aff[:, :, :]).then_inc(parted, 1)
                v.wait_ge(parted, BASE + 1)
                v.tensor_tensor(afr[:, :, :], net.aff[:, :, :], af3[:, :, :, 0], ALU.subtract).then_inc(parted, 1)
                v.wait_ge(parted, BASE + 2)
                v.tensor_copy(af3[:, :, :, 1], afr[:, :, :]).then_inc(parted, 1)
                v.wait_ge(parted, BASE + 3)
                v.tensor_tensor(af3[:, :, :, 2], afr[:, :, :], af3[:, :, :, 1], ALU.subtract).then_inc(parted, 1)
                nm.stats(v, 0)
                nm.norm(v, 0)
                parts(0, 0, first=True)
                rests(0, 0)
                picks(0, 0)
                items(v, item)

            @block.gpsimd
            def _(g):
                g.iota(iota[:, :], pattern=[[1, P]], base=0, channel_multiplier=0,
                       allow_small_or_imprecise_dtypes=True).then_inc(made, 1)
                g.wait_ge(made, BASE + 1)
                with g.Fori(0, B // 2) as i:
                    for x in range(2):
                        b = 2 * i + x
                        nm.power(g, b)
                        g.tensor_copy(slot[:, x, :, :], net.slot[:, :, bass.ds(b * E, E)]).then_inc(copied, 1)
                        g.wait_ge(copied, BASE + b + 1)
                        for e in range(E):
                            n = E * b + e
                            waited(net, g, (turned, n - 1))
                            for j in range(NT):
                                m = g.tensor_scalar(pick[:, e % 2, j, :], iota[:, :], slot[:, x, j, e:e + 1], None, ALU.is_equal)
                            m.then_inc(picked, 1)


def dump(net, out, what):
    nc = net.nc
    with Phase(net, "dump") as ph:
        done = ph.sem("done")
        with ph.start() as block:
            @block.sync
            def _(sp):
                sp.dma_start(out.rearrange("b (j p) d -> p (b j) d", p=P), net.X[:, :, :]).then_inc(done, 16)
                sp.wait_ge(done, BASE + 16)


STAGES = 99
START = 0


def program(nc, aps, out):
    run = lambda n: START < n <= STAGES
    with ExitStack() as ctx:
        net = Net(nc, aps, ctx)
        setup(net)
        if run(2):
            mla_prep(net)
            heads_t(net, "mh", DH + DR, net.QM, net.KM, 80.0, float(1.0 / np.sqrt(np.float32(DH + DR))))
            moe_top2(net, "m1", (aps["L0_attn_a_W_O"],))
        if run(3):
            with net.nc.sbuf_tensor("far_keys", [P, 2], F32) as keep:
                relative_tables(net, keep)
                relative_prep(net, keep)
            heads_relative(net, "rh", float(1.0 / np.sqrt(np.float32(DH * 3))))
            if STAGES > 3:
                moe_top2(net, "m2", (aps["L0b_WoT"], aps["L0_attn_b_bo"]))
        if run(5):
            linear_prep(net)
            heads_t(net, "lh", DH, net.QS, net.KS, None, None)
            expert_affinity(net, "lo", (aps["L1a_WoT"], aps["L1_attn_a_bo"], 1e-6))
            expert_choice(net, "lc")
            expert_ffn(net, "lf")
        if run(7):
            rotary_prep(net)
            heads_max(net, "yh", float(1.0 / np.sqrt(np.float32(DH))))
            expert_affinity(net, "yo", (aps["L1b_WoT"], aps["L1_attn_b_out_b"]))
            expert_choice(net, "yc")
            expert_ffn(net, "yf")
        dump(net, out, "X")


def rotary_mla():
    inv = np.float32(10000.0) ** (-np.arange(0, DR, 2, dtype=np.float32) / np.float32(DR))
    ang = (np.arange(S, dtype=np.float32)[:, None] * inv.astype(np.float32)).astype(np.float64)
    cos, sin = np.cos(ang).T, np.sin(ang).T
    c4 = np.repeat(cos, 2, 0)
    s4 = np.stack([-sin, sin], 1).reshape(DR, S)
    rot = np.zeros((P, S), np.float32)
    rot[:H * DR] = np.tile(c4, (H, 1))
    rot[H * DR:] = np.tile(s4, (H, 1))
    return rot


def rotary_full():
    i = np.arange(D // 2, dtype=np.float32)
    theta = (np.float32(10000.0) ** (np.float32(-2.0) * (i - np.float32(1.0)) / np.float32(D))).astype(np.float32)
    ang = (np.arange(S, dtype=np.float32)[:, None] * theta[None, :]).astype(np.float64)
    cos, sin = np.cos(ang).T, np.sin(ang).T
    return np.stack([np.repeat(cos, 2, 0), np.stack([sin, -sin], 1).reshape(D, S)], 1).astype(np.float32)


def host_layout(inputs):
    a = {k: np.ascontiguousarray(v) for k, v in inputs.items()}
    out = dict(a)
    swap = lambda w: np.ascontiguousarray(w.reshape(w.shape[0], -1, 2)[:, :, ::-1].reshape(w.shape))
    down = np.zeros((D, P), a["L0_attn_a_W_DQ"].dtype)
    down[:, 0:DL] = a["L0_attn_a_W_DQ"]
    down[:, DL:2 * DL] = a["L0_attn_a_W_DKV"]
    down[:, 2 * DL:2 * DL + DR] = a["L0_attn_a_W_KR"]
    down[:, 3 * DL:3 * DL + DR] = swap(a["L0_attn_a_W_KR"])
    out["mla_down"] = down
    out["mla_qr"] = np.concatenate([a["L0_attn_a_W_QR"], swap(a["L0_attn_a_W_QR"])], 1)
    out["mla_rot"] = rotary_mla()
    turned = lambda w: np.ascontiguousarray(w.T)
    for x in "qkvo":
        out[f"L0b_W{x}T"] = turned(a[f"L0_attn_b_W{x}"])
        out[f"L1a_W{x}T"] = turned(a[f"L1_attn_a_W{x}"])
    for x in "kq":
        out[f"L0b_Wp{x}T"] = turned(a[f"L0_attn_b_Wp{x}"])
    each = [turned(a[f"L1_attn_b_w{x}"]) for x in "qkv"]
    out["L1b_w"] = np.ascontiguousarray(np.stack([y for w in each for y in (w, swap(w))], 1))
    out["L1b_in"] = np.ascontiguousarray(np.stack([turned(w) for w in np.split(a["L1_attn_b_in_proj_w"], 3, 0)], 1))
    out["L1b_rot"] = rotary_full()
    out["L1b_WoT"] = turned(a["L1_attn_b_out_w"])
    out["relT"] = turned(a["L0_attn_b_rel_emb"])
    out["relT_reversed"] = turned(a["L0_attn_b_rel_emb"][::-1])
    out["WeT"] = np.ascontiguousarray(a["L0_ffn_We"].transpose(2, 0, 1).reshape(D, E * D))
    out["L1f_gateT"] = turned(a["L1_ffn_gate_w"])
    for x in ("gate", "up"):
        out[f"L1f_{x}"] = np.ascontiguousarray(a[f"L1_ffn_w_{x}"].transpose(2, 0, 1))
    down = a["L1_ffn_w_down"].reshape(E, D, FI // P, P)
    out["L1f_down"] = np.ascontiguousarray(down.transpose(3, 0, 2, 1))
    return out



def kernel(**inputs):
    import concourse.bacc as _bacc
    from concourse.bass_utils import run_bass_kernel_spmd as _run

    nc = _bacc.Bacc("TRN2", target_bir_lowering=False, num_devices=1)
    arrays, aps = {}, {}
    for name, a in host_layout(inputs).items():
        arrays[f"in_{name}"] = a
        aps[name] = nc.dram_tensor(f"in_{name}", a.shape, mybir.dt.from_np(a.dtype), kind="ExternalInput").ap()
    out = nc.dram_tensor("out", (B, S, D), F32, kind="ExternalOutput").ap()
    program(nc, aps, out)
    r = _run(nc, [arrays], core_ids=[0])
    return r.results[0]["out"]
```

```python
from contextlib import ExitStack

import numpy as np

import concourse.bass as bass
from concourse import mybir

F32 = mybir.dt.float32
BF16 = mybir.dt.bfloat16
ALU = mybir.AluOpType
ACT = mybir.ActivationFunctionType
AX = mybir.AxisListType.X

P = 128
B, S, D = 8, 512, 128
NT = S // P
H, DH = 16, 8
DR, DL = 4, 32
E = 8
FI = 512
KTOP = S // E * 2
REL = 64
LPART = (0, 0, 0, 1, 1, 2)
RPART = (0, 1, 2, 0, 1, 0)
NC6 = len(LPART)
RUNS = ((0, 3), (3, 5), (5, 6))
BASE = 16
LN_EPS = 1e-5
FAR = S - 3 * REL
EXT = 3 * P
TW = 2 * EXT + 2 * P
VW = 32


class Net:

    def __init__(self, nc, aps, ctx):
        self.nc, self.aps, self.ctx = nc, aps, ctx
        sb = lambda name, shape, dt=F32: ctx.enter_context(nc.sbuf_tensor(name, shape, dt))
        self.X = sb("X", [P, B * NT, D])
        self.V = sb("V", [P, B * H, NT, DH])
        self.idf = sb("idf", [P, P])
        self.idb = sb("idb", [P, P], BF16)
        self.half = sb("half", [P, NT])
        self.ones = sb("ones", [1, S])
        self.constants = ctx.enter_context(nc.semaphore("constants"))
        self.carrier = ctx.enter_context(nc.semaphore("carrier"))
        scratch = lambda name, shape, dt: nc.dram_tensor(name, shape, dt, kind="Internal").ap()
        self.QS = scratch("QS", (B * H, NC6 * DH, S), BF16)
        self.KS = scratch("KS", (B * H, NC6 * DH, S), BF16)
        self.QM = scratch("QM", (B * H, NC6 * (DH + DR), S), BF16)
        self.KM = scratch("KM", (B * H, NC6 * (DH + DR), S), BF16)
        self.KLS = scratch("KLS", (B * H, NC6 * DH, FAR), BF16)
        self.KHS = scratch("KHS", (B * H, NC6 * DH, FAR), BF16)
        self.TB = scratch("TB", (H, NC6 * DH, TW), BF16)
        self.aff = sb("aff", [P, NT, B * E])
        self.slot = sb("slot", [P, NT, B * E])
        self.CU = scratch("CU", (B * H, DH + 1, S), F32)
        self.RD = scratch("RD", (B * H, S), F32)


class Phase:

    def __init__(self, net, tag):
        self.net, self.nc, self.tag, self.ctx, self.sems = net, net.nc, tag, ExitStack(), []

    def __enter__(self):
        return self

    def __exit__(self, *a):
        if a[0] is None:
            for s in self.sems:
                self.nc.gpsimd.sem_clear(s)
            self.nc.all_engine_barrier()
        self.ctx.close()

    def start(self):
        engines = (self.nc.gpsimd, self.nc.vector, self.nc.scalar, self.nc.tensor, self.nc.sync)
        for i, s in enumerate(self.sems):
            engines[i % len(engines)].sem_inc(s, BASE)
        self.nc.all_engine_barrier()
        return self.nc.Block()

    def sb(self, name, shape, dt=F32):
        return self.ctx.enter_context(self.nc.sbuf_tensor(f"{self.tag}_{name}", shape, dt))

    def ps(self, name, shape, dt=F32):
        return self.ctx.enter_context(self.nc.psum_tensor(f"{self.tag}_{name}", shape, dt))

    def sem(self, name):
        s = self.ctx.enter_context(self.nc.semaphore(f"{self.tag}_{name}"))
        self.sems.append(s)
        return s


def waited(net, eng, *waits):
    for sem, value in waits:
        eng.wait_ge(sem, BASE + value)
    eng.sem_inc(net.carrier, 1)


def over(ap, dim, n):
    shape = list(ap.shape)
    shape.insert(dim, n)
    return ap.unsqueeze(dim).broadcast_to(shape)


def setup(net):
    nc = net.nc
    with Phase(net, "setup") as ph:
        loaded, made = ph.sem("loaded"), ph.sem("made")
        with ph.start() as block:
            @block.sync
            def _(sp):
                sp.dma_start(net.X[:, :, :], net.aps["L0_attn_a_x"].rearrange("b (j p) d -> p (b j) d", p=P)).then_inc(loaded, 16)
                sp.wait_ge(loaded, BASE + 16)

            @block.vector
            def _(v):
                v.memset(net.half[:, :], -0.5)
                v.memset(net.ones[:, :], 1.0)

            @block.gpsimd
            def _(g):
                g.memset(net.idf[:, :], 0.0).then_inc(made, 1)
                g.wait_ge(made, BASE + 1)
                g.affine_select(out=net.idf[:, :], in_=net.idf[:, :], compare_op=ALU.not_equal, fill=1.0, base=0,
                                pattern=[[-1, P]], channel_multiplier=1).then_inc(made, 1)
                g.wait_ge(made, BASE + 2)
                g.tensor_copy(net.idb[:, :], net.idf[:, :]).then_inc(net.constants, 1)


class Norm:

    def __init__(self, ph, tag, psT, used=None):
        self.net, self.psT = ph.net, psT
        self.xn = ph.sb(tag + "xn", [P, NT, D])
        self.xT = ph.sb(tag + "xT", [P, S])
        self.st = ph.sb(tag + "st", [P, NT, 6])
        self.mv = ph.sb(tag + "mv", [P, NT, 2])
        self.ve = ph.sb(tag + "ve", [P, NT])
        self.rs = ph.sb(tag + "rs", [P, NT])
        s = lambda n: ph.sem(tag + n)
        self.stats_, self.moments, self.shifted, self.inverse = s("stats"), s("moments"), s("shifted"), s("inverse")
        self.normed, self.turned, self.ready = s("normed"), s("turned"), s("ready")
        self.used = used or (self.turned, 1)

    def tile(self, b, j):
        return self.net.X[:, bass.ds(b * NT + j, 1), :].rearrange("p o d -> p (o d)")

    def stats(self, v, b):
        waited(self.net, v, (self.inverse, b))
        for j in range(NT):
            v.bn_stats(self.st[:, j, :], self.tile(b, j)).then_inc(self.stats_, 1)
        waited(self.net, v, (self.stats_, NT * b + NT))
        for j in range(NT):
            v.bn_aggr(self.mv[:, j, :], self.st[:, j, :]).then_inc(self.moments, 1)

    def power(self, g, b):
        waited(self.net, g, (self.moments, NT * b + NT))
        g.tensor_scalar(self.ve[:, :], self.mv[:, :, 1], LN_EPS, None, ALU.add).then_inc(self.shifted, 1)
        g.wait_ge(self.shifted, BASE + b + 1)
        g.wait_ge(self.normed, BASE + NT * b)
        g.tensor_tensor(self.rs[:, :], self.ve[:, :], self.net.half[:, :], ALU.pow).then_inc(self.inverse, 1)

    def norm(self, v, b):
        v.wait_ge(self.inverse, BASE + b + 1)
        v.wait_ge(self.used[0], BASE + self.used[1] * b)
        for j in range(NT):
            v.tensor_scalar(self.xn[:, j, :], self.tile(b, j), self.mv[:, j, 0:1], self.rs[:, j:j + 1],
                            ALU.subtract, ALU.mult).then_inc(self.normed, 1)

    def turn(self, pe, b):
        pe.wait_ge(self.normed, BASE + NT * b + NT)
        pe.wait_ge(self.ready, BASE + b)
        for j in range(NT):
            t = pe.transpose(self.psT[:, j * P:(j + 1) * P], self.xn[:, j, :], self.net.idf[:, :])
        t.then_inc(self.turned, 1)

    def keep(self, a, b, free):
        a.wait_ge(self.turned, BASE + b + 1)
        a.wait_ge(free[0], BASE + free[1])
        a.copy(self.xT[:, :], self.psT[:, :]).then_inc(self.ready, 1)


def batches(eng, before, body):
    before()
    with eng.Fori(0, B - 1) as b:
        body(b, True)
    body(B - 1, False)


def batch_pairs(eng, before, body):
    before()
    with eng.Fori(0, B // 2 - 1) as i:
        for x in range(2):
            body(2 * i + x, True, x)
    body(B - 2, True, 0)
    body(B - 1, False, 1)


class Split:

    def __init__(self, ph, tag, n, src, cols=S, bias=None, dmas=len(RUNS)):
        self.net, self.n, self.src, self.bias, self.dmas = ph.net, n, src, bias, dmas
        self.part = ph.sb(tag + "part", [n, 2, 3, cols], BF16)
        self.r1 = ph.sb(tag + "r1", [n, cols])
        self.first, self.rest, self.second, self.third = (ph.sem(tag + x) for x in ("first", "rest", "second", "third"))
        self.kept = [ph.sem(f"{tag}kept{x}") for x in range(2)]

    def act(self, a, b, x, have):
        a.wait_ge(have[0], BASE + have[1])
        a.wait_ge(self.kept[x], BASE + 8 * self.dmas * (b - x))
        if self.bias is None:
            a.copy(self.part[:, x, 0, :], self.src).then_inc(self.first, 1)
        else:
            a.activation(self.part[:, x, 0, :], self.src, ACT.Identity, bias=self.bias).then_inc(self.first, 1)

    def dve(self, v, b, x):
        v.wait_ge(self.first, BASE + b + 1)
        v.wait_ge(self.third, BASE + b)
        if self.bias is None:
            v.tensor_tensor(self.r1[:, :], self.src, self.part[:, x, 0, :], ALU.subtract).then_inc(self.rest, 1)
        else:
            v.scalar_tensor_tensor(self.r1[:, :], self.src, self.bias, self.part[:, x, 0, :], ALU.add, ALU.subtract)\
                .then_inc(self.rest, 1)

    def act_second(self, a, b, x):
        a.wait_ge(self.rest, BASE + b + 1)
        a.copy(self.part[:, x, 1, :], self.r1[:, :]).then_inc(self.second, 1)

    def pool(self, g, b, x):
        g.wait_ge(self.second, BASE + b + 1)
        g.tensor_tensor(self.part[:, x, 2, :], self.r1[:, :], self.part[:, x, 1, :], ALU.subtract).then_inc(self.third, 1)

    def store(self, sp, b, x, dst, left, at=0, shared=False):
        sp.wait_ge(self.third, BASE + b + 1)
        part = self.part[:, x, :, :]
        per = self.n if shared else self.n // H
        copies = dst[bass.ds(b * H, H), :, :].rearrange("h (w c) s -> h w c s", c=NC6)[:, at:at + per, :, :]
        for i, (lo, hi) in enumerate(RUNS):
            if left and self.dmas == len(RUNS):
                src = over(part[:, i, :], 1, hi - lo)
                sp.dma_start(copies[:, :, lo:hi, :].rearrange("h r c s -> (h r) c s"), src).then_inc(self.kept[x], 16)
            elif left:
                for c in range(lo, hi):
                    sp.dma_start(copies[:, :, c, :], part[:, i, :]).then_inc(self.kept[x], 16)
            else:
                rows, src = copies[:, :, lo:hi, :].rearrange("h r c s -> h r (c s)"), part[:, 0:hi - lo, :].rearrange("p c s -> p (c s)")
                if shared:
                    rows, src = rows.rearrange("h r x -> r h x"), over(src, 1, H)
                sp.dma_start(rows, src).then_inc(self.kept[x], 16)

    def end(self, sp):
        for x in range(2):
            sp.wait_ge(self.kept[x], BASE + 8 * self.dmas * B)


def mla_prep(net):
    nc, aps = net.nc, net.aps
    WD = DH + DR
    with Phase(net, "ma") as ph:
        w_down = ph.sb("w_down", [P, P])
        w_q = ph.sb("w_q", [DL, H * DH])
        w_qr = ph.sb("w_qr", [DL, 2 * H * DR])
        w_kv = ph.sb("w_kv", [2 * DL, 2 * H * DH])
        rot = ph.sb("rot", [P, S])
        lat = ph.sb("lat", [P, S])
        a1 = ph.sb("a1", [H * DR, S])
        a2 = ph.sb("a2", [H * DR, S])
        b1 = ph.sb("b1", [DR, S])
        b2 = ph.sb("b2", [DR, S])
        qr = ph.sb("qr", [H * DR, S])
        kr = ph.sb("kr", [DR, S])
        psT, psD, psQ, psR, psK, psV = (ph.ps(n, [P, S]) for n in ("psT", "psD", "psQ", "psR", "psK", "psV"))
        nm = Norm(ph, "n", psT)
        sq = Split(ph, "q", P, psQ[:, :], dmas=NC6)
        sk = Split(ph, "k", P, psK[:, :])
        sqr = Split(ph, "qr", H * DR, qr[:, :], dmas=NC6)
        skr = Split(ph, "kr", DR, kr[:, :])
        weights = ph.sem("weights")
        down, latent, up, rq, rqs, rk, rks, vals = (ph.sem(x) for x in
            ("down", "latent", "up", "rq", "rqs", "rk", "rks", "vals"))
        with ph.start() as block:
            @block.sync
            def _(sp):
                sp.dma_start(w_down[:, :], aps["mla_down"]).then_inc(weights, 16)
                sp.dma_start(w_q[:, :], aps["L0_attn_a_W_UQ"]).then_inc(weights, 16)
                sp.dma_start(w_qr[:, :], aps["mla_qr"]).then_inc(weights, 16)
                sp.dma_start(w_kv[DL:2 * DL, 0:H * DH], aps["L0_attn_a_W_UK"]).then_inc(weights, 16)
                sp.dma_start(w_kv[DL:2 * DL, H * DH:], aps["L0_attn_a_W_UV"]).then_inc(weights, 16)
                sp.dma_start(rot[:, :], aps["mla_rot"]).then_inc(weights, 16)
                with sp.Fori(0, B // 2) as i:
                    for x in range(2):
                        sq.store(sp, 2 * i + x, x, net.QM, True)
                        sk.store(sp, 2 * i + x, x, net.KM, False)
                        skr.store(sp, 2 * i + x, x, net.KM, False, DH, shared=True)
                        sqr.store(sp, 2 * i + x, x, net.QM, True, DH)
                for s in (sq, sk, sqr, skr):
                    s.end(sp)

            @block.tensor
            def _(pe):
                pe.wait_ge(weights, BASE + 16 * 6)

                def body(b, more, x):
                    pe.wait_ge(nm.ready, BASE + b + 1)
                    pe.wait_ge(latent, BASE + b)
                    pe.wait_ge(rk, BASE + 2 * b)
                    pe.matmul(psD[:, :], w_down[:, :], nm.xT[:, :], start=True, stop=True).then_inc(down, 1)
                    if more:
                        nm.turn(pe, b + 1)
                    pe.wait_ge(latent, BASE + b + 1)
                    pe.wait_ge(rq, BASE + 2 * b)
                    pe.matmul(psR[:, :], w_qr[:, :], lat[0:DL, :], start=True, stop=True).then_inc(up, 1)
                    pe.wait_ge(sq.rest, BASE + b)
                    pe.matmul(psQ[:, :], w_q[:, :], lat[0:DL, :], start=True, stop=True).then_inc(up, 1)
                    pe.wait_ge(sk.rest, BASE + b)
                    pe.matmul(psK[:, :], w_kv[DL:2 * DL, 0:P], lat[DL:2 * DL, :], start=True, stop=True).then_inc(up, 1)
                    pe.wait_ge(vals, BASE + b)
                    for j in range(NT):
                        m = pe.matmul(psV[:, j * P:(j + 1) * P], lat[DL:2 * DL, j * P:(j + 1) * P],
                                      w_kv[DL:2 * DL, P:], start=True, stop=True)
                    m.then_inc(up, 1)

                batch_pairs(pe, lambda: nm.turn(pe, 0), body)

            @block.scalar
            def _(a):
                def body(b, more, x):
                    a.wait_ge(down, BASE + b + 1)
                    a.wait_ge(up, BASE + 4 * b)
                    a.copy(lat[0:2 * DL, :], psD[0:2 * DL, :]).then_inc(latent, 1)
                    skr.act(a, b, x, (rks, b + 1))
                    if more:
                        nm.keep(a, b + 1, (down, b + 1))
                    sq.act(a, b, x, (up, 4 * b + 2))
                    sk.act(a, b, x, (up, 4 * b + 3))
                    sq.act_second(a, b, x)
                    sqr.act(a, b, x, (rqs, b + 1))
                    sk.act_second(a, b, x)
                    skr.act_second(a, b, x)
                    sqr.act_second(a, b, x)
                    a.wait_ge(up, BASE + 4 * b + 4)
                    values_out(net, a, psV, b).then_inc(vals, 1)

                batch_pairs(a, lambda: nm.keep(a, 0, (down, 0)), body)

            @block.vector
            def _(v):
                v.wait_ge(weights, BASE + 16 * 6)

                def before():
                    nm.stats(v, 0)
                    nm.norm(v, 0)

                def body(b, more, x):
                    if more:
                        nm.stats(v, b + 1)
                    v.wait_ge(down, BASE + b + 1)
                    v.wait_ge(rks, BASE + b)
                    v.tensor_tensor(b1[:, :], psD[2 * DL:2 * DL + DR, :], rot[0:DR, :], ALU.mult).then_inc(rk, 1)
                    v.tensor_tensor(b2[:, :], psD[3 * DL:3 * DL + DR, :], rot[H * DR:H * DR + DR, :], ALU.mult).then_inc(rk, 1)
                    v.wait_ge(rk, BASE + 2 * b + 2)
                    v.wait_ge(skr.rest, BASE + b)
                    v.tensor_tensor(kr[:, :], b1[:, :], b2[:, :], ALU.add).then_inc(rks, 1)
                    skr.dve(v, b, x)
                    if more:
                        nm.norm(v, b + 1)
                    v.wait_ge(up, BASE + 4 * b + 1)
                    v.wait_ge(rqs, BASE + b)
                    v.tensor_tensor(a1[:, :], psR[0:H * DR, :], rot[0:H * DR, :], ALU.mult).then_inc(rq, 1)
                    v.tensor_tensor(a2[:, :], psR[H * DR:, :], rot[H * DR:, :], ALU.mult).then_inc(rq, 1)
                    v.wait_ge(rq, BASE + 2 * b + 2)
                    v.wait_ge(sqr.rest, BASE + b)
                    v.tensor_tensor(qr[:, :], a1[:, :], a2[:, :], ALU.add).then_inc(rqs, 1)
                    sq.dve(v, b, x)
                    sk.dve(v, b, x)
                    sqr.dve(v, b, x)

                batch_pairs(v, before, body)

            @block.gpsimd
            def _(g):
                def body(b, more, x):
                    if more:
                        nm.power(g, b + 1)
                    for s in (skr, sq, sk, sqr):
                        s.pool(g, b, x)

                batch_pairs(g, lambda: nm.power(g, 0), body)


U = 4
UT = 8
R = 4
AHEAD = 3


DIAG = (0, 512, 1024, 896)
CAUSAL = 1280
QDIAG = (896, 1024, 512, 0)


class HeadLoads:

    def __init__(self, ph, rows, queries, keys):
        self.net, self.rows, self.queries, self.keys = ph.net, rows, queries, keys
        self.q = ph.sb("q", [rows, R, S], BF16)
        self.k = ph.sb("k", [rows, R, S], BF16)
        self.v1 = ph.sb("v1", [P, R, NT, VW])
        self.o = ph.sb("o", [P, UT // R, S])
        self.po = [ph.ps(f"po{i}", [P, S]) for i in range(UT // R)]
        self.loaded = [ph.sem(f"loaded{r}") for r in range(R)]
        self.stored = [ph.sem(f"stored{i}") for i in range(UT // R)]
        self.made, self.valued, self.copied = ph.sem("made"), ph.sem("valued"), ph.sem("copied")

    def sync(self, sp, scored):
        turns = B * H // UT

        def store(i, x):
            sp.wait_ge(self.copied, BASE + UT // R * i + x + 1)
            for r in range(R):
                sp.dma_start(self.net.CU[bass.ds(UT * i + R * x + r, 1), :, :], self.o[VW * r:VW * r + DH + 1, x, :])\
                    .then_inc(self.stored[x], 16)

        def turn(i, before):
            for u in range(UT):
                n, r = UT * i + u, u % R
                if before is not None or u >= R:
                    sp.wait_ge(scored, BASE + n - R + 1)
                sp.dma_start(self.q[:, r, :], self.queries[bass.ds(n, 1), :, :]).then_inc(self.loaded[r], 16)
                sp.dma_start(self.k[:, r, :], self.keys[bass.ds(n, 1), :, :]).then_inc(self.loaded[r], 16)
                if r == R - 1 and before is not None:
                    store(before, u // R)

        turn(0, None)
        with sp.Fori(0, turns - 1) as i:
            turn(i + 1, i)
        for x in range(UT // R):
            store(turns - 1, x)
        for s in self.stored:
            sp.wait_ge(s, BASE + 16 * R * turns)

    def wait_loaded(self, pe, i, u):
        pe.wait_ge(self.loaded[u % R], BASE + 32 * (UT // R * i + u // R + 1))

    def pool_start(self, g):
        g.memset(self.v1[:, :, :, :], 0.0).then_inc(self.made, 1)
        g.wait_ge(self.made, BASE + 1)
        g.memset(self.v1[:, :, :, DH:2 * DH], 1.0).then_inc(self.made, 1)
        g.wait_ge(self.made, BASE + 2)

    def pool_values(self, g, n, u, summed):
        waited(self.net, g, (summed, n - R + 1))
        g.tensor_copy(self.v1[:, u % R, :, 0:DH], self.net.V[:, bass.ds(n, 1), :, :].rearrange("p o j d -> p (o j) d"))\
            .then_inc(self.valued, 1)

    def context(self, pe, i, u, n, w, ready, summed):
        pe.wait_ge(self.valued, BASE + n + 1)
        if u % R == 0:
            pe.wait_ge(self.copied, BASE + UT // R * i + u // R - 1)
        at = VW * (u % R)
        for J in range(NT):
            pe.wait_ge(ready[J][0], BASE + ready[J][1])
            m = pe.matmul(self.po[u // R][at:at + VW, J * P:], self.v1[:, u % R, J, :],
                          w[:, DIAG[J]:DIAG[J] + S - J * P], start=J == 0, stop=J == NT - 1)
        m.then_inc(summed, 1)

    def act_copy(self, a, i, x, summed):
        a.wait_ge(summed, BASE + UT * i + R * (x + 1))
        a.wait_ge(self.stored[x], BASE + 16 * R * i)
        a.copy(self.o[:, x, :], self.po[x][:, :]).then_inc(self.copied, 1)

    def act(self, a, item, summed, after=None):
        turns = B * H // UT

        def turn(i, before):
            for u in range(UT):
                item(u, UT * i + u)
                if after and (u or before is not None):
                    after((u - 1) % UT, UT * i + u - 1)
                if u % R == 1 and (u > R or before is not None):
                    self.act_copy(a, i if u > R else before, 0 if u > R else UT // R - 1, summed)

        turn(0, None)
        with a.Fori(0, turns - 1) as i:
            turn(i + 1, i)
        if after:
            after(UT - 1, UT * turns - 1)
        self.act_copy(a, turns - 1, UT // R - 1, summed)


def heads_t(net, tag, width, queries, keys, clip, scale):
    nc = net.nc
    N = B * H
    with Phase(net, tag) as ph:
        hl = HeadLoads(ph, NC6 * width, queries, keys)
        c = ph.sb("c", [P, R, CAUSAL])
        w = ph.sb("w", [P, R, 3 * S])
        w3 = w[:, :, :].rearrange("p r (x s) -> p r x s", x=3)
        sc = [ph.ps(f"sc{i}", [P, 3 * S]) for i in range(2)]
        scored, clipped, weighed, masked, summed = (ph.sem(x) for x in ("scored", "clipped", "weighed", "masked", "summed"))
        read = weighed if clip is None else clipped
        with ph.start() as block:
            @block.sync
            def _(sp):
                hl.sync(sp, scored)

            def scores(pe, i, u, n):
                hl.wait_loaded(pe, i, u)
                pe.wait_ge(read, BASE + n - 1)
                for J in range(NT):
                    m = pe.matmul(sc[u % 2][:, DIAG[J]:DIAG[J] + S - J * P], hl.k[:, u % R, J * P:(J + 1) * P],
                                  hl.q[:, u % R, J * P:], start=True, stop=True)
                m.then_inc(scored, 1)

            @block.tensor
            def _(pe):
                def step(i, u, last):
                    t = u + AHEAD
                    if not last or t < UT:
                        scores(pe, i + t // UT, t % UT, UT * i + t)
                    hl.context(pe, i, u, UT * i + u, w[:, u % R, :], [(masked, UT * i + u + 1)] * NT, summed)

                for u in range(AHEAD):
                    scores(pe, 0, u, u)
                with pe.Fori(0, N // UT - 1) as i:
                    for u in range(UT):
                        step(i, u, False)
                for u in range(UT):
                    step(N // UT - 1, u, True)

            @block.vector
            def _(v):
                if clip is not None:
                    with v.Fori(0, N // UT) as i:
                        for u in range(UT):
                            n = UT * i + u
                            v.wait_ge(scored, BASE + n + 1)
                            v.wait_ge(weighed, BASE + n - R + 1)
                            v.tensor_scalar(c[:, u % R, :], sc[u % 2][:, 0:CAUSAL], clip, -clip, ALU.min, ALU.max)\
                                .then_inc(clipped, 1)

            @block.scalar
            def _(a):
                def item(u, n):
                    a.wait_ge(summed, BASE + n - R + 1)
                    if clip is not None:
                        a.wait_ge(clipped, BASE + n + 1)
                        a.activation(w[:, u % R, 0:CAUSAL], c[:, u % R, :], ACT.Exp, scale=scale).then_inc(weighed, 1)
                    else:
                        a.wait_ge(scored, BASE + n + 1)
                        a.copy(w[:, u % R, 0:CAUSAL], sc[u % 2][:, 0:CAUSAL]).then_inc(weighed, 1)

                hl.act(a, item, summed)

            @block.gpsimd
            def _(g):
                hl.pool_start(g)
                with g.Fori(0, N // UT) as i:
                    for u in range(UT):
                        n = UT * i + u
                        hl.pool_values(g, n, u, summed)
                        waited(net, g, (weighed, n + 1))
                        three = w3[:, u % R, :, 0:P]
                        g.affine_select(out=three, in_=three, compare_op=ALU.is_ge, fill=0.0, base=0,
                                        pattern=[[0, 3], [1, P]], channel_multiplier=-1)
                        last = w[:, u % R, DIAG[3]:DIAG[3] + P]
                        g.affine_select(out=last, in_=last, compare_op=ALU.is_ge, fill=0.0, base=0,
                                        pattern=[[1, P]], channel_multiplier=-1).then_inc(masked, 1)


class Attended:

    def __init__(self, ph, psT, psY, psG, wo, bo=None, floor=None, wg=None, hold=None):
        self.net, self.psY, self.psG, self.floor, self.hold = ph.net, psY, psG, floor, hold
        self.drams = [wo, wg] + ([bo.unsqueeze(0).broadcast_to([P, D])] if bo is not None else [])
        self.wo, self.wg, self.bo = ph.sb("wo", [P, D]), ph.sb("wg", [D, E]), ph.sb("bo", [P, D])
        self.den = ph.sb("den", [P, S])
        self.num = ph.sb("num", [P, S])
        self.inv = ph.sb("inv", [P, S])
        self.ctx = ph.sb("ctxT", [P, S])
        self.lg = ph.sb("lg", [P, B * NT, E])
        self.nm = Norm(ph, "n", psT)
        (self.w, self.dens, self.floored, self.inverted, self.kept, self.loaded, self.divided, self.out, self.added,
         self.logits, self.taken, self.held) = (ph.sem("at_" + x) for x in
            ("w", "dens", "floored", "inverted", "kept", "loaded", "divided", "out", "added", "logits", "taken", "held"))

    def sync(self, sp):
        net = self.net
        sp.dma_start(self.den[:, :], net.CU[:, DH, :]).then_inc(self.dens, 16)
        for dst, src in zip((self.wo, self.wg, self.bo), self.drams):
            sp.dma_start(dst[:, :], src).then_inc(self.w, 16)

    def sync_batches(self, sp):
        net = self.net
        sp.wait_ge(self.inverted, BASE + 1)
        sp.dma_start(net.RD, self.den[:, :]).then_inc(self.kept, 16)
        sp.wait_ge(self.kept, BASE + 16)
        with sp.Fori(0, B) as b:
            sp.wait_ge(self.divided, BASE + b)
            sp.dma_start(self.num[:, :], net.CU[bass.ds(b * H, H), 0:DH, :]).then_inc(self.loaded, 16)
            inv = over(net.RD[bass.ds(b * H, H), :], 1, DH)
            sp.dma_start(self.inv[:, :], inv).then_inc(self.loaded, 16)

    def pe(self, pe):
        nm = self.nm
        pe.wait_ge(self.w, BASE + 16 * len(self.drams))

        def output(b):
            pe.wait_ge(self.divided, BASE + b + 1)
            pe.wait_ge(self.added, BASE + b)
            for j in range(NT):
                m = pe.matmul(self.psY[:, j * P:(j + 1) * P], self.ctx[:, j * P:(j + 1) * P], self.wo[:, :], start=True, stop=True)
            m.then_inc(self.out, 1)

        def body(b, more):
            if more:
                output(b + 2)
            nm.turn(pe, b)
            pe.wait_ge(nm.ready, BASE + b + 1)
            pe.wait_ge(self.taken, BASE + b)
            for j in range(NT):
                m = pe.matmul(self.psG[:, j * E:(j + 1) * E], nm.xT[:, j * P:(j + 1) * P], self.wg[:, :], start=True, stop=True)
            m.then_inc(self.logits, 1)

        output(0)
        output(1)
        with pe.Fori(0, B - 2) as b:
            body(b, True)
        body(B - 2, False)
        body(B - 1, False)

    def act(self, a):
        nm = self.nm
        with a.Fori(0, B) as b:
            if self.hold is not None:
                a.wait_ge(self.held, BASE + b)
            nm.keep(a, b, (self.logits, b))
            if self.hold is not None:
                a.wait_ge(nm.ready, BASE + b + 1)
                a.copy(self.hold[:, bass.ds(b, 1), :].rearrange("p o s -> p (o s)"), nm.xT[:, :]).then_inc(self.held, 1)
            a.wait_ge(self.logits, BASE + b + 1)
            a.copy(self.lg[:, bass.ds(b * NT, NT), :].rearrange("p j e -> p (j e)"), self.psG[:, 0:NT * E]).then_inc(self.taken, 1)

    def dve(self, v):
        nm = self.nm
        v.wait_ge(self.dens, BASE + 16)
        if self.floor is not None:
            v.tensor_scalar(self.den[:, :], self.den[:, :], self.floor, None, ALU.max).then_inc(self.floored, 1)
            v.wait_ge(self.floored, BASE + 1)
        v.reciprocal(self.den[:, :], self.den[:, :]).then_inc(self.inverted, 1)
        if len(self.drams) == 3:
            v.wait_ge(self.w, BASE + 48)
            v.tensor_tensor(self.net.X[:, :, :], self.net.X[:, :, :], over(self.bo[:, :], 1, B * NT), ALU.add).then_inc(self.inverted, 1)
            v.wait_ge(self.inverted, BASE + 2)

        def add(b):
            x = self.net.X[:, bass.ds(b * NT, NT), :]
            v.wait_ge(self.out, BASE + b + 1)
            v.tensor_tensor(x, x, self.psY[:, :].rearrange("p (j d) -> p j d", j=NT), ALU.add).then_inc(self.added, 1)

        def stats(b):
            v.wait_ge(self.added, BASE + b + 1)
            nm.stats(v, b)

        def before():
            add(0)
            stats(0)

        def body(b, more):
            if more:
                add(b + 1)
            nm.norm(v, b)
            if more:
                stats(b + 1)

        batches(v, before, body)

    def pool(self, g):
        def divide(b):
            g.wait_ge(self.loaded, BASE + 32 * b + 32)
            g.wait_ge(self.out, BASE + b)
            g.tensor_tensor(self.ctx[:, :], self.num[:, :], self.inv[:, :], ALU.mult).then_inc(self.divided, 1)

        def body(b, more):
            if more:
                divide(b + 1)
            self.nm.power(g, b)

        batches(g, lambda: divide(0), body)


def softmax(v, at, step, count, mx, sm, ex, shifted, powered, bias=None):
    T = B * NT

    def then(ins):
        count[0] += 1
        ins.then_inc(step, 1)
        v.wait_ge(step, BASE + count[0])

    lg = at.lg[:, :, :]
    v.wait_ge(at.taken, BASE + B)
    if bias is not None:
        then(v.tensor_tensor(lg, lg, over(bias, 1, T), ALU.add))
    then(v.tensor_reduce(mx[:, :], lg, AX, ALU.max))
    v.tensor_tensor(lg, lg, over(mx[:, :], 2, E), ALU.subtract).then_inc(shifted, 1)
    v.wait_ge(powered, BASE + 1)
    then(v.reduce_sum(sm[:, :], ex[:, :, :], AX))
    then(v.reciprocal(sm[:, :], sm[:, :]))
    return then


def moe_top2(net, tag, attended):
    nc, aps = net.nc, net.aps
    T = B * NT
    with Phase(net, tag) as ph:
        psE = [[ph.ps(f"psE{r}{x}", [P, S]) for x in range(2)] for r in range(4)]
        xall = ph.sb("xall", [P, B, S])
        at = Attended(ph, psE[0][0], psE[0][1], psE[1][0], *attended, wg=aps["L0_ffn_Wg"], hold=xall)
        bg = ph.sb("bg", [P, E])
        we = ph.sb("we", [D, E * D])
        be = ph.sb("be", [1, E * D])
        rest = ph.sb("rest", [1, E * D])
        bparts = ph.sb("bparts", [1, 3, E * D], BF16)
        be3 = ph.sb("be3", [3, E * D], BF16)
        one3 = ph.sb("one3", [3, P], BF16)
        mx, sm = ph.sb("mx", [P, T]), ph.sb("sm", [P, T])
        ex, cnt, gate = ph.sb("ex", [P, T, E]), ph.sb("cnt", [P, T, E]), ph.sb("gate", [P, T, E])
        gt = ph.sb("gt", [P, T, E, E])
        xs = ph.sb("xs", [P, 2, S])
        gs = ph.sb("gs", [P, 2, NT * E])
        acc = ph.sb("acc", [P, 2, 2, D])
        weights, split, spread, made, shifted, powered, gated, fetched, gates, mixed, step, summed = (ph.sem(x) for x in
            ("weights", "split", "spread", "made", "shifted", "powered", "gated", "fetched", "gates", "mixed", "step", "summed"))
        PAIR = 2 * E

        with ph.start() as block:
            @block.sync
            def _(sp):
                at.sync(sp)
                sp.dma_start(be[:, :], aps["L0_ffn_be"].rearrange("(o e) d -> o (e d)", o=1)).then_inc(weights, 16)
                sp.dma_start(bg[:, :], aps["L0_ffn_bg"].unsqueeze(0).broadcast_to([P, E])).then_inc(weights, 16)
                sp.dma_start(we[:, :], aps["WeT"]).then_inc(weights, 16)
                at.sync_batches(sp)
                sp.wait_ge(split, BASE + 4)
                for i in range(3):
                    sp.dma_start(be3[i:i + 1, :], bparts[:, i, :]).then_inc(spread, 16)

            @block.tensor
            def _(pe):
                at.pe(pe)
                pe.wait_ge(weights, BASE + 48)
                pe.wait_ge(made, BASE + 2)
                pe.wait_ge(spread, BASE + 48)
                pe.wait_ge(at.nm.ready, BASE + B)
                pe.wait_ge(at.taken, BASE + B)
                pe.wait_ge(at.added, BASE + B)
                with pe.Fori(0, B // 2) as i:
                    for x in range(2):
                        b = 2 * i + x
                        pe.wait_ge(fetched, BASE + b + 1)
                        for j in range(NT):
                            if j % 2 == 0:
                                pe.wait_ge(summed, BASE + PAIR * (2 * b + j // 2 + 1))
                            for half in range(2):
                                out, at_ = psE[j][half][:, :], slice(half * S, (half + 1) * S)
                                pe.matmul(out, xs[:, x, j * P:(j + 1) * P], we[:, at_], start=True, stop=False)
                                m = pe.matmul(out, one3[:, :], be3[:, at_], start=False, stop=True)
                            m.then_inc(mixed, 1)

            @block.scalar
            def _(a):
                at.act(a)
                a.wait_ge(shifted, BASE + 1)
                a.activation(ex[:, :, :], at.lg[:, :, :], ACT.Exp).then_inc(powered, 1)
                a.wait_ge(at.held, BASE + B)
                with a.Fori(0, B // 2) as i:
                    for x in range(2):
                        b = 2 * i + x
                        a.wait_ge(mixed, BASE + NT * (b - 1))
                        a.copy(xs[:, x, :], xall[:, bass.ds(b, 1), :].rearrange("p o s -> p (o s)")).then_inc(fetched, 1)
                        a.wait_ge(gated, BASE + 1)
                        a.wait_ge(summed, BASE + PAIR * 2 * b)
                        a.copy(gs[:, x, :], gate[:, bass.ds(b * NT, NT), :].rearrange("p j e -> p (j e)")).then_inc(gates, 1)

            @block.vector
            def _(v):
                at.dve(v)
                v.sem_inc(summed, 2 * PAIR)
                v.wait_ge(weights, BASE + 48)
                count = [0]
                v.tensor_copy(bparts[:, 0, :], be[:, :]).then_inc(split, 1)
                v.wait_ge(split, BASE + 1)
                v.tensor_tensor(rest[:, :], be[:, :], bparts[:, 0, :], ALU.subtract).then_inc(split, 1)
                v.wait_ge(split, BASE + 2)
                v.tensor_copy(bparts[:, 1, :], rest[:, :]).then_inc(split, 1)
                v.wait_ge(split, BASE + 3)
                v.tensor_tensor(bparts[:, 2, :], rest[:, :], bparts[:, 1, :], ALU.subtract).then_inc(split, 1)
                then = softmax(v, at, step, count, mx, sm, ex, shifted, powered, bias=bg[:, :])
                pr = ex
                then(v.tensor_tensor(pr[:, :, :], ex[:, :, :], over(sm[:, :], 2, E), ALU.mult))
                v.wait_ge(made, BASE + 2)
                for f in range(E):
                    if f:
                        m = v.tensor_tensor(gt[:, :, 0:f, f], over(pr[:, :, f], 2, f), pr[:, :, 0:f], ALU.is_gt)
                    if f + 1 < E:
                        m = v.tensor_tensor(gt[:, :, f + 1:, f], over(pr[:, :, f], 2, E - 1 - f), pr[:, :, f + 1:], ALU.is_ge)
                then(m)
                then(v.reduce_sum(cnt[:, :, :], gt[:, :, :, :], AX))
                then(v.scalar_tensor_tensor(gate[:, :, :], cnt[:, :, :], 1.5, pr[:, :, :], ALU.is_lt, ALU.mult))
                then(v.reduce_sum(sm[:, :], gate[:, :, :], AX))
                then(v.reciprocal(mx[:, :], sm[:, :]))
                v.tensor_tensor(gate[:, :, :], gate[:, :, :], over(mx[:, :], 2, E), ALU.mult).then_inc(gated, 1)

                with v.Fori(0, B // 2) as i:
                    for x in range(2):
                        b = 2 * i + x
                        v.wait_ge(gates, BASE + b + 1)
                        for p in range(2):
                            v.wait_ge(mixed, BASE + NT * b + 2 * p + 2)
                            k = 0
                            for e in range(E):
                                for t in range(2):
                                    j = 2 * p + t
                                    tile = at.nm.tile(b, j)
                                    v.wait_ge(summed, BASE + PAIR * (2 * b + p + 2) + k - 1)
                                    v.scalar_tensor_tensor(tile if e == E - 1 else acc[:, t, e % 2, :],
                                                           psE[j][e // 4][:, (e % 4) * P:(e % 4 + 1) * P],
                                                           gs[:, x, j * E + e:j * E + e + 1],
                                                           acc[:, t, (e + 1) % 2, :] if e else tile,
                                                           ALU.mult, ALU.add).then_inc(summed, 1)
                                    k += 1

            @block.gpsimd
            def _(g):
                g.memset(one3[:, :], 1.0).then_inc(made, 1)
                g.memset(gt[:, :, :, :], 0.0).then_inc(made, 1)
                at.pool(g)


class Projections:

    def __init__(self, ph, bias_of):
        self.net, self.bias_of = ph.net, bias_of
        self.w = ph.sb("w", [D, 3, D])
        self.cols = ph.sb("bias_cols", [D, 2])
        self.row = ph.sb("bias_row", [P, D])
        self.loaded, self.vals = ph.sem("weights"), ph.sem("vals")

    def load(self, sp, weights):
        for n, x in enumerate(weights):
            sp.dma_start(self.w[:, n, :], x).then_inc(self.loaded, 16)
        for n in range(2):
            sp.dma_start(self.cols[:, n:n + 1], self.bias_of[n].unsqueeze(1)).then_inc(self.loaded, 16)
        sp.dma_start(self.row[:, :], self.bias_of[2].unsqueeze(0).broadcast_to([P, D])).then_inc(self.loaded, 16)

    def wait(self, eng):
        eng.wait_ge(self.loaded, BASE + 16 * 6)

    def values(self, pe, psV, x, w):
        for j in range(NT):
            m = pe.matmul(psV[:, j * P:(j + 1) * P], x[:, j * P:(j + 1) * P], w, start=True, stop=True)
        return m

    def dve_values(self, v, psV, b):
        v.tensor_tensor(self.net.V[:, bass.ds(b * H, H), :, :].rearrange("p h j d -> p j h d"),
                        psV[:, :].rearrange("p (j h d) -> p j h d", j=NT, h=H),
                        over(self.row[:, :].rearrange("p (h d) -> p h d", h=H), 1, NT), ALU.add).then_inc(self.vals, 1)


def values_out(net, a, psV, b):
    return a.copy(net.V[:, bass.ds(b * H, H), :, :].rearrange("p h j d -> p j h d"),
                  psV[:, :].rearrange("p (j h d) -> p j h d", j=NT, h=H))


def linear_prep(net, experts):
    nc, aps = net.nc, net.aps
    with Phase(net, "la") as ph:
        pr = Projections(ph, [aps[f"L1_attn_a_b{x}"] for x in "qkv"])
        low, ex, f = ph.sb("low", [P, 2, S]), ph.sb("ex", [P, 2, S]), ph.sb("f", [P, 2, S])
        high = ph.sb("high", [P, 2, S])
        psT, psQ, psK, psV = (ph.ps(n, [P, S]) for n in ("psT", "psQ", "psK", "psV"))
        nm = Norm(ph, "n", psT)
        sp_q = Split(ph, "q", P, f[:, 0, :])
        sp_k = Split(ph, "k", P, f[:, 1, :])
        proj, clipped, powered, mapped = (ph.sem(x) for x in ("proj", "clipped", "powered", "mapped"))
        with ph.start() as block:
            @block.sync
            def _(sp):
                pr.load(sp, [aps[f"L1a_W{x}T"] for x in "qkv"])
                experts.load(sp)
                with sp.Fori(0, B // 2) as i:
                    for x in range(2):
                        sp_q.store(sp, 2 * i + x, x, net.QS, True)
                        sp_k.store(sp, 2 * i + x, x, net.KS, False)
                for s in (sp_q, sp_k):
                    s.end(sp)

            @block.tensor
            def _(pe):
                pr.wait(pe)

                def body(b, more, x):
                    pe.wait_ge(nm.ready, BASE + b + 1)
                    pe.wait_ge(clipped, BASE + 4 * b)
                    pe.matmul(psQ[:, :], pr.w[:, 0, :], nm.xT[:, :], start=True, stop=True).then_inc(proj, 1)
                    pe.matmul(psK[:, :], pr.w[:, 1, :], nm.xT[:, :], start=True, stop=True).then_inc(proj, 1)
                    pe.wait_ge(pr.vals, BASE + b)
                    pr.values(pe, psV, nm.xT, pr.w[:, 2, :]).then_inc(proj, 1)
                    if more:
                        nm.turn(pe, b + 1)

                batch_pairs(pe, lambda: nm.turn(pe, 0), body)

            @block.scalar
            def _(a):
                def body(b, more, x):
                    for n in range(2):
                        a.wait_ge(clipped, BASE + 4 * b + 2 * n + 2)
                        a.wait_ge(mapped, BASE + 2 * b + n - 1)
                        a.activation(ex[:, n, :], low[:, n, :], ACT.Exp).then_inc(powered, 1)
                    if more:
                        nm.keep(a, b + 1, (proj, 3 * b + 3))
                    sp_q.act(a, b, x, (mapped, 2 * b + 1))
                    sp_k.act(a, b, x, (mapped, 2 * b + 2))
                    sp_q.act_second(a, b, x)
                    sp_k.act_second(a, b, x)

                batch_pairs(a, lambda: nm.keep(a, 0, (proj, 0)), body)

            @block.vector
            def _(v):
                pr.wait(v)

                def before():
                    nm.stats(v, 0)
                    nm.norm(v, 0)

                def body(b, more, x):
                    v.wait_ge(powered, BASE + 2 * b)
                    v.wait_ge(mapped, BASE + 2 * b)
                    for n, ps in enumerate((psQ, psK)):
                        v.wait_ge(proj, BASE + 3 * b + n + 1)
                        v.tensor_scalar(high[:, n, :], ps[:, :], pr.cols[:, n:n + 1], 0.0, ALU.add, ALU.max).then_inc(clipped, 1)
                        v.tensor_scalar(low[:, n, :], ps[:, :], pr.cols[:, n:n + 1], 0.0, ALU.add, ALU.min).then_inc(clipped, 1)
                    if more:
                        nm.stats(v, b + 1)
                    v.wait_ge(proj, BASE + 3 * b + 3)
                    pr.dve_values(v, psV, b)
                    for n, s in enumerate((sp_q, sp_k)):
                        v.wait_ge(powered, BASE + 2 * b + n + 1)
                        v.wait_ge(s.rest, BASE + b)
                        v.tensor_tensor(f[:, n, :], high[:, n, :], ex[:, n, :], ALU.add).then_inc(mapped, 1)
                    if more:
                        nm.norm(v, b + 1)
                    sp_q.dve(v, b, x)
                    sp_k.dve(v, b, x)

                batch_pairs(v, before, body)

            @block.gpsimd
            def _(g):
                def body(b, more, x):
                    if more:
                        nm.power(g, b + 1)
                    sp_q.pool(g, b, x)
                    sp_k.pool(g, b, x)

                batch_pairs(g, lambda: nm.power(g, 0), body)


def relative_tables(net, keep):
    nc, aps = net.nc, net.aps
    with Phase(net, "rt") as ph:
        w = ph.sb("w", [D, 2, D])
        bias = ph.sb("bias", [1, 2, D])
        rel = ph.sb("rel", [D, 2, P])
        tab = ph.sb("tab", [P, TW])
        r1 = ph.sb("r1", [P, TW])
        part = ph.sb("part", [P, 3, TW], BF16)
        zero = ph.sb("zero", [P, P])
        psP, psQ = ph.ps("psP", [P, P]), ph.ps("psQ", [P, P])
        weights, proj, filled, first, rest, second, third, kept, zeroed = (ph.sem(x) for x in
            ("weights", "proj", "filled", "first", "rest", "second", "third", "kept", "zeroed"))
        with ph.start() as block:
            @block.sync
            def _(sp):
                for n, x in enumerate(("k", "q")):
                    sp.dma_start(w[:, n, :], aps[f"L0b_Wp{x}T"]).then_inc(weights, 16)
                    sp.dma_start(bias[:, n, :], aps[f"L0_attn_b_bp{x}"].unsqueeze(0)).then_inc(weights, 16)
                sp.dma_start(rel[:, 0, :], aps["relT"]).then_inc(weights, 16)
                sp.dma_start(rel[:, 1, :], aps["relT_reversed"]).then_inc(weights, 16)
                sp.wait_ge(third, BASE + 1)
                copies = net.TB.rearrange("h (r c) x -> (h r) c x", c=NC6)
                for i, (lo, hi) in enumerate(RUNS):
                    sp.dma_start(copies[:, lo:hi, 0:EXT], part[:, 0:hi - lo, 0:EXT]).then_inc(kept, 16)
                    sp.dma_start(copies[:, lo:hi, EXT:], over(part[:, i, EXT:], 1, hi - lo)).then_inc(kept, 16)
                sp.wait_ge(kept, BASE + 32 * len(RUNS))

            @block.tensor
            def _(pe):
                pe.wait_ge(weights, BASE + 16 * 6)
                for n, ps in enumerate((psP, psQ)):
                    pe.matmul(ps[:, :], w[:, n, :], rel[:, n, :], start=True, stop=False)
                    pe.matmul(ps[:, :], bias[:, n, :], net.ones[:, 0:P], start=False, stop=True).then_inc(proj, 1)

            @block.vector
            def _(v):
                v.memset(zero[:, :], 0.0).then_inc(zeroed, 1)
                v.wait_ge(zeroed, BASE + 1)
                v.wait_ge(proj, BASE + 2)
                z = zero[:, :]
                fill = lambda lo, hi, col: v.tensor_scalar(tab[:, lo:hi], zero[:, 0:hi - lo], col, None, ALU.add).then_inc(filled, 1)
                first_k, last_k, first_q, last_q = psP[:, 0:1], psP[:, P - 1:P], psQ[:, P - 1:P], psQ[:, 0:1]
                fill(0, P - 1, first_k)
                v.tensor_copy(tab[:, P - 1:2 * P - 1], psP[:, :]).then_inc(filled, 1)
                fill(2 * P - 1, 3 * P - 1, last_k)
                fill(3 * P - 1, 3 * P, last_k)
                fill(EXT, EXT + P, last_q)
                v.tensor_copy(tab[:, EXT + P:EXT + 2 * P], psQ[:, :]).then_inc(filled, 1)
                fill(EXT + 2 * P, 2 * EXT, first_q)
                fill(2 * EXT, 2 * EXT + P, first_q)
                fill(2 * EXT + P, TW, last_q)
                v.wait_ge(filled, BASE + 9)
                v.tensor_copy(keep[:, 0:1], tab[:, 0:1])
                v.tensor_copy(keep[:, 1:2], tab[:, EXT - 1:EXT])
                v.tensor_copy(part[:, 0, :], tab[:, :]).then_inc(first, 1)
                v.wait_ge(first, BASE + 1)
                v.tensor_tensor(r1[:, :], tab[:, :], part[:, 0, :], ALU.subtract).then_inc(rest, 1)
                v.wait_ge(rest, BASE + 1)
                v.tensor_copy(part[:, 1, :], r1[:, :]).then_inc(second, 1)
                v.wait_ge(second, BASE + 1)
                v.tensor_tensor(part[:, 2, :], r1[:, :], part[:, 1, :], ALU.subtract).then_inc(third, 1)


def relative_prep(net, keep):
    nc, aps = net.nc, net.aps
    with Phase(net, "ra") as ph:
        pr = Projections(ph, [aps[f"L0_attn_b_b{x}"] for x in "qkv"])
        far = ph.sb("far", [P, 2, FAR])
        psT, psQ, psK, psV = (ph.ps(n, [P, S]) for n in ("psT", "psQ", "psK", "psV"))
        nm = Norm(ph, "n", psT)
        sp_q = Split(ph, "q", P, psQ[:, :], bias=pr.cols[:, 0:1])
        sp_k = Split(ph, "k", P, psK[:, :], bias=pr.cols[:, 1:2])
        sp_l = Split(ph, "l", P, far[:, 0, :], FAR)
        sp_h = Split(ph, "h", P, far[:, 1, :], FAR)
        proj, shifted = ph.sem("proj"), ph.sem("shifted")
        with ph.start() as block:
            @block.sync
            def _(sp):
                pr.load(sp, [aps[f"L0b_W{x}T"] for x in "qkv"])
                with sp.Fori(0, B // 2) as i:
                    for x in range(2):
                        sp_q.store(sp, 2 * i + x, x, net.QS, True)
                        sp_k.store(sp, 2 * i + x, x, net.KS, False)
                        sp_l.store(sp, 2 * i + x, x, net.KLS, False)
                        sp_h.store(sp, 2 * i + x, x, net.KHS, False)
                for s in (sp_q, sp_k, sp_l, sp_h):
                    s.end(sp)

            @block.tensor
            def _(pe):
                pr.wait(pe)

                def body(b, more, x):
                    pe.wait_ge(nm.ready, BASE + b + 1)
                    pe.wait_ge(sp_q.rest, BASE + b)
                    pe.matmul(psQ[:, :], pr.w[:, 0, :], nm.xT[:, :], start=True, stop=True).then_inc(proj, 1)
                    pe.wait_ge(sp_k.rest, BASE + b)
                    pe.wait_ge(shifted, BASE + 2 * b)
                    pe.matmul(psK[:, :], pr.w[:, 1, :], nm.xT[:, :], start=True, stop=True).then_inc(proj, 1)
                    pe.wait_ge(pr.vals, BASE + b)
                    pr.values(pe, psV, nm.xT, pr.w[:, 2, :]).then_inc(proj, 1)
                    if more:
                        nm.turn(pe, b + 1)

                batch_pairs(pe, lambda: nm.turn(pe, 0), body)

            @block.scalar
            def _(a):
                def body(b, more, x):
                    sp_q.act(a, b, x, (proj, 3 * b + 1))
                    sp_k.act(a, b, x, (proj, 3 * b + 2))
                    if more:
                        nm.keep(a, b + 1, (proj, 3 * b + 3))
                    sp_q.act_second(a, b, x)
                    sp_k.act_second(a, b, x)
                    sp_l.act(a, b, x, (shifted, 2 * b + 1))
                    sp_h.act(a, b, x, (shifted, 2 * b + 2))
                    sp_l.act_second(a, b, x)
                    sp_h.act_second(a, b, x)

                batch_pairs(a, lambda: nm.keep(a, 0, (proj, 0)), body)

            @block.vector
            def _(v):
                pr.wait(v)

                def before():
                    nm.stats(v, 0)
                    nm.norm(v, 0)

                def body(b, more, x):
                    if more:
                        nm.stats(v, b + 1)
                    sp_q.dve(v, b, x)
                    sp_k.dve(v, b, x)
                    v.wait_ge(sp_k.rest, BASE + b + 1)
                    for n, s in enumerate((sp_l, sp_h)):
                        v.wait_ge(s.rest, BASE + b)
                        v.tensor_scalar(far[:, n, :], psK[:, n * (S - FAR):n * (S - FAR) + FAR], pr.cols[:, 1:2],
                                        keep[:, n:n + 1], ALU.add, ALU.add).then_inc(shifted, 1)
                    if more:
                        nm.norm(v, b + 1)
                    v.wait_ge(proj, BASE + 3 * b + 3)
                    pr.dve_values(v, psV, b)
                    sp_l.dve(v, b, x)
                    sp_h.dve(v, b, x)

                batch_pairs(v, before, body)

            @block.gpsimd
            def _(g):
                def body(b, more, x):
                    if more:
                        nm.power(g, b + 1)
                    for s in (sp_q, sp_k, sp_l, sp_h):
                        s.pool(g, b, x)

                batch_pairs(g, lambda: nm.power(g, 0), body)


def rotary_prep(net):
    nc, aps = net.nc, net.aps
    with Phase(net, "ya") as ph:
        wx = ph.sb("wx", [D, 6, D])
        bias = aps["L1_attn_b_in_proj_b"]
        pr = Projections(ph, [bias[n * D:(n + 1) * D] for n in range(3)])
        rot = ph.sb("rot", [D, 2, S])
        t = ph.sb("t", [D, 3, 2, S])
        turned = ph.sb("turned", [D, 3, S])
        psT, psQ, psK, psV = (ph.ps(n, [P, S]) for n in ("psT", "psQ", "psK", "psV"))
        ps = [[ph.ps(f"ps{i}{x}", [P, S]) for x in range(2)] for i in range(2)]
        nm = Norm(ph, "n", psT)
        sp_q = Split(ph, "q", P, psQ[:, :], bias=pr.cols[:, 0:1])
        sp_k = Split(ph, "k", P, psK[:, :], bias=pr.cols[:, 1:2])
        weights, first, products, rotated, proj = (ph.sem(x) for x in
            ("weights_x", "first", "products", "rotated", "proj"))
        with ph.start() as block:
            @block.sync
            def _(sp):
                sp.dma_start(wx[:, :, :], aps["L1b_w"]).then_inc(weights, 16)
                sp.dma_start(rot[:, :, :], aps["L1b_rot"]).then_inc(weights, 16)
                pr.load(sp, [aps["L1b_in"][:, n, :] for n in range(3)])
                with sp.Fori(0, B // 2) as i:
                    for x in range(2):
                        sp_q.store(sp, 2 * i + x, x, net.QS, True)
                        sp_k.store(sp, 2 * i + x, x, net.KS, False)
                for s in (sp_q, sp_k):
                    s.end(sp)

            @block.tensor
            def _(pe):
                pe.wait_ge(weights, BASE + 32)
                pr.wait(pe)

                def turning(b, n):
                    m = 3 * b + n
                    pe.wait_ge(products, BASE + 2 * m - 2)
                    for x in range(2):
                        mm = pe.matmul(ps[n % 2][x][:, :], wx[:, 2 * n + x, :], nm.xT[:, :], start=True, stop=True)
                    mm.then_inc(first, 1)

                def projection(b, n):
                    pe.wait_ge(rotated, BASE + 3 * b + n + 1)
                    if n == 2:
                        pe.wait_ge(pr.vals, BASE + b)
                        pr.values(pe, psV, turned[:, 2, :], pr.w[:, 2, :]).then_inc(proj, 1)
                    else:
                        pe.wait_ge((sp_q, sp_k)[n].rest, BASE + b)
                        pe.matmul((psQ, psK)[n][:, :], pr.w[:, n, :], turned[:, n, :], start=True, stop=True).then_inc(proj, 1)

                def body(b, more, x):
                    pe.wait_ge(nm.ready, BASE + b + 1)
                    turning(b, 0)
                    turning(b, 1)
                    projection(b, 0)
                    turning(b, 2)
                    projection(b, 1)
                    if more:
                        nm.turn(pe, b + 1)
                    projection(b, 2)

                batch_pairs(pe, lambda: nm.turn(pe, 0), body)

            @block.scalar
            def _(a):
                def body(b, more, x):
                    sp_q.act(a, b, x, (proj, 3 * b + 1))
                    sp_k.act(a, b, x, (proj, 3 * b + 2))
                    sp_q.act_second(a, b, x)
                    if more:
                        nm.keep(a, b + 1, (first, 3 * b + 3))
                    sp_k.act_second(a, b, x)

                batch_pairs(a, lambda: nm.keep(a, 0, (first, 0)), body)

            @block.vector
            def _(v):
                v.wait_ge(weights, BASE + 32)
                pr.wait(v)

                def before():
                    nm.stats(v, 0)
                    nm.norm(v, 0)

                def body(b, more, x):
                    for n in range(3):
                        m = 3 * b + n
                        v.wait_ge(first, BASE + m + 1)
                        v.wait_ge(rotated, BASE + m - 2)
                        for y in range(2):
                            v.tensor_tensor(t[:, n, y, :], ps[n % 2][y][:, :], rot[:, y, :], ALU.mult).then_inc(products, 1)
                        if more and n == 0:
                            nm.stats(v, b + 1)
                        if n == 1:
                            sp_q.dve(v, b, x)
                        if n == 2:
                            sp_k.dve(v, b, x)
                    if more:
                        nm.norm(v, b + 1)
                    v.wait_ge(proj, BASE + 3 * b + 3)
                    pr.dve_values(v, psV, b)

                batch_pairs(v, before, body)

            @block.gpsimd
            def _(g):
                def body(b, more, x):
                    if more:
                        nm.power(g, b + 1)
                    for n in range(3):
                        m = 3 * b + n
                        g.wait_ge(products, BASE + 2 * m + 2)
                        g.wait_ge(proj, BASE + m - 2)
                        g.tensor_tensor(turned[:, n, :], t[:, n, 0, :], t[:, n, 1, :], ALU.add).then_inc(rotated, 1)
                    sp_q.pool(g, b, x)
                    sp_k.pool(g, b, x)

                batch_pairs(g, lambda: nm.power(g, 0), body)


QDIAG = (896, 1024, 512, 0)


def heads_max(net, tag, scale):
    nc = net.nc
    N = B * H
    ORDER = (3, 2, 0, 1)
    with Phase(net, tag) as ph:
        hl = HeadLoads(ph, NC6 * DH, net.QS, net.KS)
        mask = ph.sb("mask", [P, CAUSAL])
        mx = ph.sb("mx", [P, R, NT])
        nm = ph.sb("nm", [P, R, NT])
        e = ph.sb("e", [P, R, CAUSAL])
        w = ph.sb("w", [P, R, CAUSAL])
        sc = ph.ps("sc", [P, 3 * S])
        tr = ph.ps("tr", [P, 3 * S])
        masks, scored, found, negated, powered, turned, weighed, weighed_a, summed = (ph.sem(x) for x in
            ("masks", "scored", "found", "negated", "powered", "turned", "weighed", "weighed_a", "summed"))
        with ph.start() as block:
            @block.sync
            def _(sp):
                hl.sync(sp, scored)

            def scores(pe, i, u, n):
                hl.wait_loaded(pe, i, u)
                for x, I in enumerate(ORDER):
                    at, width = QDIAG[I], (I + 1) * P
                    pe.wait_ge(found, BASE + NT * (n - 1) + (x + 1 if x != 1 else 3))
                    m = pe.matmul(sc[:, at:at + width], hl.q[:, u % R, I * P:width], hl.k[:, u % R, 0:width],
                                  start=True, stop=True)
                m.then_inc(scored, 1)

            def turn(pe, u, n):
                pe.wait_ge(powered, BASE + NT * n + NT)
                for tiles, sem, count in (((0,), weighed, 2 * n - 1), ((1, 3), weighed_a, n), ((2,), weighed, 2 * n)):
                    pe.wait_ge(sem, BASE + count)
                    for J in tiles:
                        for I in range(J, NT):
                            at, to = QDIAG[I] + J * P, DIAG[J] + (I - J) * P
                            m = pe.transpose(tr[:, to:to + P], e[:, u % R, at:at + P], net.idf[:, :])
                    m.then_inc(turned, 1)

            @block.tensor
            def _(pe):
                def step(i, u, last):
                    t = u + AHEAD
                    if not last or t < UT:
                        scores(pe, i + t // UT, t % UT, UT * i + t)
                    if not last or u + 1 < UT:
                        turn(pe, (u + 1) % UT, UT * i + u + 1)
                    n = UT * i + u
                    even = [(weighed, 2 * n + 1), (weighed, 2 * n + 2)]
                    hl.context(pe, i, u, n, w[:, u % R, :], [even[0], (weighed_a, n + 1), even[1], (weighed_a, n + 1)], summed)

                for u in range(AHEAD):
                    scores(pe, 0, u, u)
                turn(pe, 0, 0)
                with pe.Fori(0, N // UT - 1) as i:
                    for u in range(UT):
                        step(i, u, False)
                for u in range(UT):
                    step(N // UT - 1, u, True)

            @block.vector
            def _(v):
                v.wait_ge(masks, BASE + 2)

                def find(u, n):
                    v.wait_ge(scored, BASE + n + 1)
                    waited(net, v, (turned, 3 * (n - R + 1)))
                    for I in ORDER:
                        part = slice(QDIAG[I], QDIAG[I] + (I + 1) * P)
                        v.tensor_tensor_reduce(e[:, u % R, part], sc[:, part], mask[:, part], 1.0, -3e38,
                                               ALU.add, ALU.max, mx[:, u % R, I:I + 1]).then_inc(found, 1)
                    v.wait_ge(found, BASE + NT * n + NT)
                    v.tensor_scalar(nm[:, u % R, :], mx[:, u % R, :], -scale, None, ALU.mult).then_inc(negated, 1)

                def keep(u, n):
                    v.wait_ge(summed, BASE + n - R + 1)
                    for x, part in ((0, slice(0, S)), (2, slice(2 * S, CAUSAL))):
                        v.wait_ge(turned, BASE + 3 * n + x + 1)
                        v.tensor_copy(w[:, u % R, part], tr[:, part]).then_inc(weighed, 1)

                def step(i, u, last):
                    t = u + AHEAD
                    if not last or t < UT:
                        find(t % UT, UT * i + t)
                    if not last or u + 1 < UT:
                        keep((u + 1) % UT, UT * i + u + 1)

                for u in range(AHEAD):
                    find(u, u)
                keep(0, 0)
                with v.Fori(0, N // UT - 1) as i:
                    for u in range(UT):
                        step(i, u, False)
                for u in range(UT):
                    step(N // UT - 1, u, True)

            @block.scalar
            def _(a):
                def item(u, n):
                    a.wait_ge(negated, BASE + n + 1)
                    for I in ORDER:
                        part = slice(QDIAG[I], QDIAG[I] + (I + 1) * P)
                        a.activation(e[:, u % R, part], e[:, u % R, part], ACT.Exp, bias=nm[:, u % R, I:I + 1],
                                     scale=scale).then_inc(powered, 1)

                def keep(u, n):
                    a.wait_ge(turned, BASE + 3 * n + 2)
                    a.wait_ge(summed, BASE + n - R + 1)
                    a.copy(w[:, u % R, S:2 * S], tr[:, S:2 * S]).then_inc(weighed_a, 1)

                hl.act(a, item, summed, after=keep)

            @block.gpsimd
            def _(g):
                g.memset(mask[:, :], 0.0).then_inc(masks, 1)
                hl.pool_start(g)
                for I in range(NT):
                    x = mask[:, QDIAG[I] + I * P:QDIAG[I] + (I + 1) * P]
                    m = g.affine_select(out=x, in_=x, compare_op=ALU.is_ge, fill=-1e30, base=0,
                                        pattern=[[-1, P]], channel_multiplier=1)
                m.then_inc(masks, 1)
                with g.Fori(0, N // UT) as i:
                    for u in range(UT):
                        hl.pool_values(g, UT * i + u, u, summed)


C1, C2 = NT * P, (NT - 1) * P


def heads_relative(net, tag, scale):
    nc = net.nc
    rows = NC6 * DH
    G = 16
    with Phase(net, tag) as ph:
        q = ph.sb("q", [rows, B, S], BF16)
        k = ph.sb("k", [rows, B, S], BF16)
        kl = ph.sb("kl", [rows, B, FAR], BF16)
        kh = ph.sb("kh", [rows, B, FAR], BF16)
        tb = ph.sb("tb", [rows, TW], BF16)
        c0 = ph.sb("c0", [P, B, NT, P])
        c1 = ph.sb("c1", [P, B, NT - 1, P])
        d0 = ph.sb("d0", [P, B, NT, P])
        d1 = ph.sb("d1", [P, B, NT - 1, P])
        bf = ph.sb("bf", [P, NT * (S + P)])
        v1 = ph.sb("v1", [P, B, NT, VW])
        mx = ph.sb("mx", [P, R, NT])
        nm = ph.sb("nm", [P, R, NT])
        ss = ph.sb("ss", [P, R, NT, S])
        w = ph.sb("w", [P, NT, S])
        o = ph.sb("o", [P, 2, S])
        sc = [ph.ps(f"sc{i}", [P, S]) for i in range(2)]
        pc = [ph.ps(f"pc{i}", [P, S]) for i in range(2)]
        tr = [ph.ps(f"tr{i}", [P, S]) for i in range(2)]
        po = [ph.ps(f"po{i}", [P, S]) for i in range(2)]
        names = ("stacks", "fars", "tabled", "ctab", "dtab", "turned", "biased", "scored", "full", "negated", "powered",
                 "blocks", "summed", "copied", "valued", "made", "placed")
        (stacks, fars, tabled, ctab, dtab, turned, biased_, scored, full, negated, powered, blocks, summed, copied,
         valued, made, placed) = (ph.sem(x) for x in names)
        weighed = [ph.sem(f"weighed{i}") for i in range(2)]
        stored = [ph.sem(f"stored{i}") for i in range(2)]
        keysL, posF, posL = EXT, 2 * EXT, 2 * EXT + P
        CH = P // G
        LAG = 2

        with ph.start() as block:
            @block.sync
            def _(sp):
                heads = lambda t: t.rearrange("(b h) r s -> h r b s", b=B)

                def load(h):
                    for dst, src, sem in ((q, net.QS, stacks), (k, net.KS, stacks),
                                          (kl, net.KLS, fars), (kh, net.KHS, fars)):
                        if dst is kl:
                            sp.dma_start(tb[:, :], net.TB[bass.ds(h, 1), :, :].rearrange("o r s -> (o r) s")).then_inc(stacks, 16)
                        sp.dma_start(dst[:, :, :], heads(src)[bass.ds(h, 1), :, :, :].rearrange("o r b s -> (o r) b s"))\
                            .then_inc(sem, 16)

                def store(h, g):
                    sp.wait_ge(copied, BASE + 2 * h + g + 1)
                    for u in range(U):
                        bh = (U * g + u) * H + h
                        sp.dma_start(net.CU[bass.ds(bh, 1), :, :], o[VW * u:VW * u + DH + 1, g, :]).then_inc(stored[g], 16)

                load(0)
                with sp.Fori(0, H - 1) as h:
                    store(h, 0)
                    sp.wait_ge(scored, BASE + NT * B * (h + 1))
                    load(h + 1)
                    store(h, 1)
                store(H - 1, 0)
                store(H - 1, 1)
                for x in stored:
                    sp.wait_ge(x, BASE + 16 * U * H)

            @block.tensor
            def _(pe):
                def tables(h):
                    pe.wait_ge(stacks, BASE + 48 * h + 48)
                    qv = q[:, :, :].rearrange("r b (i s) -> r s b i", i=NT)
                    kv = k[:, :, :].rearrange("r b (i s) -> r s b i", i=NT)
                    pe.wait_ge(full, BASE + NT * B * h)
                    for c in range(CH):
                        if c >= 2:
                            pe.wait_ge(ctab, BASE + 2 * CH * h + 2 * c - 2)
                        banks = pc if c % 2 else sc
                        offsets = [(s, G * c + s, 191 - G * c - s) for s in range(G)]
                        for s, x, at in offsets:
                            pe.matmul(banks[0][:, 32 * s:32 * s + 32], tb[:, at:at + P], qv[:, x, :, :], start=True, stop=True)
                        for s, x, at in offsets:
                            pe.matmul(banks[1][64:128, 24 * s:24 * s + 24], tb[:, at - 64:at], qv[:, x, :, 1:NT], start=True, stop=True)
                        for s, x, at in offsets:
                            m = pe.matmul(banks[1][0:64, 24 * s:24 * s + 24], tb[:, at + P:at + P + 64], qv[:, x, :, 0:NT - 1],
                                          start=True, stop=True)
                        m.then_inc(tabled, 1)
                        if c:
                            pe.wait_ge(dtab, BASE + 2 * CH * h + 2 * c)
                        else:
                            for x in weighed:
                                pe.wait_ge(x, BASE + 2 * (B * h - LAG))
                        for s in range(G):
                            x = G * c + s
                            full_, part = tr[0][:, 32 * s:32 * s + 32], tr[1][:, 24 * s:24 * s + 24]
                            at = keysL + 191 - x
                            pe.matmul(full_, tb[:, at:at + P], kv[:, x, :, :], start=True, stop=True)
                            if x >= REL:
                                m = pe.matmul(part, tb[:, at + P:at + 2 * P], kv[:, x, :, 0:NT - 1], start=True, stop=True)
                            else:
                                m = pe.matmul(part, tb[:, at - P:at], kv[:, x, :, 1:NT], start=True, stop=True)
                        m.then_inc(tabled, 1)
                    pe.wait_ge(ctab, BASE + 2 * CH * h + 2 * CH)
                    pe.wait_ge(dtab, BASE + 2 * CH * h + 2 * CH)
                    pe.wait_ge(fars, BASE + 32 * h + 32)

                def positions(h, b):
                    pe.wait_ge(biased_, BASE + 3 * (B * h + b))
                    for i in range(NT):
                        pe.transpose(pc[0][:, i * P:(i + 1) * P], c0[:, b, i, :], net.idf[:, :])
                    for i in range(NT - 1):
                        m = pe.transpose(pc[1][:, i * P:(i + 1) * P], c1[:, b, i, :], net.idf[:, :])
                    m.then_inc(turned, 1)

                def scores(h, b, I):
                    s = sc[I % 2]
                    pe.wait_ge(full, BASE + NT * (B * h + b) + I - 1)
                    lo, hi = max(0, I * P - REL), min(S, I * P + P + REL)
                    qi = q[:, b, I * P:(I + 1) * P]
                    if lo:
                        pe.matmul(s[:, 0:lo], qi, kl[:, b, 0:lo], start=True, stop=False)
                        pe.matmul(s[:, 0:lo], tb[:, posF:posF + P], k[:, b, 0:lo], start=False, stop=True)
                    if hi < S:
                        pe.matmul(s[:, hi:S], qi, kh[:, b, hi - (S - FAR):FAR], start=True, stop=False)
                        pe.matmul(s[:, hi:S], tb[:, posL:posL + P], k[:, b, hi:S], start=False, stop=True)
                    pe.matmul(s[:, lo:hi], qi, k[:, b, lo:hi], start=True, stop=True).then_inc(scored, 1)

                def turn(h, b, J):
                    n = B * h + b
                    if J == 0:
                        pe.wait_ge(powered, BASE + NT * n + NT)
                    pe.wait_ge(weighed[J % 2], BASE + 2 * n + J // 2)
                    for I in range(NT):
                        m = pe.transpose(tr[J % 2][:, I * P:(I + 1) * P], ss[:, b % R, I, J * P:(J + 1) * P], net.idf[:, :])
                    m.then_inc(blocks, 1)

                def context(h, b, J):
                    n = B * h + b
                    if J == 0:
                        pe.wait_ge(valued, BASE + n + 1)
                        if b % U == 0:
                            pe.wait_ge(copied, BASE + 2 * h + b // U - 1)
                    pe.wait_ge(weighed[J % 2], BASE + 2 * n + J // 2 + 1)
                    pe.matmul(po[b // U][VW * (b % U):VW * (b % U + 1), :], v1[:, b, J, :], w[:, J, :],
                              start=J == 0, stop=J == NT - 1).then_inc(summed, 1)

                def front(h, b, back=None):
                    if b == 0:
                        positions(h, 0)
                    scores(h, b, 0)
                    scores(h, b, 1)
                    if back:
                        turn(*back, 0)
                        turn(*back, 1)
                    scores(h, b, 2)
                    scores(h, b, 3)
                    contexts(back, (h, b + 1))

                def contexts(back, ahead=None):
                    if back:
                        context(*back, 0)
                        turn(*back, 2)
                        context(*back, 1)
                        turn(*back, 3)
                    if ahead and ahead[1] < B:
                        positions(*ahead)
                    if back:
                        context(*back, 2)
                        context(*back, 3)

                tables(0)
                for b in range(LAG):
                    front(0, b)
                with pe.Fori(0, H - 1) as h:
                    for b in range(B - LAG):
                        front(h, b + LAG, (h, b))
                    tables(h + 1)
                    for b in range(LAG):
                        front(h + 1, b, (h, b + B - LAG))
                for b in range(B - LAG):
                    front(H - 1, b + LAG, (H - 1, b))
                for b in range(B - LAG, B):
                    turn(H - 1, b, 0)
                    turn(H - 1, b, 1)
                    contexts((H - 1, b))

            @block.vector
            def _(v):
                v.memset(bf[:, :], 0.0).then_inc(placed, 1)
                v.wait_ge(placed, BASE + 1)

                def window(first, n, width):
                    run = bf[:, first:first + n * (S + P)]
                    return run.rearrange("p (n w) -> p n w", n=n)[:, :, 0:width]

                def tables(h):
                    for c in range(CH):
                        banks = pc if c % 2 else sc
                        v.wait_ge(tabled, BASE + 2 * CH * h + 2 * c + 1)
                        v.tensor_copy(c0[:, :, :, G * c:G * c + G],
                                      banks[0][:, :].rearrange("p (s b i) -> p b i s", s=G, b=B)).then_inc(ctab, 1)
                        v.tensor_copy(c1[:, :, :, G * c:G * c + G],
                                      banks[1][:, 0:24 * G].rearrange("p (s b i) -> p b i s", s=G, b=B)).then_inc(ctab, 1)
                    v.wait_ge(dtab, BASE + 2 * CH * h + 2 * CH)

                def keep(h, b, J):
                    n = B * h + b
                    v.wait_ge(blocks, BASE + NT * n + J + 1)
                    v.wait_ge(summed, BASE + NT * (n - 1) + J + 1)
                    v.tensor_copy(w[:, J, :], tr[0][:, :]).then_inc(weighed[0], 1)

                def bias(h, b):
                    n = B * h + b
                    v.wait_ge(turned, BASE + n + 1)
                    v.wait_ge(full, BASE + NT * n)
                    v.tensor_tensor(window(0, NT, P), pc[0][:, :].rearrange("p (i k) -> p i k", i=NT), d0[:, b, :, :],
                                    ALU.add).then_inc(biased_, 1)
                    side = pc[1][:, 0:C2].rearrange("p (i k) -> p i k", i=NT - 1)
                    v.tensor_tensor(window(S + REL, NT - 1, REL), side[:, :, REL:P], d1[:, b, :, REL:P],
                                    ALU.add).then_inc(biased_, 1)
                    v.tensor_tensor(window(P, NT - 1, REL), side[:, :, 0:REL], d1[:, b, :, 0:REL],
                                    ALU.add).then_inc(biased_, 1)

                def front(h, b, back=None):
                    n, x = B * h + b, b % R
                    if b == 0:
                        bias(h, 0)
                    v.wait_ge(biased_, BASE + 3 * n + 3)
                    for I in range(NT):
                        waited(net, v, (scored, NT * n + I + 1), *([(blocks, NT * (n - R + 1))] if I == 0 else []))
                        v.tensor_tensor_reduce(ss[:, x, I, :], sc[I % 2][:, :], bf[:, I * S:(I + 1) * S], 1.0, -3e38,
                                               ALU.add, ALU.max, mx[:, x, I:I + 1]).then_inc(full, 1)
                        if I == 1 and back:
                            keep(*back, 0)
                    v.wait_ge(full, BASE + NT * n + NT)
                    v.wait_ge(powered, BASE + NT * (n - R + 1))
                    v.tensor_scalar(nm[:, x, :], mx[:, x, :], -scale, None, ALU.mult).then_inc(negated, 1)
                    if back:
                        keep(*back, 2)
                    if b + 1 < B:
                        bias(h, b + 1)

                tables(0)
                for b in range(LAG):
                    front(0, b)
                with v.Fori(0, H - 1) as h:
                    for b in range(B - LAG):
                        front(h, b + LAG, (h, b))
                    tables(h + 1)
                    for b in range(LAG):
                        front(h + 1, b, (h, b + B - LAG))
                for b in range(B - LAG):
                    front(H - 1, b + LAG, (H - 1, b))
                for b in range(B - LAG, B):
                    keep(H - 1, b, 0)
                    keep(H - 1, b, 2)

            @block.scalar
            def _(a):
                def tables(h):
                    for c in range(CH):
                        a.wait_ge(tabled, BASE + 2 * CH * h + 2 * c + 2)
                        a.copy(d0[:, :, :, G * c:G * c + G],
                               tr[0][:, :].rearrange("p (s b i) -> p b i s", s=G, b=B)).then_inc(dtab, 1)
                        a.copy(d1[:, :, :, G * c:G * c + G],
                               tr[1][:, 0:24 * G].rearrange("p (s b i) -> p b i s", s=G, b=B)).then_inc(dtab, 1)

                def keep(h, b, J):
                    n = B * h + b
                    a.wait_ge(blocks, BASE + NT * n + J + 1)
                    a.wait_ge(summed, BASE + NT * (n - 1) + J + 1)
                    a.copy(w[:, J, :], tr[1][:, :]).then_inc(weighed[1], 1)

                def power(h, b, I):
                    x = ss[:, b % R, I, :]
                    a.activation(x, x, ACT.Exp, bias=nm[:, b % R, I:I + 1], scale=scale).then_inc(powered, 1)

                def contexts(h, b):
                    g = b // U
                    a.wait_ge(summed, BASE + NT * (B * h + b) + NT)
                    a.wait_ge(stored[g], BASE + 16 * U * h)
                    a.copy(o[:, g, :], po[g][:, :]).then_inc(copied, 1)

                def front(h, b, back=None):
                    if back:
                        keep(*back, 1)
                        keep(*back, 3)
                    a.wait_ge(negated, BASE + B * h + b + 1)
                    for I in range(NT):
                        power(h, b, I)
                    if back and back[1] % U == U - 1:
                        contexts(*back)

                tables(0)
                for b in range(LAG):
                    front(0, b)
                with a.Fori(0, H - 1) as h:
                    for b in range(B - LAG):
                        front(h, b + LAG, (h, b))
                    tables(h + 1)
                    for b in range(LAG):
                        front(h + 1, b, (h, b + B - LAG))
                for b in range(B - LAG):
                    front(H - 1, b + LAG, (H - 1, b))
                for b in range(B - LAG, B):
                    keep(H - 1, b, 1)
                    keep(H - 1, b, 3)
                contexts(H - 1, B - 1)

            @block.gpsimd
            def _(g):
                g.memset(v1[:, :, :, :], 0.0).then_inc(made, 1)
                g.wait_ge(made, BASE + 1)
                g.memset(v1[:, :, :, DH:2 * DH], 1.0).then_inc(made, 1)
                g.wait_ge(made, BASE + 2)

                def values(h, b):
                    g.tensor_copy(v1[:, b, :, 0:DH], net.V[:, bass.ds(b * H + h, 1), :, :].rearrange("p o j d -> p (o j) d"))\
                        .then_inc(valued, 1)

                for b in range(B):
                    values(0, b)
                with g.Fori(0, H - 1) as h:
                    for b in range(B):
                        waited(net, g, (summed, NT * (B * h + b + 1)))
                        values(h + 1, b)


def expert_affinity(net, tag, attended):
    nc, aps = net.nc, net.aps
    T = B * NT
    with Phase(net, tag) as ph:
        at = Attended(ph, *(ph.ps(n, [P, S]) for n in ("psT", "psY", "psG")), *attended, wg=aps["L1f_gateT"])
        mx, sm = ph.sb("mx", [P, T]), ph.sb("sm", [P, T])
        ex = ph.sb("ex", [P, T, E])
        shifted, powered, step = (ph.sem(x) for x in ("shifted", "powered", "step"))
        with ph.start() as block:
            @block.sync
            def _(sp):
                at.sync(sp)
                at.sync_batches(sp)

            @block.tensor
            def _(pe):
                at.pe(pe)

            @block.scalar
            def _(a):
                at.act(a)
                a.wait_ge(shifted, BASE + 1)
                a.activation(ex[:, :, :], at.lg[:, :, :], ACT.Exp).then_inc(powered, 1)

            @block.vector
            def _(v):
                at.dve(v)
                softmax(v, at, step, [0], mx, sm, ex, shifted, powered)
                v.tensor_tensor(net.aff[:, :, :].rearrange("p j (b e) -> p b j e", b=B),
                                ex[:, :, :].rearrange("p (b j) e -> p b j e", b=B),
                                over(sm[:, :].rearrange("p (b j) -> p b j", b=B), 3, E), ALU.mult)

            @block.gpsimd
            def _(g):
                at.pool(g)


def expert_choice(net, tag):
    nc = net.nc
    L = B * E
    with Phase(net, tag) as ph:
        work = ph.sb("work", [L, S])
        best = ph.sb("best", [L, 8])
        taken = ph.sb("taken", [L, S])
        ones = ph.sb("ones", [L, S])
        count = ph.sb("count", [L, S])
        place = ph.sb("place", [L, S])
        psA, psB = ph.ps("psA", [L, S]), ph.ps("psB", [P, NT * L])
        turned, ready, top, replaced, last, placed, back = (ph.sem(x) for x in
            ("turned", "ready", "top", "replaced", "last", "placed", "back"))
        with ph.start() as block:
            @block.tensor
            def _(pe):
                for j in range(NT):
                    m = pe.transpose(psA[:, j * P:(j + 1) * P], net.aff[:, j, :], net.idf[:, :])
                m.then_inc(turned, 1)
                pe.wait_ge(placed, BASE + 1)
                for j in range(NT):
                    m = pe.transpose(psB[:, j * L:(j + 1) * L], place[:, j * P:(j + 1) * P], net.idf[0:L, 0:L])
                m.then_inc(back, 1)

            @block.vector
            def _(v):
                v.memset(ones[:, :], 1.0)
                v.wait_ge(turned, BASE + 1)
                v.tensor_copy(work[:, :], psA[:, :]).then_inc(ready, 1)
                v.wait_ge(ready, BASE + 1)
                with v.Fori(0, KTOP // 8) as i:
                    waited(net, v, (replaced, i))
                    v.max(best[:, :], work[:, :]).then_inc(top, 1)
                    waited(net, v, (top, i + 1))
                    v.match_replace(work[:, :], best[:, :], work[:, :], -1.0).then_inc(replaced, 1)
                v.wait_ge(replaced, BASE + KTOP // 8)
                v.tensor_scalar(taken[:, :], work[:, :], 0.0, None, ALU.is_lt).then_inc(last, 1)
                v.wait_ge(last, BASE + 1)
                v.tensor_tensor_scan(count[:, :], ones[:, :], taken[:, :], 0.0, ALU.mult, ALU.add).then_inc(last, 1)
                v.wait_ge(last, BASE + 2)
                v.tensor_tensor(count[:, :], count[:, :], taken[:, :], ALU.mult).then_inc(last, 1)
                v.wait_ge(last, BASE + 3)
                v.tensor_scalar(place[:, :], count[:, :], -1.0, None, ALU.add).then_inc(placed, 1)
                v.wait_ge(back, BASE + 1)
                v.tensor_copy(net.slot[:, :, :], psB[:, :].rearrange("p (j l) -> p j l", j=NT)).then_inc(last, 1)


class Experts:

    def __init__(self, net, ctx):
        sb = lambda name, shape: ctx.enter_context(net.nc.sbuf_tensor(name, shape, F32))
        self.net = net
        self.gate, self.up = sb("w_gate", [D, E, FI]), sb("w_up", [D, E, FI])
        self.down = sb("w_down", [P, E, FI // P, D])
        self.loaded = ctx.enter_context(net.nc.semaphore("experts_loaded"))

    def load(self, eng):
        for dst, x in ((self.gate[:, :, :], "L1f_gate"), (self.up[:, :, :], "L1f_up"), (self.down[:, :, :, :], "L1f_down")):
            eng.dma_start(dst, self.net.aps[x]).then_inc(self.loaded, 16)


def expert_ffn(net, tag, experts):
    nc, aps = net.nc, net.aps
    FT = FI // P
    with Phase(net, tag) as ph:
        w_gate, w_up, w_down = experts.gate, experts.up, experts.down
        iota = ph.sb("iota", [P, P])
        slot = ph.sb("slot", [P, 2, NT, E])
        af3 = ph.sb("af3", [P, NT, B * E, 3], BF16)
        afr = ph.sb("afr", [P, NT, B * E])
        xn3 = ph.sb("xn3", [P, 2, NT, 3, D], BF16)
        xr = ph.sb("xr", [P, NT, D])
        pick = ph.sb("pick", [P, 2, NT, P], BF16)
        pickT = ph.sb("pickT", [P, 2, S])
        xg = ph.sb("xg", [P, P])
        weight = ph.sb("weight", [P, 2])
        act_ = ph.sb("act", [P, FI])
        hid = ph.sb("hid", [P, FI])
        y = ph.sb("y", [P, D])
        psX, psG, psU, psD, psO, psO1, psW = (ph.ps(n, [P, S]) for n in ("psX", "psG", "psU", "psD", "psO", "psO1", "psW"))
        psP = ph.ps("psP", [P, S], BF16)
        psO = (psO, psO1)
        (made, parted, copied, picked, gathered, turned, got, gotT, gotW, inner, silu, hidden, down, scaled, scattered,
         added, split) = (ph.sem(x) for x in ("made", "parted", "copied", "picked", "gathered", "turned", "got", "gotT", "gotW",
            "inner", "silu", "hidden", "down", "scaled", "scattered", "added", "split"))
        nm = Norm(ph, "n", None, used=(split, 4))

        def items(eng, item):
            with eng.Fori(0, B // 2 - 1) as i:
                for m in range(2 * E):
                    item(i, m, False, True)
            for m in range(2 * E):
                item(B // 2 - 1, m, m == 2 * E - 1, m < E)

        with ph.start() as block:
            @block.tensor
            def _(pe):
                def gather(i, m):
                    n, e, x = 2 * E * i + m, m % E, m // E % 2
                    g = pick[:, m % 2, :, :]
                    pe.wait_ge(picked, BASE + n + 1)
                    if e == 0:
                        pe.wait_ge(split, BASE + 4 * (2 * i + m // E) + 4)
                    pe.wait_ge(got, BASE + n)
                    for j in range(NT):
                        for part in range(3):
                            mm = pe.matmul(psX[:, 0:P], xn3[:, x, j, part, :], g[:, j, :], start=j == 0 and part == 0,
                                           stop=j == NT - 1 and part == 2)
                    mm.then_inc(gathered, 1)
                    pe.wait_ge(gotW, BASE + n)
                    pe.wait_ge(gotT, BASE + n)
                    for j in range(NT):
                        pe.matmul(psW[:, 0:3], g[:, j, :], af3[:, j, bass.ds(n, 1), :].rearrange("p o c -> p (o c)"),
                                  start=j == 0, stop=j == NT - 1)
                    for j in range(NT):
                        mm = pe.transpose(psP[:, j * P:(j + 1) * P], g[:, j, :], net.idb[:, :])
                    mm.then_inc(turned, 1)

                def up(i, m):
                    n, e = 2 * E * i + m, m % E
                    pe.wait_ge(got, BASE + n + 1)
                    pe.wait_ge(hidden, BASE + n)
                    for ps, w in ((psG, w_gate), (psU, w_up)):
                        for t in range(FT):
                            mm = pe.matmul(ps[:, t * P:(t + 1) * P], w[:, e, t * P:(t + 1) * P], xg[:, :], start=True, stop=True)
                        mm.then_inc(inner, 1)

                def project(i, m):
                    n, e = 2 * E * i + m, m % E
                    pe.wait_ge(hidden, BASE + n + 1)
                    pe.wait_ge(scaled, BASE + n)
                    for t in range(FT):
                        mm = pe.matmul(psD[:, 0:D], hid[:, t * P:(t + 1) * P], w_down[:, e, t, :], start=t == 0, stop=t == FT - 1)
                    mm.then_inc(down, 1)

                def scatter(i, m):
                    n, e = 2 * E * i + m, m % E
                    pe.wait_ge(scaled, BASE + n + 1)
                    pe.wait_ge(gotT, BASE + n + 1)
                    if e == 0:
                        pe.wait_ge(added, BASE + 2 * i + m // E - 1)
                    out = psO[m // E]
                    for j in range(NT):
                        mm = pe.matmul(out[:, j * P:(j + 1) * P], pickT[:, m % 2, j * P:(j + 1) * P], y[:, :],
                                       start=e == 0 and j == 0, stop=e == E - 1 and j == NT - 1, skip_group_check=True)
                    mm.then_inc(scattered, 1)

                def item(i, m, last, more):
                    if not last:
                        gather(i, m + 1)
                    project(i, m)
                    if not last:
                        up(i, m + 1)
                    scatter(i, m)

                pe.wait_ge(parted, BASE + 4)
                gather(0, 0)
                pe.wait_ge(experts.loaded, 48)
                up(0, 0)
                items(pe, item)

            @block.scalar
            def _(a):
                def tokens(i, m):
                    n = 2 * E * i + m
                    a.wait_ge(gathered, BASE + n + 1)
                    a.wait_ge(inner, BASE + 2 * n)
                    a.copy(xg[:, :], psX[:, 0:P]).then_inc(got, 1)

                def item(i, m, last, more):
                    n = 2 * E * i + m
                    a.wait_ge(inner, BASE + 2 * n + 1)
                    a.wait_ge(hidden, BASE + n)
                    a.activation(act_[:, :], psG[:, :], ACT.Silu).then_inc(silu, 1)
                    if not last:
                        tokens(i, m + 1)

                tokens(0, 0)
                items(a, item)

            @block.vector
            def _(v):
                def parts(b, x, first=False):
                    full = lambda p: xn3[:, x, :, p, :]
                    v.wait_ge(nm.normed, BASE + NT * b + NT)
                    if not first:
                        v.wait_ge(gathered, BASE + E * (b - 1))
                    v.tensor_copy(full(0), nm.xn[:, :, :]).then_inc(split, 1)
                    v.wait_ge(split, BASE + 4 * b + 1)
                    v.tensor_tensor(xr[:, :, :], nm.xn[:, :, :], full(0), ALU.subtract).then_inc(split, 1)

                def rests(b, x):
                    full = lambda p: xn3[:, x, :, p, :]
                    v.wait_ge(split, BASE + 4 * b + 2)
                    v.tensor_copy(full(1), xr[:, :, :]).then_inc(split, 1)
                    v.wait_ge(split, BASE + 4 * b + 3)
                    v.tensor_tensor(full(2), xr[:, :, :], full(1), ALU.subtract).then_inc(split, 1)

                def picks(i, m):
                    n = 2 * E * i + m
                    v.wait_ge(turned, BASE + n + 1)
                    v.wait_ge(scattered, BASE + n - 1)
                    v.tensor_copy(pickT[:, m % 2, :], psP[:, :]).then_inc(gotT, 1)
                    v.wait_ge(scaled, BASE + n - 1)
                    v.reduce_sum(weight[:, m % 2:m % 2 + 1], psW[:, 0:3], AX).then_inc(gotW, 1)

                def item(i, m, last, more):
                    n, e, b = 2 * E * i + m, m % E, 2 * i + m // E
                    v.wait_ge(silu, BASE + n + 1)
                    v.wait_ge(inner, BASE + 2 * n + 2)
                    v.wait_ge(down, BASE + n)
                    v.tensor_tensor(hid[:, :], act_[:, :], psU[:, :], ALU.mult).then_inc(hidden, 1)
                    if not last:
                        picks(i, m + 1)
                    v.wait_ge(down, BASE + n + 1)
                    v.wait_ge(gotW, BASE + n + 1)
                    v.wait_ge(scattered, BASE + n)
                    v.tensor_scalar(y[:, :], psD[:, 0:D], weight[:, m % 2:m % 2 + 1], None, ALU.mult).then_inc(scaled, 1)
                    if more and e == 1:
                        nm.stats(v, b + 1)
                    if more and e == 3:
                        nm.norm(v, b + 1)
                    if more and e == 4:
                        parts(b + 1, (m // E + 1) % 2)
                    if more and e == 5:
                        rests(b + 1, (m // E + 1) % 2)
                    if e == E - 1:
                        v.wait_ge(scattered, BASE + n + 1)
                        tiles = net.X[:, bass.ds(b * NT, NT), :]
                        v.tensor_tensor(tiles, tiles, psO[m // E][:, :].rearrange("p (j d) -> p j d", j=NT), ALU.add).then_inc(added, 1)

                v.tensor_copy(af3[:, :, :, 0], net.aff[:, :, :]).then_inc(parted, 1)
                v.wait_ge(parted, BASE + 1)
                v.tensor_tensor(afr[:, :, :], net.aff[:, :, :], af3[:, :, :, 0], ALU.subtract).then_inc(parted, 1)
                v.wait_ge(parted, BASE + 2)
                v.tensor_copy(af3[:, :, :, 1], afr[:, :, :]).then_inc(parted, 1)
                v.wait_ge(parted, BASE + 3)
                v.tensor_tensor(af3[:, :, :, 2], afr[:, :, :], af3[:, :, :, 1], ALU.subtract).then_inc(parted, 1)
                nm.stats(v, 0)
                nm.norm(v, 0)
                parts(0, 0, first=True)
                rests(0, 0)
                picks(0, 0)
                items(v, item)

            @block.gpsimd
            def _(g):
                g.iota(iota[:, :], pattern=[[1, P]], base=0, channel_multiplier=0,
                       allow_small_or_imprecise_dtypes=True).then_inc(made, 1)
                g.wait_ge(made, BASE + 1)
                with g.Fori(0, B // 2) as i:
                    for x in range(2):
                        b = 2 * i + x
                        nm.power(g, b)
                        g.tensor_copy(slot[:, x, :, :], net.slot[:, :, bass.ds(b * E, E)]).then_inc(copied, 1)
                        g.wait_ge(copied, BASE + b + 1)
                        for e in range(E):
                            n = E * b + e
                            waited(net, g, (turned, n - 1))
                            for j in range(NT):
                                m = g.tensor_scalar(pick[:, e % 2, j, :], iota[:, :], slot[:, x, j, e:e + 1], None, ALU.is_equal)
                            m.then_inc(picked, 1)


def dump(net, out):
    nc = net.nc
    with Phase(net, "dump") as ph:
        done = ph.sem("done")
        with ph.start() as block:
            @block.sync
            def _(sp):
                sp.dma_start(out.rearrange("b (j p) d -> p (b j) d", p=P), net.X[:, :, :]).then_inc(done, 16)
                sp.wait_ge(done, BASE + 16)


def program(nc, aps, out):
    with ExitStack() as ctx:
        net = Net(nc, aps, ctx)
        setup(net)
        mla_prep(net)
        heads_t(net, "mh", DH + DR, net.QM, net.KM, 80.0, float(1.0 / np.sqrt(np.float32(DH + DR))))
        moe_top2(net, "m1", (aps["L0_attn_a_W_O"],))
        with nc.sbuf_tensor("far_keys", [P, 2], F32) as keep:
            relative_tables(net, keep)
            relative_prep(net, keep)
        heads_relative(net, "rh", float(1.0 / np.sqrt(np.float32(DH * 3))))
        moe_top2(net, "m2", (aps["L0b_WoT"], aps["L0_attn_b_bo"]))
        experts = Experts(net, ctx)
        linear_prep(net, experts)
        heads_t(net, "lh", DH, net.QS, net.KS, None, None)
        expert_affinity(net, "lo", (aps["L1a_WoT"], aps["L1_attn_a_bo"], 1e-6))
        expert_choice(net, "lc")
        expert_ffn(net, "lf", experts)
        rotary_prep(net)
        heads_max(net, "yh", float(1.0 / np.sqrt(np.float32(DH))))
        expert_affinity(net, "yo", (aps["L1b_WoT"], aps["L1_attn_b_out_b"]))
        expert_choice(net, "yc")
        expert_ffn(net, "yf", experts)
        dump(net, out)


def rotary_mla():
    inv = np.float32(10000.0) ** (-np.arange(0, DR, 2, dtype=np.float32) / np.float32(DR))
    ang = (np.arange(S, dtype=np.float32)[:, None] * inv.astype(np.float32)).astype(np.float64)
    cos, sin = np.cos(ang).T, np.sin(ang).T
    c4 = np.repeat(cos, 2, 0)
    s4 = np.stack([-sin, sin], 1).reshape(DR, S)
    rot = np.zeros((P, S), np.float32)
    rot[:H * DR] = np.tile(c4, (H, 1))
    rot[H * DR:] = np.tile(s4, (H, 1))
    return rot


def rotary_full():
    i = np.arange(D // 2, dtype=np.float32)
    theta = (np.float32(10000.0) ** (np.float32(-2.0) * (i - np.float32(1.0)) / np.float32(D))).astype(np.float32)
    ang = (np.arange(S, dtype=np.float32)[:, None] * theta[None, :]).astype(np.float64)
    cos, sin = np.cos(ang).T, np.sin(ang).T
    return np.stack([np.repeat(cos, 2, 0), np.stack([sin, -sin], 1).reshape(D, S)], 1).astype(np.float32)


def host_layout(inputs):
    a = {k: np.ascontiguousarray(v) for k, v in inputs.items()}
    out = dict(a)
    swap = lambda w: np.ascontiguousarray(w.reshape(w.shape[0], -1, 2)[:, :, ::-1].reshape(w.shape))
    down = np.zeros((D, P), a["L0_attn_a_W_DQ"].dtype)
    down[:, 0:DL] = a["L0_attn_a_W_DQ"]
    down[:, DL:2 * DL] = a["L0_attn_a_W_DKV"]
    down[:, 2 * DL:2 * DL + DR] = a["L0_attn_a_W_KR"]
    down[:, 3 * DL:3 * DL + DR] = swap(a["L0_attn_a_W_KR"])
    out["mla_down"] = down
    out["mla_qr"] = np.concatenate([a["L0_attn_a_W_QR"], swap(a["L0_attn_a_W_QR"])], 1)
    out["mla_rot"] = rotary_mla()
    turned = lambda w: np.ascontiguousarray(w.T)
    for x in "qkvo":
        out[f"L0b_W{x}T"] = turned(a[f"L0_attn_b_W{x}"])
        out[f"L1a_W{x}T"] = turned(a[f"L1_attn_a_W{x}"])
    for x in "kq":
        out[f"L0b_Wp{x}T"] = turned(a[f"L0_attn_b_Wp{x}"])
    each = [turned(a[f"L1_attn_b_w{x}"]) for x in "qkv"]
    out["L1b_w"] = np.ascontiguousarray(np.stack([y for w in each for y in (w, swap(w))], 1))
    out["L1b_in"] = np.ascontiguousarray(np.stack([turned(w) for w in np.split(a["L1_attn_b_in_proj_w"], 3, 0)], 1))
    out["L1b_rot"] = rotary_full()
    out["L1b_WoT"] = turned(a["L1_attn_b_out_w"])
    out["relT"] = turned(a["L0_attn_b_rel_emb"])
    out["relT_reversed"] = turned(a["L0_attn_b_rel_emb"][::-1])
    out["WeT"] = np.ascontiguousarray(a["L0_ffn_We"].transpose(2, 0, 1).reshape(D, E * D))
    out["L1f_gateT"] = turned(a["L1_ffn_gate_w"])
    for x in ("gate", "up"):
        out[f"L1f_{x}"] = np.ascontiguousarray(a[f"L1_ffn_w_{x}"].transpose(2, 0, 1))
    down = a["L1_ffn_w_down"].reshape(E, D, FI // P, P)
    out["L1f_down"] = np.ascontiguousarray(down.transpose(3, 0, 2, 1))
    return out



def kernel(**inputs):
    import concourse.bacc as _bacc
    from concourse.bass_utils import run_bass_kernel_spmd as _run

    nc = _bacc.Bacc("TRN2", target_bir_lowering=False, num_devices=1)
    arrays, aps = {}, {}
    for name, a in host_layout(inputs).items():
        arrays[f"in_{name}"] = a
        aps[name] = nc.dram_tensor(f"in_{name}", a.shape, mybir.dt.from_np(a.dtype), kind="ExternalInput").ap()
    out = nc.dram_tensor("out", (B, S, D), F32, kind="ExternalOutput").ap()
    program(nc, aps, out)
    r = _run(nc, [arrays], core_ids=[0])
    return r.results[0]["out"]
```
